# Optimizing a Trainium2 kernel written in Bass

```python
import numpy as np
import jax
import jax.numpy as jnp

def _softmax(x, axis=-1):
    return jax.nn.softmax(x, axis=axis)

def _gelu(x):
    return jax.nn.gelu(x, approximate=True)

def _silu(x):
    return jax.nn.silu(x)

def _sigmoid(x):
    return jax.nn.sigmoid(x)

def _layernorm(x, axis=-1, eps=1e-05):
    m = jnp.mean(x, axis=axis, keepdims=True)
    v = jnp.var(x, axis=axis, keepdims=True)
    return (x - m) / jnp.sqrt(v + eps)

def _scatter_add(tgt, idx, src, axis=0):
    return tgt.at[idx].add(src)

def _segment_sum(src, seg, n):
    return jax.ops.segment_sum(src, seg, n)
kernel_name = 'mk_flamingo_gated_d4_seqx_r4_3a4d47'

def setup_inputs(seed: int=0):
    np.random.seed(seed)
    _w = jnp.asarray

    def _rec_inputs():
        import jax
        import jax.numpy as jnp
        _rk = jax.random.key(seed)
        x = -0.0003929 + 0.9999 * jax.random.normal(jax.random.fold_in(_rk, 1), (8, 112, 256), jnp.float32)
        _lenS = 112 - jax.random.randint(jax.random.fold_in(_rk, 7), (8,), 0, max(1, 112 // 4) + 1, jnp.int32)
        _lenS2 = 375 - jax.random.randint(jax.random.fold_in(_rk, 8), (8,), 0, max(1, 375 // 4) + 1, jnp.int32)
        _ctx_1024P = jax.random.normal(jax.random.fold_in(_rk, 11), (8, 16, 256), jnp.float32)
        _ctx_1024c = jax.random.dirichlet(jax.random.fold_in(_rk, 511), 0.3 * jnp.ones((16,), jnp.float32), (8, 375))
        _ctx_1024t = jnp.einsum('bsk,bkd->bsd', _ctx_1024c, _ctx_1024P)
        _ctx_1024t = _ctx_1024t * jax.lax.rsqrt(jnp.mean(jnp.square(_ctx_1024t)) + 1e-12) * 0.953939
        ctx_1024 = 0.000227908 + 0.99994 * (_ctx_1024t + 0.3 * jax.random.normal(jax.random.fold_in(_rk, 611), (8, 375, 256), jnp.float32))
        _validS = jnp.arange(112)[None, :] < _lenS[:, None]
        _validS2 = jnp.arange(375)[None, :] < _lenS2[:, None]
        _causal = jnp.tril(jnp.ones((112, 112), dtype=bool))
        mask_BxS2_bf1 = jnp.ones((8, 375), dtype=bool)
        _g = jax.random.normal(jax.random.fold_in(_rk, 9001), (2, 4), jnp.float32)
        _g = jnp.sign(_g) * jnp.maximum(jnp.abs(_g), 1.0) + (_g == 0) * 1.0
        g_xattn = _g[0]
        g_ffn = _g[1]
        return (x, ctx_1024, mask_BxS2_bf1, g_xattn, g_ffn)
    x, ctx_1024, mask_BxS2_bf1, g_xattn, g_ffn = _rec_inputs()

    def _L0_xattn_setup():
        import jax, jax.numpy as jnp
        import numpy as np
        DIM = 256
        HEADS = 16
        HEAD_DIM = 64
        INNER = HEADS * HEAD_DIM
        SCALE = 8.0
        LN_EPS = 1e-05
        NORM_EPS = 1e-12

        def layer_norm(x, g, b):
            m = jnp.mean(x, axis=-1, keepdims=True)
            v = jnp.mean((x - m) ** 2, axis=-1, keepdims=True)
            return (x - m) * jax.lax.rsqrt(v + LN_EPS) * g + b

        def l2_normalize(x):
            n = jnp.sqrt(jnp.sum(x * x, axis=-1, keepdims=True))
            return x / jnp.maximum(n, NORM_EPS)
        key = jax.random.key(seed)
        ks = jax.random.split(key, 8)
        B, N, T = (4, 1024, 64)
        s = 0.02
        return {'x': jax.random.normal(ks[0], (B, N, DIM), jnp.float32), 'context': jax.random.normal(ks[1], (B, T, DIM), jnp.float32), 'Wq': jax.random.normal(ks[2], (DIM, INNER), jnp.float32) * s, 'Wkv': jax.random.normal(ks[3], (DIM, 2 * INNER), jnp.float32) * s, 'Wo': jax.random.normal(ks[4], (INNER, DIM), jnp.float32) * s, 'null_kv': jax.random.normal(ks[5], (2, HEAD_DIM), jnp.float32), 'q_scale': jnp.ones((HEAD_DIM,), jnp.float32), 'k_scale': jnp.ones((HEAD_DIM,), jnp.float32), 'ln_in_g': jnp.ones((DIM,), jnp.float32), 'ln_in_b': jnp.zeros((DIM,), jnp.float32), 'ln_ctx_g': jnp.ones((DIM,), jnp.float32), 'ln_ctx_b': jnp.zeros((DIM,), jnp.float32), 'ln_out_g': jnp.ones((DIM,), jnp.float32), 'ln_out_b': jnp.zeros((DIM,), jnp.float32)}
    _L0_xattn_all = _L0_xattn_setup()
    _L0_xattn_in = {k: v for k, v in _L0_xattn_all.items() if k in ('Wq', 'Wkv', 'Wo', 'null_kv', 'q_scale', 'k_scale', 'ln_in_g', 'ln_in_b', 'ln_ctx_g', 'ln_ctx_b', 'ln_out_g', 'ln_out_b')}
    del _L0_xattn_all

    def _L0_ffn_setup():
        import jax, jax.numpy as jnp
        import numpy as np
        NHEAD = 16
        NUM_GROUPS = 4
        EXPERTS_PER_GROUP = 2
        LN_EPS = 1e-05

        def _layernorm(x, g, b):
            mu = jnp.mean(x, axis=-1, keepdims=True)
            var = jnp.mean(jnp.square(x - mu), axis=-1, keepdims=True)
            return (x - mu) * jax.lax.rsqrt(var + LN_EPS) * g + b

        def _mha(x, wi, bi, wo, bo):
            B, S, D = x.shape
            hd = D // NHEAD
            qkv = x @ wi.T + bi
            q, k, v = jnp.split(qkv, 3, axis=-1)

            def heads(t):
                return t.reshape(B, S, NHEAD, hd).transpose(0, 2, 1, 3)
            q, k, v = (heads(q), heads(k), heads(v))
            scores = jnp.einsum('bhqd,bhkd->bhqk', q, k) / jnp.sqrt(jnp.asarray(hd, x.dtype))
            attn = jax.nn.softmax(scores, axis=-1)
            o = jnp.einsum('bhqk,bhkd->bhqd', attn, v)
            o = o.transpose(0, 2, 1, 3).reshape(B, S, D)
            return o @ wo.T + bo

        def _hier_moe(x, w_group, b_group, w_expert, b_expert, w1, b1, w2, b2):
            B, S, D = x.shape
            xt = x.reshape(B * S, D)
            T = xt.shape[0]
            E = NUM_GROUPS * EXPERTS_PER_GROUP
            gp = jax.nn.softmax(xt @ w_group + b_group, axis=-1)
            g_idx = jnp.argmax(gp, axis=-1)
            g_prob = jnp.max(gp, axis=-1)
            elog = jnp.einsum('td,gde->tge', xt, w_expert) + b_expert
            ep = jax.nn.softmax(elog, axis=-1)
            ep_sel = jnp.take_along_axis(ep, g_idx[:, None, None], axis=1)[:, 0, :]
            e_idx_local = jnp.argmax(ep_sel, axis=-1)
            e_prob = jnp.max(ep_sel, axis=-1)
            flat_e = g_idx * EXPERTS_PER_GROUP + e_idx_local
            combine = jax.nn.one_hot(flat_e, E, dtype=xt.dtype) * (g_prob * e_prob)[:, None]
            h = jax.nn.relu(jnp.einsum('td,edf->etf', xt, w1) + b1[:, None, :])
            y = jnp.einsum('etf,efd->etd', h, w2) + b2[:, None, :]
            out = jnp.einsum('te,etd->td', combine, y)
            return out.reshape(B, S, D)
        key = jax.random.key(seed)
        ks = jax.random.split(key, 8)
        B, S, D, F = (2, 256, 256, 512)
        G, Epg = (NUM_GROUPS, EXPERTS_PER_GROUP)
        E = G * Epg
        sc = lambda fan: 1.0 / np.sqrt(fan)
        return {'x': jax.random.normal(ks[0], (B, S, D), jnp.float32), 'in_proj_w': jax.random.normal(ks[1], (3 * D, D), jnp.float32) * sc(D), 'in_proj_b': jnp.zeros((3 * D,), jnp.float32), 'out_proj_w': jax.random.normal(ks[2], (D, D), jnp.float32) * sc(D), 'out_proj_b': jnp.zeros((D,), jnp.float32), 'ln1_g': jnp.ones((D,), jnp.float32), 'ln1_b': jnp.zeros((D,), jnp.float32), 'ln2_g': jnp.ones((D,), jnp.float32), 'ln2_b': jnp.zeros((D,), jnp.float32), 'w_group': jax.random.normal(ks[3], (D, G), jnp.float32) * sc(D), 'b_group': jnp.zeros((G,), jnp.float32), 'w_expert': jax.random.normal(ks[4], (G, D, Epg), jnp.float32) * sc(D), 'b_expert': jnp.zeros((G, Epg), jnp.float32), 'w1': jax.random.normal(ks[5], (E, D, F), jnp.float32) * sc(D), 'b1': jnp.zeros((E, F), jnp.float32), 'w2': jax.random.normal(ks[6], (E, F, D), jnp.float32) * sc(F), 'b2': jnp.zeros((E, D), jnp.float32)}
    _L0_ffn_all = _L0_ffn_setup()
    _L0_ffn_in = {k: v for k, v in _L0_ffn_all.items() if k in ('in_proj_w', 'in_proj_b', 'out_proj_w', 'out_proj_b', 'ln1_g', 'ln1_b', 'ln2_g', 'ln2_b', 'w_group', 'b_group', 'w_expert', 'b_expert', 'w1', 'b1', 'w2', 'b2')}
    del _L0_ffn_all

    def _L1_xattn_setup():
        import jax, jax.numpy as jnp
        import numpy as np
        D_MODEL = 256
        NHEAD = 16
        D_K = D_MODEL // NHEAD
        key = jax.random.key(seed)
        ks = jax.random.split(key, 12)
        B, L = (4, 512)
        s = 1.0 / np.sqrt(D_MODEL)
        inp = {'query': jax.random.normal(ks[0], (B, L, D_MODEL), jnp.float32), 'key': jax.random.normal(ks[1], (B, L, D_MODEL), jnp.float32), 'value': jax.random.normal(ks[2], (B, L, D_MODEL), jnp.float32), 'Wq': jax.random.normal(ks[3], (D_MODEL, D_MODEL), jnp.float32) * s, 'bq': jnp.zeros((D_MODEL,), jnp.float32), 'Wk': jax.random.normal(ks[4], (D_MODEL, D_MODEL), jnp.float32) * s, 'bk': jnp.zeros((D_MODEL,), jnp.float32), 'Wv': jax.random.normal(ks[5], (D_MODEL, D_MODEL), jnp.float32) * s, 'bv': jnp.zeros((D_MODEL,), jnp.float32), 'Wo': jax.random.normal(ks[6], (D_MODEL, D_MODEL), jnp.float32) * s, 'bo': jnp.zeros((D_MODEL,), jnp.float32)}
        return inp
    _L1_xattn_all = _L1_xattn_setup()
    _L1_xattn_in = {k: v for k, v in _L1_xattn_all.items() if k in ('Wq', 'bq', 'Wk', 'bk', 'Wv', 'bv', 'Wo', 'bo')}
    del _L1_xattn_all

    def _L1_ffn_setup():
        import jax, jax.numpy as jnp
        import numpy as np
        E, K = (8, 4)
        B, S, D = (4, 256, 256)
        H = D * 2 * 4 // 3

        def _swiglu(u, w1, w2, w3):
            h = jnp.einsum('...d,hd->...h', u, w1)
            v = jnp.einsum('...d,hd->...h', u, w2)
            return jnp.einsum('...h,dh->...d', jax.nn.sigmoid(h) * h * v, w3)
        key = jax.random.key(seed)
        ks = jax.random.split(key, 9)
        std = 0.02
        return {'x': jax.random.normal(ks[0], (B, S, D), jnp.float32), 'Wg': jax.random.normal(ks[1], (E, D), jnp.float32) * std, 'routing_bias': jnp.zeros((E,), jnp.float32), 'W1': jax.random.normal(ks[2], (E, H, D), jnp.float32) * std, 'W2': jax.random.normal(ks[3], (E, H, D), jnp.float32) * std, 'W3': jax.random.normal(ks[4], (E, D, H), jnp.float32) * std, 'Ws1': jax.random.normal(ks[5], (H, D), jnp.float32) * std, 'Ws2': jax.random.normal(ks[6], (H, D), jnp.float32) * std, 'Ws3': jax.random.normal(ks[7], (D, H), jnp.float32) * std}
    _L1_ffn_all = _L1_ffn_setup()
    _L1_ffn_in = {k: v for k, v in _L1_ffn_all.items() if k in ('Wg', 'routing_bias', 'W1', 'W2', 'W3', 'Ws1', 'Ws2', 'Ws3')}
    del _L1_ffn_all

    def _L2_xattn_setup():
        import jax, jax.numpy as jnp
        import numpy as np
        D_MODEL = 256
        NUM_HEADS = 16
        HEAD_DIM = D_MODEL // NUM_HEADS
        key = jax.random.key(seed)
        kq, kk, kv, kw, kb = jax.random.split(key, 5)
        N, S = (2, 512)
        query = jax.random.normal(kq, (N, S, D_MODEL), dtype=jnp.float32)
        key_t = jax.random.normal(kk, (N, S, D_MODEL), dtype=jnp.float32)
        value = jax.random.normal(kv, (N, S, D_MODEL), dtype=jnp.float32)
        lim = 1.0 / np.sqrt(D_MODEL)
        W_out = jax.random.uniform(kw, (D_MODEL, D_MODEL), minval=-lim, maxval=lim, dtype=jnp.float32)
        b_out = jax.random.uniform(kb, (D_MODEL,), minval=-lim, maxval=lim, dtype=jnp.float32)
        return {'query': query, 'key': key_t, 'value': value, 'W_out': W_out, 'b_out': b_out}
    _L2_xattn_all = _L2_xattn_setup()
    _L2_xattn_in = {k: v for k, v in _L2_xattn_all.items() if k in ('W_out', 'b_out')}
    del _L2_xattn_all

    def _L2_ffn_setup():
        import jax, jax.numpy as jnp
        import numpy as np
        D_MODEL = 256
        D_FF = 1024
        N_EXPERTS = 8
        INIT_SCALE = 0.1

        def _trunc_normal(key, shape, std):
            return std * jax.random.truncated_normal(key, -2.0, 2.0, shape, dtype=jnp.float32)
        key = jax.random.key(seed)
        ks = jax.random.split(key, 5)
        x = jax.random.normal(ks[0], (4, 256, D_MODEL), dtype=jnp.float32)
        router_W = _trunc_normal(ks[1], (D_MODEL, N_EXPERTS), INIT_SCALE / np.sqrt(D_MODEL))
        router_b = jnp.zeros((N_EXPERTS,), dtype=jnp.float32)
        W1 = _trunc_normal(ks[2], (N_EXPERTS, D_MODEL, D_FF), INIT_SCALE / np.sqrt(D_MODEL))
        b1 = jnp.zeros((N_EXPERTS, D_FF), dtype=jnp.float32)
        W2 = _trunc_normal(ks[3], (N_EXPERTS, D_FF, D_MODEL), INIT_SCALE / np.sqrt(D_FF))
        b2 = jnp.zeros((N_EXPERTS, D_MODEL), dtype=jnp.float32)
        return {'x': x, 'router_W': router_W, 'router_b': router_b, 'W1': W1, 'b1': b1, 'W2': W2, 'b2': b2}
    _L2_ffn_all = _L2_ffn_setup()
    _L2_ffn_in = {k: v for k, v in _L2_ffn_all.items() if k in ('router_W', 'router_b', 'W1', 'b1', 'W2', 'b2')}
    del _L2_ffn_all

    def _L3_xattn_setup():
        import jax, jax.numpy as jnp
        import numpy as np
        GAMMA = 10.0
        BASE = 10000.0
        SCALE = 64 ** (-0.5)
        NUM_HEADS = 16

        def _larope(t, seq_len):
            B, H, L, D = t.shape
            inv_freq = 1.0 / BASE ** (jnp.arange(0, D, 2, dtype=jnp.float32) / D)
            pos = GAMMA * (jnp.arange(L, dtype=jnp.float32) / float(seq_len))
            ang = pos[:, None] * inv_freq
            cos = jnp.cos(ang)
            sin = jnp.sin(ang)
            te, to = (t[..., 0::2], t[..., 1::2])
            re = te * cos - to * sin
            ro = te * sin + to * cos
            return jnp.stack([re, ro], axis=-1).reshape(t.shape)
        key = jax.random.key(seed)
        ks = jax.random.split(key, 8)
        B, Lq, Lk, D = (8, 512, 128, 256)
        s = D ** (-0.5)
        return {'x': jax.random.normal(ks[0], (B, Lq, D), jnp.float32), 'context': jax.random.normal(ks[1], (B, Lk, D), jnp.float32), 'context_mask': jnp.ones((B, Lk), dtype=bool), 'Wq': jax.random.normal(ks[2], (D, D), jnp.float32) * s, 'bq': jnp.zeros((D,), jnp.float32), 'Wkv': jax.random.normal(ks[3], (D, 2 * D), jnp.float32) * s, 'bkv': jnp.zeros((2 * D,), jnp.float32), 'Wo': jax.random.normal(ks[4], (D, D), jnp.float32) * s, 'bo': jnp.zeros((D,), jnp.float32)}
    _L3_xattn_all = _L3_xattn_setup()
    _L3_xattn_in = {k: v for k, v in _L3_xattn_all.items() if k in ('Wq', 'bq', 'Wkv', 'bkv', 'Wo', 'bo')}
    del _L3_xattn_all

    def _L3_ffn_setup():
        import jax, jax.numpy as jnp
        import numpy as np
        B, S, D, O, E, R = (8, 512, 256, 256, 8, 4)
        TOP_K = 2
        SCALING = 4.0 / 4.0
        key = jax.random.key(seed)
        k0, k1, k2, k3, k4 = jax.random.split(key, 5)
        hidden_states = jax.random.normal(k0, (B, S, D), dtype=jnp.float32)
        W_lin = jax.random.normal(k1, (O, D), dtype=jnp.float32) * 0.02
        b_lin = jnp.zeros((O,), dtype=jnp.float32)
        gate_w = jax.random.normal(k2, (E, D), dtype=jnp.float32) * 0.02
        left = jax.random.normal(k3, (E, D, R), dtype=jnp.float32) * 0.02
        right = jax.random.normal(k4, (E, R, O), dtype=jnp.float32) * 0.02
        return {'hidden_states': hidden_states, 'W_lin': W_lin, 'b_lin': b_lin, 'gate_w': gate_w, 'left': left, 'right': right}
    _L3_ffn_all = _L3_ffn_setup()
    _L3_ffn_in = {k: v for k, v in _L3_ffn_all.items() if k in ('W_lin', 'b_lin', 'gate_w', 'left', 'right')}
    del _L3_ffn_all
    return {'x': x, 'ctx_1024': ctx_1024, 'mask_BxS2_bf1': mask_BxS2_bf1, 'g_xattn': g_xattn, 'g_ffn': g_ffn, 'L0_xattn_Wq': _L0_xattn_in['Wq'], 'L0_xattn_Wkv': _L0_xattn_in['Wkv'], 'L0_xattn_Wo': _L0_xattn_in['Wo'], 'L0_xattn_null_kv': _L0_xattn_in['null_kv'], 'L0_xattn_q_scale': _L0_xattn_in['q_scale'], 'L0_xattn_k_scale': _L0_xattn_in['k_scale'], 'L0_xattn_ln_in_g': _L0_xattn_in['ln_in_g'], 'L0_xattn_ln_in_b': _L0_xattn_in['ln_in_b'], 'L0_xattn_ln_ctx_g': _L0_xattn_in['ln_ctx_g'], 'L0_xattn_ln_ctx_b': _L0_xattn_in['ln_ctx_b'], 'L0_xattn_ln_out_g': _L0_xattn_in['ln_out_g'], 'L0_xattn_ln_out_b': _L0_xattn_in['ln_out_b'], 'L0_ffn_in_proj_w': _L0_ffn_in['in_proj_w'], 'L0_ffn_in_proj_b': _L0_ffn_in['in_proj_b'], 'L0_ffn_out_proj_w': _L0_ffn_in['out_proj_w'], 'L0_ffn_out_proj_b': _L0_ffn_in['out_proj_b'], 'L0_ffn_ln1_g': _L0_ffn_in['ln1_g'], 'L0_ffn_ln1_b': _L0_ffn_in['ln1_b'], 'L0_ffn_ln2_g': _L0_ffn_in['ln2_g'], 'L0_ffn_ln2_b': _L0_ffn_in['ln2_b'], 'L0_ffn_w_group': _L0_ffn_in['w_group'], 'L0_ffn_b_group': _L0_ffn_in['b_group'], 'L0_ffn_w_expert': _L0_ffn_in['w_expert'], 'L0_ffn_b_expert': _L0_ffn_in['b_expert'], 'L0_ffn_w1': _L0_ffn_in['w1'], 'L0_ffn_b1': _L0_ffn_in['b1'], 'L0_ffn_w2': _L0_ffn_in['w2'], 'L0_ffn_b2': _L0_ffn_in['b2'], 'L1_xattn_Wq': _L1_xattn_in['Wq'], 'L1_xattn_bq': _L1_xattn_in['bq'], 'L1_xattn_Wk': _L1_xattn_in['Wk'], 'L1_xattn_bk': _L1_xattn_in['bk'], 'L1_xattn_Wv': _L1_xattn_in['Wv'], 'L1_xattn_bv': _L1_xattn_in['bv'], 'L1_xattn_Wo': _L1_xattn_in['Wo'], 'L1_xattn_bo': _L1_xattn_in['bo'], 'L1_ffn_Wg': _L1_ffn_in['Wg'], 'L1_ffn_routing_bias': _L1_ffn_in['routing_bias'], 'L1_ffn_W1': _L1_ffn_in['W1'], 'L1_ffn_W2': _L1_ffn_in['W2'], 'L1_ffn_W3': _L1_ffn_in['W3'], 'L1_ffn_Ws1': _L1_ffn_in['Ws1'], 'L1_ffn_Ws2': _L1_ffn_in['Ws2'], 'L1_ffn_Ws3': _L1_ffn_in['Ws3'], 'L2_xattn_W_out': _L2_xattn_in['W_out'], 'L2_xattn_b_out': _L2_xattn_in['b_out'], 'L2_ffn_router_W': _L2_ffn_in['router_W'], 'L2_ffn_router_b': _L2_ffn_in['router_b'], 'L2_ffn_W1': _L2_ffn_in['W1'], 'L2_ffn_b1': _L2_ffn_in['b1'], 'L2_ffn_W2': _L2_ffn_in['W2'], 'L2_ffn_b2': _L2_ffn_in['b2'], 'L3_xattn_Wq': _L3_xattn_in['Wq'], 'L3_xattn_bq': _L3_xattn_in['bq'], 'L3_xattn_Wkv': _L3_xattn_in['Wkv'], 'L3_xattn_bkv': _L3_xattn_in['bkv'], 'L3_xattn_Wo': _L3_xattn_in['Wo'], 'L3_xattn_bo': _L3_xattn_in['bo'], 'L3_ffn_W_lin': _L3_ffn_in['W_lin'], 'L3_ffn_b_lin': _L3_ffn_in['b_lin'], 'L3_ffn_gate_w': _L3_ffn_in['gate_w'], 'L3_ffn_left': _L3_ffn_in['left'], 'L3_ffn_right': _L3_ffn_in['right']}

def reference(x, ctx_1024, mask_BxS2_bf1, g_xattn, g_ffn, L0_xattn_Wq, L0_xattn_Wkv, L0_xattn_Wo, L0_xattn_null_kv, L0_xattn_q_scale, L0_xattn_k_scale, L0_xattn_ln_in_g, L0_xattn_ln_in_b, L0_xattn_ln_ctx_g, L0_xattn_ln_ctx_b, L0_xattn_ln_out_g, L0_xattn_ln_out_b, L0_ffn_in_proj_w, L0_ffn_in_proj_b, L0_ffn_out_proj_w, L0_ffn_out_proj_b, L0_ffn_ln1_g, L0_ffn_ln1_b, L0_ffn_ln2_g, L0_ffn_ln2_b, L0_ffn_w_group, L0_ffn_b_group, L0_ffn_w_expert, L0_ffn_b_expert, L0_ffn_w1, L0_ffn_b1, L0_ffn_w2, L0_ffn_b2, L1_xattn_Wq, L1_xattn_bq, L1_xattn_Wk, L1_xattn_bk, L1_xattn_Wv, L1_xattn_bv, L1_xattn_Wo, L1_xattn_bo, L1_ffn_Wg, L1_ffn_routing_bias, L1_ffn_W1, L1_ffn_W2, L1_ffn_W3, L1_ffn_Ws1, L1_ffn_Ws2, L1_ffn_Ws3, L2_xattn_W_out, L2_xattn_b_out, L2_ffn_router_W, L2_ffn_router_b, L2_ffn_W1, L2_ffn_b1, L2_ffn_W2, L2_ffn_b2, L3_xattn_Wq, L3_xattn_bq, L3_xattn_Wkv, L3_xattn_bkv, L3_xattn_Wo, L3_xattn_bo, L3_ffn_W_lin, L3_ffn_b_lin, L3_ffn_gate_w, L3_ffn_left, L3_ffn_right):
    import jax
    import jax.numpy as jnp

    def _L0_xattn_ref(x, context, Wq, Wkv, Wo, null_kv, q_scale, k_scale, ln_in_g, ln_in_b, ln_ctx_g, ln_ctx_b, ln_out_g, ln_out_b):
        import jax, jax.numpy as jnp
        import numpy as np
        DIM = 256
        HEADS = 16
        HEAD_DIM = 64
        INNER = HEADS * HEAD_DIM
        SCALE = 8.0
        LN_EPS = 1e-05
        NORM_EPS = 1e-12

        def layer_norm(x, g, b):
            m = jnp.mean(x, axis=-1, keepdims=True)
            v = jnp.mean((x - m) ** 2, axis=-1, keepdims=True)
            return (x - m) * jax.lax.rsqrt(v + LN_EPS) * g + b

        def l2_normalize(x):
            n = jnp.sqrt(jnp.sum(x * x, axis=-1, keepdims=True))
            return x / jnp.maximum(n, NORM_EPS)
        B, N, _ = x.shape
        T = context.shape[1]
        xn = layer_norm(x, ln_in_g, ln_in_b)
        cn = layer_norm(context, ln_ctx_g, ln_ctx_b)
        q = xn @ Wq
        kv = cn @ Wkv
        k, v = jnp.split(kv, 2, axis=-1)

        def split_heads(t):
            b, s, _ = t.shape
            return t.reshape(b, s, HEADS, HEAD_DIM).transpose(0, 2, 1, 3)
        q, k, v = (split_heads(q), split_heads(k), split_heads(v))
        nk = jnp.broadcast_to(null_kv[0], (B, HEADS, 1, HEAD_DIM))
        nv = jnp.broadcast_to(null_kv[1], (B, HEADS, 1, HEAD_DIM))
        k = jnp.concatenate([k, nk], axis=2)
        v = jnp.concatenate([v, nv], axis=2)
        q = l2_normalize(q) * q_scale
        k = l2_normalize(k) * k_scale
        scores = jnp.einsum('bhid,bhkd->bhik', q, k) * SCALE
        attn = jax.nn.softmax(scores, axis=-1)
        out = jnp.einsum('bhik,bhkd->bhid', attn, v)
        out = out.transpose(0, 2, 1, 3).reshape(B, N, INNER)
        out = out @ Wo
        return layer_norm(out, ln_out_g, ln_out_b)

    def _L0_ffn_ref(x, in_proj_w, in_proj_b, out_proj_w, out_proj_b, ln1_g, ln1_b, ln2_g, ln2_b, w_group, b_group, w_expert, b_expert, w1, b1, w2, b2):
        import jax, jax.numpy as jnp
        import numpy as np
        NHEAD = 16
        NUM_GROUPS = 4
        EXPERTS_PER_GROUP = 2
        LN_EPS = 1e-05

        def _layernorm(x, g, b):
            mu = jnp.mean(x, axis=-1, keepdims=True)
            var = jnp.mean(jnp.square(x - mu), axis=-1, keepdims=True)
            return (x - mu) * jax.lax.rsqrt(var + LN_EPS) * g + b

        def _mha(x, wi, bi, wo, bo):
            B, S, D = x.shape
            hd = D // NHEAD
            qkv = x @ wi.T + bi
            q, k, v = jnp.split(qkv, 3, axis=-1)

            def heads(t):
                return t.reshape(B, S, NHEAD, hd).transpose(0, 2, 1, 3)
            q, k, v = (heads(q), heads(k), heads(v))
            scores = jnp.einsum('bhqd,bhkd->bhqk', q, k) / jnp.sqrt(jnp.asarray(hd, x.dtype))
            attn = jax.nn.softmax(scores, axis=-1)
            o = jnp.einsum('bhqk,bhkd->bhqd', attn, v)
            o = o.transpose(0, 2, 1, 3).reshape(B, S, D)
            return o @ wo.T + bo

        def _hier_moe(x, w_group, b_group, w_expert, b_expert, w1, b1, w2, b2):
            B, S, D = x.shape
            xt = x.reshape(B * S, D)
            T = xt.shape[0]
            E = NUM_GROUPS * EXPERTS_PER_GROUP
            gp = jax.nn.softmax(xt @ w_group + b_group, axis=-1)
            g_idx = jnp.argmax(gp, axis=-1)
            g_prob = jnp.max(gp, axis=-1)
            elog = jnp.einsum('td,gde->tge', xt, w_expert) + b_expert
            ep = jax.nn.softmax(elog, axis=-1)
            ep_sel = jnp.take_along_axis(ep, g_idx[:, None, None], axis=1)[:, 0, :]
            e_idx_local = jnp.argmax(ep_sel, axis=-1)
            e_prob = jnp.max(ep_sel, axis=-1)
            flat_e = g_idx * EXPERTS_PER_GROUP + e_idx_local
            combine = jax.nn.one_hot(flat_e, E, dtype=xt.dtype) * (g_prob * e_prob)[:, None]
            h = jax.nn.relu(jnp.einsum('td,edf->etf', xt, w1) + b1[:, None, :])
            y = jnp.einsum('etf,efd->etd', h, w2) + b2[:, None, :]
            out = jnp.einsum('te,etd->td', combine, y)
            return out.reshape(B, S, D)
        attn_out = _mha(x, in_proj_w, in_proj_b, out_proj_w, out_proj_b)
        x = _layernorm(x + attn_out, ln1_g, ln1_b)
        moe_out = _hier_moe(x, w_group, b_group, w_expert, b_expert, w1, b1, w2, b2)
        x = _layernorm(x + moe_out, ln2_g, ln2_b)
        return x

    def _L1_xattn_ref(query, key, value, Wq, bq, Wk, bk, Wv, bv, Wo, bo):
        import jax, jax.numpy as jnp
        import numpy as np
        D_MODEL = 256
        NHEAD = 16
        D_K = D_MODEL // NHEAD
        B, Lq, _ = query.shape
        Lk = key.shape[1]
        Q = (query @ Wq + bq).reshape(B, Lq, NHEAD, D_K).transpose(0, 2, 1, 3)
        K = (key @ Wk + bk).reshape(B, Lk, NHEAD, D_K).transpose(0, 2, 1, 3)
        V = (value @ Wv + bv).reshape(B, Lk, NHEAD, D_K).transpose(0, 2, 1, 3)
        scale = 1.0 / jnp.sqrt(jnp.asarray(D_K, Q.dtype))
        scores = jnp.einsum('bhqd,bhkd->bhqk', Q, K) * scale
        attn = jax.nn.softmax(scores, axis=-1)
        context = jnp.einsum('bhqk,bhkd->bhqd', attn, V)
        context = context.transpose(0, 2, 1, 3).reshape(B, Lq, D_MODEL)
        return context @ Wo + bo

    def _L1_ffn_ref(x, Wg, routing_bias, W1, W2, W3, Ws1, Ws2, Ws3):
        import jax, jax.numpy as jnp
        import numpy as np
        E, K = (8, 4)
        B, S, D = (4, 256, 256)
        H = D * 2 * 4 // 3

        def _swiglu(u, w1, w2, w3):
            h = jnp.einsum('...d,hd->...h', u, w1)
            v = jnp.einsum('...d,hd->...h', u, w2)
            return jnp.einsum('...h,dh->...d', jax.nn.sigmoid(h) * h * v, w3)
        gate = jnp.einsum('bsd,ed->bse', x, Wg) + routing_bias
        _, top_idx = jax.lax.top_k(gate, K)
        mask = jax.nn.one_hot(top_idx, E, dtype=gate.dtype).sum(-2)
        masked_gate = jnp.where(mask > 0, gate, -jnp.inf)
        probs = jax.nn.softmax(masked_gate, axis=-1)
        weights = probs * mask
        out = _swiglu(x, Ws1, Ws2, Ws3)
        h1 = jnp.einsum('bsd,ehd->ebsh', x, W1)
        h2 = jnp.einsum('bsd,ehd->ebsh', x, W2)
        eo = jnp.einsum('ebsh,edh->ebsd', jax.nn.sigmoid(h1) * h1 * h2, W3)
        out = out + jnp.einsum('ebsd,bse->bsd', eo, weights)
        return out

    def _L2_xattn_ref(query, key, value, W_out, b_out):
        import jax, jax.numpy as jnp
        import numpy as np
        D_MODEL = 256
        NUM_HEADS = 16
        HEAD_DIM = D_MODEL // NUM_HEADS
        N, Lq, _ = query.shape
        Lk = key.shape[1]
        q = query.reshape(N, Lq, NUM_HEADS, HEAD_DIM)
        k = key.reshape(N, Lk, NUM_HEADS, HEAD_DIM)
        v = value.reshape(N, Lk, NUM_HEADS, HEAD_DIM)
        scores = jnp.einsum('nqhd,nkhd->nhqk', q, k)
        attn = jax.nn.softmax(scores, axis=3)
        out = jnp.einsum('nhqk,nkhd->nqhd', attn, v).reshape(N, Lq, D_MODEL)
        return out @ W_out.T + b_out

    def _L2_ffn_ref(x, router_W, router_b, W1, b1, W2, b2):
        import jax, jax.numpy as jnp
        import numpy as np
        D_MODEL = 256
        D_FF = 1024
        N_EXPERTS = 8
        INIT_SCALE = 0.1

        def _trunc_normal(key, shape, std):
            return std * jax.random.truncated_normal(key, -2.0, 2.0, shape, dtype=jnp.float32)
        logits = jnp.einsum('bsd,de->bse', x.astype(jnp.float32), router_W) + router_b
        probs = jax.nn.softmax(logits, axis=-1)
        top1 = jnp.argmax(probs, axis=-1)
        mask = jax.nn.one_hot(top1, N_EXPERTS, dtype=x.dtype)
        gates = mask * probs.astype(x.dtype)
        h = jax.nn.relu(jnp.einsum('bsd,edf->besf', x, W1) + b1[:, None, :])
        y = jnp.einsum('besf,efd->besd', h, W2) + b2[:, None, :]
        out = jnp.einsum('bse,besd->bsd', gates, y)
        return out

    def _L3_xattn_ref(x, context, context_mask, Wq, bq, Wkv, bkv, Wo, bo):
        import jax, jax.numpy as jnp
        import numpy as np
        GAMMA = 10.0
        BASE = 10000.0
        SCALE = 64 ** (-0.5)
        NUM_HEADS = 16

        def _larope(t, seq_len):
            B, H, L, D = t.shape
            inv_freq = 1.0 / BASE ** (jnp.arange(0, D, 2, dtype=jnp.float32) / D)
            pos = GAMMA * (jnp.arange(L, dtype=jnp.float32) / float(seq_len))
            ang = pos[:, None] * inv_freq
            cos = jnp.cos(ang)
            sin = jnp.sin(ang)
            te, to = (t[..., 0::2], t[..., 1::2])
            re = te * cos - to * sin
            ro = te * sin + to * cos
            return jnp.stack([re, ro], axis=-1).reshape(t.shape)
        B, Lq, D = x.shape
        Lk = context.shape[1]
        H = NUM_HEADS
        hd = D // H
        q = x @ Wq + bq
        kv = context @ Wkv + bkv
        k, v = jnp.split(kv, 2, axis=-1)
        q = q.reshape(B, Lq, H, hd).transpose(0, 2, 1, 3)
        k = k.reshape(B, Lk, H, hd).transpose(0, 2, 1, 3)
        v = v.reshape(B, Lk, H, hd).transpose(0, 2, 1, 3)
        q = _larope(q, Lq)
        k = _larope(k, Lk)
        scores = jnp.einsum('bhqd,bhkd->bhqk', q, k) * SCALE
        scores = jnp.where(context_mask[:, None, None, :], scores, -jnp.inf)
        attn = jax.nn.softmax(scores, axis=-1)
        out = jnp.einsum('bhqk,bhkd->bhqd', attn, v)
        out = out.transpose(0, 2, 1, 3).reshape(B, Lq, H * hd)
        return out @ Wo + bo

    def _L3_ffn_ref(hidden_states, W_lin, b_lin, gate_w, left, right):
        import jax, jax.numpy as jnp
        import numpy as np
        B, S, D, O, E, R = (8, 512, 256, 256, 8, 4)
        TOP_K = 2
        SCALING = 4.0 / 4.0
        bsz, seq, d_in = hidden_states.shape
        x = hidden_states.reshape(-1, d_in)
        logits = x @ gate_w.T
        scores = jax.nn.softmax(logits, axis=-1)
        weights, idx = jax.lax.top_k(scores, TOP_K)
        base = x @ W_lin.T + b_lin
        left_sel = left[idx]
        right_sel = right[idx]
        t = jnp.einsum('nd,nkdr->nkr', x, left_sel)
        out_k = jnp.einsum('nkr,nkro->nko', t, right_sel)
        lora = jnp.sum(weights[..., None] * out_k, axis=1) * SCALING
        return (base + lora).reshape(bsz, seq, -1)
    x = x + jnp.tanh(g_xattn[0]) * _L0_xattn_ref(_layernorm(x, axis=-1), ctx_1024, L0_xattn_Wq, L0_xattn_Wkv, L0_xattn_Wo, L0_xattn_null_kv, L0_xattn_q_scale, L0_xattn_k_scale, L0_xattn_ln_in_g, L0_xattn_ln_in_b, L0_xattn_ln_ctx_g, L0_xattn_ln_ctx_b, L0_xattn_ln_out_g, L0_xattn_ln_out_b)
    x = x + jnp.tanh(g_ffn[0]) * _L0_ffn_ref(_layernorm(x, axis=-1), L0_ffn_in_proj_w, L0_ffn_in_proj_b, L0_ffn_out_proj_w, L0_ffn_out_proj_b, L0_ffn_ln1_g, L0_ffn_ln1_b, L0_ffn_ln2_g, L0_ffn_ln2_b, L0_ffn_w_group, L0_ffn_b_group, L0_ffn_w_expert, L0_ffn_b_expert, L0_ffn_w1, L0_ffn_b1, L0_ffn_w2, L0_ffn_b2)
    x = x + jnp.tanh(g_xattn[1]) * _L1_xattn_ref(_layernorm(x, axis=-1), ctx_1024, ctx_1024, L1_xattn_Wq, L1_xattn_bq, L1_xattn_Wk, L1_xattn_bk, L1_xattn_Wv, L1_xattn_bv, L1_xattn_Wo, L1_xattn_bo)
    x = x + jnp.tanh(g_ffn[1]) * _L1_ffn_ref(_layernorm(x, axis=-1), L1_ffn_Wg, L1_ffn_routing_bias, L1_ffn_W1, L1_ffn_W2, L1_ffn_W3, L1_ffn_Ws1, L1_ffn_Ws2, L1_ffn_Ws3)
    x = x + jnp.tanh(g_xattn[2]) * _L2_xattn_ref(_layernorm(x, axis=-1), ctx_1024, ctx_1024, L2_xattn_W_out, L2_xattn_b_out)
    x = x + jnp.tanh(g_ffn[2]) * _L2_ffn_ref(_layernorm(x, axis=-1), L2_ffn_router_W, L2_ffn_router_b, L2_ffn_W1, L2_ffn_b1, L2_ffn_W2, L2_ffn_b2)
    x = x + jnp.tanh(g_xattn[3]) * _L3_xattn_ref(_layernorm(x, axis=-1), ctx_1024, mask_BxS2_bf1, L3_xattn_Wq, L3_xattn_bq, L3_xattn_Wkv, L3_xattn_bkv, L3_xattn_Wo, L3_xattn_bo)
    x = x + jnp.tanh(g_ffn[3]) * _L3_ffn_ref(_layernorm(x, axis=-1), L3_ffn_W_lin, L3_ffn_b_lin, L3_ffn_gate_w, L3_ffn_left, L3_ffn_right)
    return x

_drawn_inputs = setup_inputs


def setup_inputs(seed=0):
    import zlib

    import numpy as np

    out = dict(_drawn_inputs(seed))
    spreads = {'L0_xattn_q_scale': (1.0, 0.2),
     'L0_xattn_k_scale': (1.0, 0.2),
     'L0_xattn_ln_in_g': (1.0, 0.2),
     'L0_xattn_ln_in_b': (0.0, 0.1),
     'L0_xattn_ln_ctx_g': (1.0, 0.2),
     'L0_xattn_ln_ctx_b': (0.0, 0.1),
     'L0_xattn_ln_out_g': (1.0, 0.2),
     'L0_xattn_ln_out_b': (0.0, 0.1),
     'L0_ffn_in_proj_b': (0.0, 0.1),
     'L0_ffn_out_proj_b': (0.0, 0.1),
     'L0_ffn_ln1_g': (1.0, 0.2),
     'L0_ffn_ln1_b': (0.0, 0.1),
     'L0_ffn_ln2_g': (1.0, 0.2),
     'L0_ffn_ln2_b': (0.0, 0.1),
     'L0_ffn_b_group': (0.0, 0.1),
     'L0_ffn_b_expert': (0.0, 0.305),
     'L0_ffn_b1': (0.0, 0.404),
     'L0_ffn_b2': (0.0, 0.287),
     'L1_xattn_bq': (0.0, 0.377),
     'L1_xattn_bk': (0.0, 2.0),
     'L1_xattn_bv': (0.0, 0.1),
     'L1_xattn_bo': (0.0, 0.1),
     'L1_ffn_routing_bias': (0.0, 0.8),
     'L2_ffn_router_b': (0.0, 0.8),
     'L2_ffn_b1': (0.0, 0.8),
     'L2_ffn_b2': (0.0, 0.8),
     'L3_xattn_bq': (0.0, 2.0),
     'L3_xattn_bkv': (0.0, 0.1),
     'L3_xattn_bo': (0.0, 0.1),
     'L3_ffn_b_lin': (0.0, 0.1)}
    factors = {'g_ffn': 43.488,
     'L1_ffn_Wg': 6.262,
     'L1_ffn_W1': 4.367,
     'L1_ffn_W2': 4.311,
     'L1_ffn_W3': 4.381,
     'L2_ffn_router_W': 7.21,
     'L2_ffn_W1': 8.0,
     'L2_ffn_W2': 8.0,
     'L3_ffn_gate_w': 8.0,
     'L3_ffn_left': 8.0,
     'L3_ffn_right': 8.0,
     'L1_ffn_Ws1': 2.741,
     'L1_ffn_Ws2': 2.79,
     'L1_ffn_Ws3': 2.8,
     'L2_xattn_b_out': 3.323}
    for name, (base, spread) in spreads.items():
        noise = np.random.default_rng([zlib.crc32(name.encode()), seed]).standard_normal(out[name].shape)
        drawn = base * np.exp(spread * noise) if base else spread * noise
        out[name] = jnp.asarray(drawn.astype(out[name].dtype))
    for name, factor in factors.items():
        out[name] = (out[name] * factor).astype(out[name].dtype)
    return out
```

```python
from contextlib import ExitStack

import numpy as np

import concourse.bass as bass
from concourse import mybir

FP32 = mybir.dt.float32
BF16 = mybir.dt.bfloat16
U8 = mybir.dt.uint8
ALU = mybir.AluOpType
ACT = mybir.ActivationFunctionType
AX = mybir.AxisListType

B, TQ, D = 8, 112, 256
N = B * TQ
P = 128
KD = D // P
CK, KT = 375, 125
H = 16
GROUPS = H // 2
HALF = N // 2
BANK = 512
LN_EPS = 1e-5


def bcast(ap, axis, n):
    ap = ap.unsqueeze(axis)
    shape = list(ap.shape)
    shape[axis] = n
    return ap.broadcast_to(shape)


class Chain:

    def __init__(self, engine, sem, start=0):
        self.engine, self.sem, self.start, self.k = engine, sem, start, 0

    def step(self, instruction):
        self.k += 1
        instruction.then_inc(self.sem, 1)
        self.engine.wait_ge(self.sem, self.start + self.k)


class Phases:

    def __init__(self, nc):
        self.nc, self.used, self.clearing = nc, [], []

    def sem(self, name):
        held = self.nc.semaphore(name)
        s = held.__enter__()
        self.used.append((held, s))
        return s

    def block(self, c):
        nc = self.nc
        for held, _ in self.clearing:
            held.__exit__(None, None, None)
        self.clearing, old = [], self.before
        block = c.enter_context(nc.Block())
        if old:
            @block.gpsimd
            def _(pool):
                for _, s in old:
                    pool.sem_clear(s)
        self.clearing, self.before, self.used = old, self.used, []
        return block

    before = ()



def layernorm_all(nc, core, tag, src, dst, affine=None, update=None, xT=None, xT_affine=None):
    ps, ident = core["ps"], core["ident"]
    with ExitStack() as c:
        sb = lambda n, s: c.enter_context(nc.sbuf_tensor(f"{tag}_{n}", s, FP32))
        sem = lambda n: core["phases"].sem(f"{tag}_{n}")
        stats, mv = sb("stats", [TQ, B, 6]), sb("mv", [TQ, B, 2])
        var_eps, std, rstd = sb("var_eps", [TQ, B]), sb("std", [TQ, B]), sb("rstd", [TQ, B])
        stats_ready, mv_ready, var_ready = sem("stats_ready"), sem("mv_ready"), sem("var_ready")
        std_ready, rstd_ready, rows_normal = sem("std_ready"), sem("rstd_ready"), sem("rows_normal")
        scaled, rows_ready, updated = sem("scaled"), sem("rows_ready"), sem("updated")
        transposed, copied = sem("transposed"), sem("copied")
        block = core["phases"].block(c)

        @block.vector
        def _(dve):
            for b in range(B):
                nc.vector.bn_stats(stats[:, b, :], src[:, b, :]).then_inc(stats_ready, 1)
            for b in range(B):
                dve.wait_ge(stats_ready, b + 1)
                nc.vector.bn_aggr(mv[:, b, :], stats[:, b, :]).then_inc(mv_ready, 1)
            dve.wait_ge(mv_ready, B)
            nc.vector.tensor_scalar(var_eps[:], mv[:, :, 1], LN_EPS, None, ALU.add).then_inc(var_ready, 1)
            dve.wait_ge(std_ready, 1)
            nc.vector.reciprocal(rstd[:], std[:]).then_inc(rstd_ready, 1)
            dve.wait_ge(rstd_ready, 1)
            first = rows_ready if affine is None else rows_normal
            for b in range(B):
                nc.vector.tensor_scalar(dst[:, b, :], src[:, b, :], mv[:, b, 0:1], rstd[:, b:b + 1],
                                        ALU.subtract, ALU.mult).then_inc(first, 1)
            if affine is not None:
                for b in range(B):
                    dve.wait_ge(rows_normal, b + 1)
                    nc.vector.tensor_tensor(dst[:, b, :], dst[:, b, :], affine[0][:], ALU.mult).then_inc(scaled, 1)
                for b in range(B):
                    dve.wait_ge(scaled, b + 1)
                    nc.vector.tensor_tensor(dst[:, b, :], dst[:, b, :], affine[1][:], ALU.add).then_inc(rows_ready, 1)
            if update is not None:
                x, gate = update
                for b in range(B):
                    dve.wait_ge(rows_ready, b + 1)
                    nc.vector.scalar_tensor_tensor(x[:, b, :], dst[:, b, :], gate, x[:, b, :],
                                                   ALU.mult, ALU.add).then_inc(updated, 1)

        @block.scalar
        def _(act):
            act.wait_ge(var_ready, 1)
            nc.scalar.activation(std[:], var_eps[:], ACT.Sqrt).then_inc(std_ready, 1)
            if xT is not None:
                for i in range(2 * KD):
                    chunk, k = divmod(i, KD)
                    act.wait_ge(transposed, i + 1)
                    to = xT[:, k, chunk * HALF:(chunk + 1) * HALF]
                    if xT_affine is None:
                        nc.scalar.activation(to, ps[:, i, 0:HALF], ACT.Copy).then_inc(copied, 1)
                    else:
                        nc.scalar.activation(to, ps[:, i, 0:HALF], ACT.Identity, scale=xT_affine[0][:, k:k + 1],
                                             bias=xT_affine[1][:, k:k + 1]).then_inc(copied, 1)

        if xT is not None:
            @block.tensor
            def _(pe):
                for i in range(2 * KD):
                    chunk, k = divmod(i, KD)
                    pe.wait_ge(rows_ready, 4 * (chunk + 1))
                    for j in range(4):
                        last = nc.tensor.transpose(ps[:, i, j * TQ:(j + 1) * TQ],
                                                   dst[:, 4 * chunk + j, k * P:(k + 1) * P], ident[0:TQ, 0:TQ])
                    last.then_inc(transposed, 1)



def load_all(nc, core, tag, loads, zero=()):
    with ExitStack() as c:
        landed = core["phases"].sem(f"{tag}_landed")
        cleared = core["phases"].sem(f"{tag}_cleared")
        block = core["phases"].block(c)

        @block.vector
        def _(dve):
            for t in zero:
                nc.vector.memset(t, 0.0).then_inc(cleared, 1)

        @block.sync
        def _(sp):
            if zero:
                sp.wait_ge(cleared, len(zero))
            for to, src in loads:
                sp.dma_start(to, src).then_inc(landed, 16)
            sp.wait_ge(landed, 16 * len(loads))


def attention(nc, core, tag, kind, A, x, gate, xn, xnT, out=None):
    ps, ident = core["ps"], core["ident"]
    cosine, self_, rope, raw = kind == "cosine", kind == "self", kind == "rope", kind == "raw"
    hd = 64 if cosine else 16
    width = 64 if cosine else 32
    per_set = P // width
    SETS = H // per_set
    per_half = P // hd
    inner = H * hd
    KI = inner // P
    nk = CK + 1 if cosine else TQ if self_ else CK
    tiles = [(0, TQ)] if self_ else [(t * KT, KT + (cosine and t == 2)) for t in range(3)]
    NT = len(tiles)
    scale = {"cosine": 8.0, "self": 0.25, "linear": 0.25, "rope": 0.125, "raw": 1.0}[kind]
    with ExitStack() as c:
        def sb(name, shape):
            return c.enter_context(nc.sbuf_tensor(f"{tag}_{name}", shape, FP32))

        def sem(name):
            return core["phases"].sem(f"{tag}_{name}")

        loads, zero = [], [ps[:, 4, :], ps[:, 5, :], ps[:, 6, :], ps[:, 7, :]]
        wo = sb("wo", [P, SETS, D])
        if cosine:
            loads.append((wo[:], A["wo"].rearrange("(s p) n -> p s n", p=P)))
        else:
            zero.append(wo[:])
            rows = A["wo"].rearrange("(s j r) n -> j r s n", j=per_set, r=hd)
            for j in range(per_set):
                loads.append((wo[j * width:j * width + hd, :, :], rows[j]))
        mask = sb("mask", [P, per_half])
        loads.append((mask[:], A["mask"]))
        if not raw:
            wq, wk, wv = sb("wq", [P, KD, inner]), sb("wk", [P, KD, inner]), sb("wv", [P, KD, inner])
            for w, name in ((wq, "wq"), (wk, "wk"), (wv, "wv")):
                loads.append((w[:], A[name].rearrange("(k p) n -> p k n", p=P)))
        if not raw and not cosine:
            bq, bk, bv = sb("bq", [P, KD]), sb("bk", [P, KD]), sb("bv", [KT, D])
            loads += [(bq[:], A["bq"]), (bk[:], A["bk"]), (bv[:], A["bv"].partition_broadcast(KT))]
        if not cosine:
            bo = sb("bo", [TQ, D])
            loads.append((bo[:], A["bo"].partition_broadcast(TQ)))
        if rope:
            rot, cosq, sinq = sb("rot", [P, P]), sb("cosq", [P, TQ]), sb("sinq", [P, TQ])
            cosk, sink = sb("cosk", [P, CK]), sb("sink", [P, CK])
            loads += [(rot[:], A["rot"]), (cosq[:], A["cosq"]), (sinq[:], A["sinq"]), (cosk[:], A["cosk"]), (sink[:], A["sink"])]
            allow8 = c.enter_context(nc.sbuf_tensor(f"{tag}_allow8", [1, B, CK], U8))
            hidden = c.enter_context(nc.sbuf_tensor(f"{tag}_hidden", [P, B, CK], BF16))
            one_row = c.enter_context(nc.sbuf_tensor(f"{tag}_one_row", [P, TQ], BF16))
            loads.append((allow8[:], A["allow"].rearrange("(o b) k -> o b k", o=1)))
            zero += [hidden[:], one_row[:]]
            q_raw, k_raw = sb("q_raw", [P, KD, TQ]), sb("k_raw", [P, KD, CK])
            q_cos, k_sin = sb("q_cos", [P, KD, TQ]), sb("k_sin", [P, KD, CK])
            q_sin = sb("q_sin", [P, KD, TQ])
        if cosine:
            qk_gain = sb("qk_gain", [P, 2])
            loads += [(qk_gain[:, 0:1], A["q_scale"]), (qk_gain[:, 1:2], A["k_scale"])]
            ctx_gain, ctx_offset = sb("ctx_gain", [P, KD]), sb("ctx_offset", [P, KD])
            loads += [(ctx_gain[:], A["ctx_gain"]), (ctx_offset[:], A["ctx_offset"])]
            head_mask = sb("head_mask", [P, per_half])
            null_k = sb("null_k", [KT, H, hd])
            cx = sb("cx", [KT, 3, D])
            cn = sb("cn", [KT, 3, D])
            cmv, crs = sb("cmv", [KT, 3 * B, 2]), sb("crs", [KT, 3 * B])
            k_tok, sq = sb("k_tok", [KT, 3, inner]), sb("sq", [KT, 2, BANK])
            q_tok = sb("q_tok", [TQ, inner])
            k_ss, k_norm, k_inv = sb("k_ss", [KT, 4 * H]), sb("k_norm", [KT, 4 * H]), sb("k_inv", [KT, 4 * H])
            zero.append(k_ss[:])

        xs = sb("xs", [P, KD, TQ]) if (self_ or cosine) else None
        cT = sb("cT", [P, KD, CK]) if not self_ else None
        kT = sb("kT", [P, KI, nk]) if not raw else cT
        v = sb("v", [KT + 1 if cosine else KT, 3, inner])
        qm = sb("qm", [P, H, TQ])
        probs = sb("probs", [TQ, 4, nk])
        probsT = sb("probsT", [KT + 1, 8, NT * TQ])
        nmax, sums, inv = sb("nmax", [TQ, H]), sb("sums", [TQ, H]), sb("inv", [TQ, H])
        inv_wide, invT = sb("inv_wide", [TQ, H, width]), sb("invT", [P, SETS * TQ])
        headsT = sb("headsT", [P, SETS * TQ])
        part = sb("part", [TQ, D])
        if cosine:
            loads.append((v[KT:KT + 1, 2, :].rearrange("p (h d) -> p h d", h=H), bcast(A["null_v"], 1, H)))
        load_all(nc, core, tag, loads, zero)

        if rope:
            mask_row(nc, core, tag, allow8, hidden, one_row, sb)
        if cosine:
            context_stats(nc, core, tag, A, cmv, crs)
            null_row(nc, core, tag, A, kT, head_mask, mask, qk_gain, hd, sb)

        names = ("ctx_ready vctx_ready xs_ready q_ready k_ready v_ready q_done k_done v_done rot_ready "
                 "qm_ready kT_ready scores_ready max_ready probs_ready pT_ready pTs_ready heads_ready inv_ready "
                 "invT_ready invTs_ready headsT_ready out_ready iter_done chain summed q_cos_ready "
                 "cn_ready cnT_ready cT_ready ss_ready norm_ready k_scaled kTp_ready sq_ready qTp_ready").split()
        (ctx_ready, vctx_ready, xs_ready, q_ready, k_ready, v_ready, q_done, k_done, v_done, rot_ready,
         qm_ready, kT_ready, scores_ready, max_ready, probs_ready, pT_ready, pTs_ready, heads_ready, inv_ready,
         invT_ready, invTs_ready, headsT_ready, out_ready, iter_done, chain_sem, summed, q_cos_ready,
         cn_ready, cnT_ready, cT_ready, ss_ready, norm_ready, k_scaled, kTp_ready, sq_ready,
         qTp_ready) = [sem(n) for n in names]
        block = c.enter_context(nc.Block())
        KOUT = NT * (inner // BANK) if cosine else KD
        CHAIN = {"cosine": 2, "self": 2, "linear": 2, "rope": 6, "raw": 2}[kind]

        @block.sync
        def _(sp):
            if self_:
                return
            with sp.Fori(0, B, 1) as b:
                if raw:
                    sp.wait_ge(iter_done, b + 1)
                    sp.dma_start(cT[:], A["ctxT"][b]).then_inc(ctx_ready, 16)
                    sp.dma_start(v[:, :, :], A["ctx"][b].rearrange("(t p) d -> p t d", p=KT)).then_inc(vctx_ready, 16)
                elif cosine:
                    sp.wait_ge(cn_ready, b + 1)
                    sp.dma_start(cx[:], A["ctx"][b].rearrange("(t p) d -> p t d", p=KT)).then_inc(ctx_ready, 16)
                else:
                    sp.wait_ge(v_ready, NT * b + 1)
                    sp.dma_start(cT[:], A["ctxT"][b]).then_inc(ctx_ready, 16)

        @block.gpsimd
        def _(pool):
            if self_ or cosine:
                with pool.Fori(0, B, 1) as b:
                    pool.wait_ge(iter_done, b + 1)
                    pool.tensor_copy(xs[:], xnT[:, :, bass.ds(b * TQ, TQ)]).then_inc(xs_ready, 1)
            if rope:
                with pool.Fori(0, B, 1) as b:
                    pool.wait_ge(q_done, KD * (b + 1))
                    pool.tensor_tensor(q_cos[:], q_raw[:], bcast(cosq[:], 1, KD), ALU.mult).then_inc(q_cos_ready, 1)
                    for k in range(KD):
                        pool.wait_ge(k_done, KD * b + k + 1)
                        pool.wait_ge(iter_done, b + 1)
                        pool.tensor_tensor(kT[:, k, :], k_raw[:, k, :], cosk[:], ALU.mult).then_inc(q_cos_ready, 1)

        @block.tensor
        def _(pe):
            if not cosine:
                pe.sem_inc(v_ready, 1)
            with pe.Fori(0, B, 1) as b:
                pe.wait_ge(iter_done, b + 1)
                if cosine:
                    pe.wait_ge(cn_ready, b + 2)
                    for k in range(KD):
                        for t in range(3):
                            last = nc.tensor.transpose(ps[:, k, t * KT:(t + 1) * KT], cn[:, t, k * P:(k + 1) * P],
                                                       ident[0:KT, 0:KT])
                        last.then_inc(cnT_ready, 1)
                    pe.wait_ge(xs_ready, b + 1)
                    for n in range(2):
                        for k in range(KD):
                            last = nc.tensor.matmul(ps[0:TQ, 2 + n, :], xs[:, k, :], wq[:, k, n * BANK:(n + 1) * BANK],
                                                    start=k == 0, stop=k == KD - 1)
                        last.then_inc(q_ready, 1)
                    pe.wait_ge(cT_ready, KD * (b + 1))
                    for i in range(KOUT):
                        t, n = divmod(i, 2)
                        if i >= 4:
                            pe.wait_ge(k_done, KOUT * b + i - 3)
                        for k in range(KD):
                            last = nc.tensor.matmul(ps[0:KT, 4 + i % 4, :], cT[:, k, t * KT:(t + 1) * KT],
                                                    wk[:, k, n * BANK:(n + 1) * BANK], start=k == 0, stop=k == KD - 1)
                        last.then_inc(k_ready, 1)
                    for i in range(KOUT):
                        t, n = divmod(i, 2)
                        if i < 2:
                            pe.wait_ge(k_done, KOUT * b + i + 3)
                        elif i < 4:
                            pe.wait_ge(k_done, KOUT * b + i + 3)
                        else:
                            pe.wait_ge(v_done, KOUT * b + i - 3)
                        bank = 4 + (i + 2) % 4
                        for k in range(KD):
                            last = nc.tensor.matmul(ps[0:KT, bank, :], cT[:, k, t * KT:(t + 1) * KT],
                                                    wv[:, k, n * BANK:(n + 1) * BANK], start=k == 0, stop=k == KD - 1)
                        last.then_inc(v_ready, 1)
                    pe.wait_ge(k_scaled, 4 * (b + 1))
                    for i in range(2):
                        if i == 0:
                            pe.wait_ge(q_done, 2 * (b + 1))
                        for j in range(4):
                            last = nc.tensor.transpose(ps[:, 2 + i, j * TQ:(j + 1) * TQ],
                                                       q_tok[:, (4 * i + j) * P:(4 * i + j + 1) * P], ident[0:TQ, 0:TQ])
                        last.then_inc(qTp_ready, 1)
                    for i in range(KI):
                        if i >= 2:
                            pe.wait_ge(kT_ready, KI * b + i - 1)
                        else:
                            pe.wait_ge(cT_ready, KD * (b + 1))
                        for t in range(3):
                            last = nc.tensor.transpose(ps[:, i % 2, t * KT:(t + 1) * KT], k_tok[:, t, i * P:(i + 1) * P],
                                                       ident[0:KT, 0:KT])
                        last.then_inc(kTp_ready, 1)
                elif not raw:
                    if self_:
                        pe.wait_ge(xs_ready, b + 1)
                    else:
                        pe.wait_ge(ctx_ready, 16 * b + 16)
                    src = xs if self_ else cT
                    for m in range(KD):
                        for k in range(KD):
                            last = nc.tensor.matmul(ps[:, 0, m * TQ:(m + 1) * TQ], wq[:, k, m * P:(m + 1) * P],
                                                    xs[:, k, :] if self_ else xnT[:, k, bass.ds(b * TQ, TQ)],
                                                    start=k == 0, stop=k == KD - 1)
                    last.then_inc(q_ready, 1)
                    for m in range(KD):
                        for k in range(KD):
                            last = nc.tensor.matmul(ps[:, 1 + m, 0:nk], wk[:, k, m * P:(m + 1) * P], src[:, k, :],
                                                    start=k == 0, stop=k == KD - 1)
                        last.then_inc(k_ready, 1)
                    for t, (at, kt) in enumerate(tiles):
                        for k in range(KD):
                            last = nc.tensor.matmul(ps[0:kt, 3 + t, 0:D], src[:, k, at:at + kt], wv[:, k, :],
                                                    start=k == 0, stop=k == KD - 1)
                        last.then_inc(v_ready, 1)
                    last_proj = last
                    if rope:
                        pe.wait_ge(q_done, KD * (b + 1))
                        for m in range(KD):
                            last = nc.tensor.matmul(ps[:, 6, m * TQ:(m + 1) * TQ], rot[:], q_raw[:, m, :], start=True, stop=True)
                        last.then_inc(rot_ready, 1)
                        for m in range(KD):
                            pe.wait_ge(k_done, KD * b + m + 1)
                            nc.tensor.matmul(ps[:, 1 + m, 0:nk], rot[:], k_raw[:, m, :], start=True, stop=True).then_inc(rot_ready, 1)
                if raw:
                    pe.wait_ge(ctx_ready, 16 * b + 16)
                    pe.wait_ge(vctx_ready, 16 * b + 16)
                else:
                    pe.wait_ge(kT_ready, (KI if cosine else KD) * (b + 1))
                pe.wait_ge(qm_ready, 2 * (b + 1))
                if not raw:
                    pe.wait_ge(v_done, (KOUT if cosine else NT) * (b + 1))
                sets_done = 0
                for step in range(GROUPS + 4):
                    if step < GROUPS:
                        if step >= 2:
                            pe.wait_ge(probs_ready, H * b + 2 * (step - 1))
                        for h in (2 * step, 2 * step + 1):
                            last = nc.tensor.matmul(ps[0:TQ, h % 4, 0:nk], qm[:, h, :], kT[:, h // per_half, :],
                                                    start=True, stop=not rope)
                            if rope:
                                last = nc.tensor.matmul(ps[0:TQ, h % 4, 0:nk], one_row[:], hidden[:, b, :], start=False, stop=True)
                        last.then_inc(scores_ready, 1)
                    if 2 <= step < GROUPS + 2:
                        for h in (2 * step - 4, 2 * step - 3):
                            pe.wait_ge(probs_ready, H * b + h + 1)
                            if h >= 2:
                                pe.wait_ge(pTs_ready, H * b + h - 1)
                            for t, (at, kt) in enumerate(tiles):
                                last = nc.tensor.transpose(ps[0:kt, 4 + h % 2, t * TQ:(t + 1) * TQ],
                                                           probs[:, h % 4, at:at + kt], ident[0:TQ, 0:TQ])
                            last.then_inc(pT_ready, 1)
                    while sets_done < SETS and (sets_done + 1) * per_set <= 2 * (step - 2):
                        s = sets_done
                        pe.wait_ge(pTs_ready, H * b + (s + 1) * per_set)
                        for t, (at, kt) in enumerate(tiles):
                            for j in range(per_set):
                                h = s * per_set + j
                                last = nc.tensor.matmul(
                                    ps[j * width:j * width + hd, 6 + s // 4, (s % 4) * TQ:(s % 4 + 1) * TQ],
                                    v[0:kt, t, h * hd:(h + 1) * hd], probsT[0:kt, h % 8, t * TQ:(t + 1) * TQ],
                                    start=t == 0, stop=t == NT - 1)
                        last.then_inc(heads_ready, 1)
                        sets_done += 1
                assert sets_done == SETS
                pe.wait_ge(inv_ready, b + 1)
                for s in range(SETS):
                    last = nc.tensor.transpose(ps[:, s // 4, (s % 4) * TQ:(s % 4 + 1) * TQ],
                                               inv_wide[:, s * per_set:(s + 1) * per_set, :].rearrange("p h w -> p (h w)"),
                                               ident[0:TQ, 0:TQ])
                last.then_inc(invT_ready, 1)
                pe.wait_ge(headsT_ready, (SETS // 4) * (b + 1))
                for s in range(SETS):
                    last = nc.tensor.matmul(ps[0:TQ, 2, 0:D], headsT[:, s * TQ:(s + 1) * TQ], wo[:, s, :],
                                            start=s == 0, stop=s == SETS - 1)
                last.then_inc(out_ready, 1)
                if not (self_ or raw or cosine):
                    pass

        @block.scalar
        def _(act):
            with act.Fori(0, B, 1) as b:
                if cosine:
                    for k in range(KD):
                        act.wait_ge(cnT_ready, KD * b + k + 1)
                        nc.scalar.activation(cT[:, k, :], ps[:, k, 0:CK], ACT.Identity, scale=ctx_gain[:, k:k + 1],
                                             bias=ctx_offset[:, k:k + 1]).then_inc(cT_ready, 1)
                    for i in range(2 + KOUT):
                        if i < 2:
                            act.wait_ge(q_ready, 2 * b + i + 1)
                            src = ps[0:TQ, 2 + i, :]
                            to = sq[0:TQ, i % 2, :]
                        else:
                            act.wait_ge(k_ready, KOUT * b + i - 1)
                            src = ps[0:KT, 4 + (i - 2) % 4, :]
                            to = sq[:, i % 2, :]
                        if i >= 2:
                            act.wait_ge(summed, (2 + KOUT) * b + i - 1)
                        nc.scalar.activation(to, src, ACT.Square).then_inc(sq_ready, 1)
                    for i in range(KOUT):
                        t, n = divmod(i, 2)
                        act.wait_ge(v_ready, KOUT * b + i + 1)
                        nc.scalar.activation(v[0:KT, t, n * BANK:(n + 1) * BANK], ps[0:KT, 4 + (i + 2) % 4, :],
                                             ACT.Copy).then_inc(v_done, 1)
                    act.wait_ge(ss_ready, b + 1)
                    nc.scalar.activation(k_norm[:], k_ss[:], ACT.Sqrt).then_inc(norm_ready, 1)
                    for i in range(KI):
                        act.wait_ge(kTp_ready, KI * b + i + 1)
                        nc.scalar.activation(kT[:, i, 0:CK], ps[:, i % 2, 0:CK], ACT.Copy).then_inc(kT_ready, 1)
                elif not raw:
                    if rope:
                        act.wait_ge(q_ready, b + 1)
                        for m in range(KD):
                            nc.scalar.activation(q_raw[:, m, :], ps[:, 0, m * TQ:(m + 1) * TQ], ACT.Identity,
                                                 bias=bq[:, m:m + 1]).then_inc(q_done, 1)
                    for m in range(KD):
                        act.wait_ge(k_ready, KD * b + m + 1)
                        to = k_raw if rope else kT
                        nc.scalar.activation(to[:, m, :], ps[:, 1 + m, 0:nk], ACT.Identity,
                                             bias=bk[:, m:m + 1]).then_inc(k_done if rope else kT_ready, 1)
                for h in range(H):
                    act.wait_ge(max_ready, GROUPS * b + h // 2 + 1)
                    if h >= 4:
                        act.wait_ge(pT_ready, H * b + h - 3)
                    src = ps[0:TQ, h % 4, 0:nk]
                    nc.scalar.activation(probs[:, h % 4, :], src, ACT.Exp, bias=nmax[:, h:h + 1],
                                         accum_out=sums[:, h:h + 1]).then_inc(probs_ready, 1)
                act.wait_ge(invT_ready, b + 1)
                for i in range(SETS // 4):
                    nc.scalar.activation(invT[:, i * 4 * TQ:(i + 1) * 4 * TQ], ps[:, i, 0:4 * TQ],
                                         ACT.Copy).then_inc(invTs_ready, 1)

        @block.vector
        def _(dve):
            dve.sem_inc(iter_done, 1)
            if cosine:
                dve.sem_inc(cn_ready, 1)
            with dve.Fori(0, B, 1) as b:
                chain = Chain(dve, chain_sem, CHAIN * b)
                if cosine:
                    dve.wait_ge(ctx_ready, 16 * b + 16)
                    for t in range(3):
                        mean, inv_std = cmv[:, bass.ds(3 * b + t, 1), 0], crs[:, bass.ds(3 * b + t, 1)]
                        last = nc.vector.tensor_scalar(cn[:, t, :], cx[:, t, :], mean, inv_std, ALU.subtract, ALU.mult)
                    last.then_inc(cn_ready, 1)
                    for i in range(2 + KOUT):
                        dve.wait_ge(sq_ready, (2 + KOUT) * b + i + 1)
                        if i < 2:
                            rows, bank, to = TQ, 2 + i, q_tok[:, i * BANK:(i + 1) * BANK]
                            done, at = q_done, i * 8
                        else:
                            t, n = divmod(i - 2, 2)
                            rows, bank, to = KT, 4 + (i - 2) % 4, k_tok[:, t, n * BANK:(n + 1) * BANK]
                            done, at = k_done, (t + 1) * H + n * 8
                        nc.vector.tensor_copy(to, ps[0:rows, bank, :]).then_inc(done, 1)
                        nc.vector.tensor_reduce(k_ss[0:rows, at:at + 8], sq[0:rows, i % 2, :].rearrange("p (h d) -> p h d", d=hd),
                                                AX.X, ALU.add).then_inc(summed, 1)
                    dve.wait_ge(summed, (2 + KOUT) * (b + 1))
                    nc.vector.tensor_scalar(k_ss[:], k_ss[:], 1e-24, None, ALU.max).then_inc(ss_ready, 1)
                    dve.wait_ge(norm_ready, b + 1)
                    chain.step(nc.vector.reciprocal(k_inv[:], k_norm[:]))
                    q3 = q_tok[:].rearrange("p (h d) -> p h d", d=hd)
                    nc.vector.tensor_tensor(q3, q3, bcast(k_inv[0:TQ, 0:H], 2, hd), ALU.mult).then_inc(k_scaled, 1)
                    for t in range(3):
                        k3 = k_tok[:, t, :].rearrange("p (h d) -> p h d", d=hd)
                        nc.vector.tensor_tensor(k3, k3, bcast(k_inv[:, (t + 1) * H:(t + 2) * H], 2, hd),
                                                ALU.mult).then_inc(k_scaled, 1)
                    for i in range(2):
                        dve.wait_ge(qTp_ready, 2 * b + i + 1)
                        nc.vector.tensor_tensor(
                            qm[:, 8 * i:8 * i + 8, :].rearrange("p (i j) q -> p i j q", j=2),
                            bcast(ps[:, 2 + i, 0:4 * TQ].rearrange("p (i q) -> p i q", q=TQ), 2, 2),
                            bcast(bcast(head_mask[:], 1, 4), 3, TQ), ALU.mult).then_inc(qm_ready, 1)
                elif raw:
                    for m in range(KD):
                        nc.vector.tensor_tensor(qm[:, m * per_half:(m + 1) * per_half, :],
                                                bcast(xnT[:, m, bass.ds(b * TQ, TQ)], 1, per_half),
                                                bcast(mask[:], 2, TQ), ALU.mult).then_inc(qm_ready, 1)
                else:
                    if not rope:
                        dve.wait_ge(q_ready, b + 1)
                        for m in range(KD):
                            nc.vector.scalar_tensor_tensor(qm[:, m * per_half:(m + 1) * per_half, :],
                                                           bcast(ps[:, 0, m * TQ:(m + 1) * TQ], 1, per_half), bq[:, m:m + 1],
                                                           bcast(mask[:], 2, TQ), ALU.add, ALU.mult).then_inc(qm_ready, 1)
                    for t, (at, kt) in enumerate(tiles):
                        dve.wait_ge(v_ready, NT * b + t + 2)
                        nc.vector.tensor_tensor(v[0:kt, t, :], ps[0:kt, 3 + t, 0:D], bv[0:kt, :], ALU.add).then_inc(v_done, 1)
                    if rope:
                        dve.wait_ge(rot_ready, 3 * b + 1)
                        chain.step(nc.vector.tensor_tensor(q_sin[:], ps[:, 6, 0:KD * TQ].rearrange("p (k q) -> p k q", k=KD),
                                                           bcast(sinq[:], 1, KD), ALU.mult))
                        dve.wait_ge(q_cos_ready, 3 * b + 1)
                        chain.step(nc.vector.tensor_tensor(q_sin[:], q_sin[:], q_cos[:], ALU.add))
                        for m in range(KD):
                            nc.vector.tensor_tensor(qm[:, m * per_half:(m + 1) * per_half, :],
                                                    bcast(q_sin[:, m, :], 1, per_half), bcast(mask[:], 2, TQ),
                                                    ALU.mult).then_inc(qm_ready, 1)
                        for m in range(KD):
                            dve.wait_ge(rot_ready, 3 * b + 2 + m)
                            chain.step(nc.vector.tensor_tensor(k_sin[:, m, :], ps[:, 1 + m, 0:nk], sink[:], ALU.mult))
                            dve.wait_ge(q_cos_ready, 3 * b + 2 + m)
                            nc.vector.tensor_tensor(kT[:, m, :], kT[:, m, :], k_sin[:, m, :], ALU.add).then_inc(kT_ready, 1)
                for step in range(GROUPS + 2):
                    if step < GROUPS:
                        g = step
                        dve.wait_ge(scores_ready, GROUPS * b + g + 1)
                        lo = 2 * (g % 2)
                        nc.vector.tensor_reduce(nmax[:, 2 * g:2 * g + 2], ps[0:TQ, lo:lo + 2, 0:nk], AX.X, ALU.max,
                                                negate=True).then_inc(max_ready, 1)
                    if step >= 2:
                        for h in (2 * step - 4, 2 * step - 3):
                            dve.wait_ge(pT_ready, H * b + h + 1)
                            if h >= 8:
                                dve.wait_ge(heads_ready, SETS * b + (h - 8) // per_set + 1)
                            rows = tiles[-1][1]
                            nc.vector.tensor_copy(probsT[0:rows, h % 8, :], ps[0:rows, 4 + h % 2, 0:NT * TQ]).then_inc(pTs_ready, 1)
                dve.wait_ge(probs_ready, H * (b + 1))
                chain.step(nc.vector.reciprocal(inv[:], sums[:]))
                nc.vector.tensor_copy(inv_wide[:], bcast(inv[:], 2, width)).then_inc(inv_ready, 1)
                dve.wait_ge(heads_ready, SETS * (b + 1))
                for i in range(SETS // 4):
                    dve.wait_ge(invTs_ready, (SETS // 4) * b + i + 1)
                    nc.vector.tensor_tensor(headsT[:, i * 4 * TQ:(i + 1) * 4 * TQ], ps[:, 6 + i, 0:4 * TQ],
                                            invT[:, i * 4 * TQ:(i + 1) * 4 * TQ], ALU.mult).then_inc(headsT_ready, 1)
                dve.wait_ge(out_ready, b + 1)
                if cosine:
                    nc.vector.tensor_copy(out[:, b, :], ps[0:TQ, 2, 0:D]).then_inc(iter_done, 1)
                else:
                    chain.step(nc.vector.tensor_tensor(part[:], ps[0:TQ, 2, 0:D], bo[:], ALU.add))
                    if self_:
                        nc.vector.tensor_tensor(out[:, b, :], part[:], xn[:, b, :], ALU.add).then_inc(iter_done, 1)
                    else:
                        nc.vector.scalar_tensor_tensor(x[:, b, :], part[:], gate, x[:, b, :], ALU.mult,
                                                       ALU.add).then_inc(iter_done, 1)
                assert chain.k == CHAIN


def mask_row(nc, core, tag, allow8, hidden, one_row, sb):
    allow = sb("allow", [1, B, CK])
    with ExitStack() as c:
        steps = core["phases"].sem(f"{tag}_mask_steps")
        block = core["phases"].block(c)

        @block.vector
        def _(dve):
            chain = Chain(dve, steps)
            chain.step(nc.vector.tensor_copy(allow[:], allow8[:]))
            chain.step(nc.vector.tensor_scalar(hidden[0:1, :, :], allow[:], 1.0, 3e38, ALU.subtract, ALU.mult))
            chain.step(nc.vector.memset(one_row[0:1, :], 1.0))


def context_stats(nc, core, tag, A, cmv, crs):
    R = 3 * B
    with ExitStack() as c:
        sb = lambda n, s: c.enter_context(nc.sbuf_tensor(f"{tag}_{n}", s, FP32))
        sem = lambda n: core["phases"].sem(f"{tag}_c_{n}")
        rows, stats, var_eps, std = sb("rows", [KT, R, D]), sb("rstats", [KT, R, 6]), sb("var_eps", [KT, R]), sb("rstd", [KT, R])
        landed = [sem(f"landed_{q}") for q in range(4)]
        stats_ready, mv_ready, var_ready, std_ready, inv_ready = [sem(n) for n in ("stats", "mv", "var", "std", "inv")]
        block = core["phases"].block(c)

        @block.sync
        def _(sp):
            for q in range(4):
                sp.dma_start(rows[:, 6 * q:6 * q + 6, :],
                             A["ctx"][2 * q:2 * q + 2].rearrange("b (t p) d -> p (b t) d", p=KT)).then_inc(landed[q], 16)

        @block.vector
        def _(dve):
            for r in range(R):
                if r % 6 == 0:
                    dve.wait_ge(landed[r // 6], 16)
                nc.vector.bn_stats(stats[:, r, :], rows[:, r, :]).then_inc(stats_ready, 1)
            for r in range(R):
                dve.wait_ge(stats_ready, r + 1)
                nc.vector.bn_aggr(cmv[:, r, :], stats[:, r, :]).then_inc(mv_ready, 1)
            dve.wait_ge(mv_ready, R)
            nc.vector.tensor_scalar(var_eps[:], cmv[:, :, 1], LN_EPS, None, ALU.add).then_inc(var_ready, 1)
            dve.wait_ge(std_ready, 1)
            nc.vector.reciprocal(crs[:], std[:]).then_inc(inv_ready, 1)
            dve.wait_ge(inv_ready, 1)

        @block.scalar
        def _(act):
            act.wait_ge(var_ready, 1)
            nc.scalar.activation(std[:], var_eps[:], ACT.Sqrt).then_inc(std_ready, 1)


def null_row(nc, core, tag, A, kT, head_mask, mask, qk_gain, hd, sb):
    ps = core["ps"]
    nk_col, sq_col, both, tmp = sb("null_col", [P, 1]), sb("null_sq", [P, 1]), sb("same_head", [P, P]), sb("null_norm", [P, 4])
    with ExitStack() as c:
        sem = lambda n: core["phases"].sem(f"{tag}_n_{n}")
        landed, dve_steps, norm_ready, root = sem("landed"), sem("steps"), sem("norm_ready"), sem("root")
        block = core["phases"].block(c)

        @block.sync
        def _(sp):
            sp.dma_start(nk_col[:], A["null_k"]).then_inc(landed, 16)
            sp.dma_start(both[:], A["same_head"]).then_inc(landed, 16)
            sp.wait_ge(landed, 32)

        @block.vector
        def _(dve):
            chain = Chain(dve, dve_steps)
            dve.wait_ge(landed, 32)
            chain.step(nc.vector.tensor_tensor(sq_col[:], nk_col[:], nk_col[:], ALU.mult))
            dve.wait_ge(norm_ready, 1)
            chain.step(nc.vector.tensor_scalar(tmp[:, 0:1], ps[:, 0, 0:1], 1e-24, None, ALU.max))
            dve.wait_ge(root, 1)
            chain.step(nc.vector.reciprocal(tmp[:, 2:3], tmp[:, 1:2]))
            chain.step(nc.vector.tensor_tensor(tmp[:, 3:4], nk_col[:], tmp[:, 2:3], ALU.mult))
            chain.step(nc.vector.tensor_copy(kT[:, :, CK:CK + 1], bcast(tmp[:, 3:4], 1, kT.shape[1])))
            chain.step(nc.vector.tensor_scalar(head_mask[:], mask[:], qk_gain[:, 0:1], qk_gain[:, 1:2], ALU.mult, ALU.mult))

        @block.tensor
        def _(pe):
            pe.wait_ge(dve_steps, 1)
            nc.tensor.matmul(ps[:, 0, 0:1], both[:], sq_col[:], start=True, stop=True).then_inc(norm_ready, 1)

        @block.scalar
        def _(act):
            act.wait_ge(dve_steps, 2)
            nc.scalar.activation(tmp[:, 1:2], tmp[:, 0:1], ACT.Sqrt).then_inc(root, 1)



def ranks(nc, chain, logits, before, E, greater, equal, rank):
    over_j, over_e = bcast(logits, 2, E), bcast(logits, 3, E)
    chain.step(nc.vector.tensor_tensor(greater, over_j, over_e, ALU.is_gt))
    chain.step(nc.vector.tensor_tensor(equal, over_j, over_e, ALU.is_equal))
    chain.step(nc.vector.tensor_tensor(equal, equal, bcast(before, 1, B), ALU.mult))
    chain.step(nc.vector.tensor_tensor(greater, greater, equal, ALU.add))
    chain.step(nc.vector.tensor_reduce(rank, greater, AX.X, ALU.add))


def route(nc, core, tag, kind, A, xT, gates, y=None):
    ps, ident = core["ps"], core["ident"]
    G, E = 4, 8
    cols = G + E if kind == "hier" else E
    b2_in = kind in ("hier", "top1")
    with ExitStack() as c:
        sb = lambda n, s: c.enter_context(nc.sbuf_tensor(f"{tag}_{n}", s, FP32))
        sem = lambda n: core["phases"].sem(f"{tag}_{n}")
        wr, bias, before = sb("wr", [P, KD, cols]), sb("bias", [TQ, cols]), sb("before", [TQ, E, E])
        logits = sb("logits", [TQ, B, cols])
        greater, equal = sb("greater", [TQ, B, E, E]), sb("equal", [TQ, B, E, E])
        rank, top, picked = sb("rank", [TQ, B, E]), sb("top", [TQ, B]), sb("picked", [TQ, B, E])
        shifted, exps = sb("shifted", [TQ, B, E]), sb("exps", [TQ, B, E])
        total, inv = sb("total", [TQ, B]), sb("inv", [TQ, B])
        loads = [(wr[:], A["wr"].rearrange("(k p) n -> p k n", p=P)), (before[:], A["before"].partition_broadcast(TQ))]
        if "br" in A:
            loads.append((bias[:], A["br"].partition_broadcast(TQ)))
        if b2_in:
            b2, gatesT = sb("b2", [E, D]), sb("gatesT", [E, N])
            loads.append((b2[:], A["b2"]))
        if kind == "hier":
            etop, eshift, eexp = sb("etop", [TQ, B, G]), sb("eshift", [TQ, B, G, 2]), sb("eexp", [TQ, B, G, 2])
            etotal, einv, epick = sb("etotal", [TQ, B, G]), sb("einv", [TQ, B, G]), sb("epick", [TQ, B, G, 2])
        load_all(nc, core, tag, loads)
        logits_ready, steps, exp_asked, exp_ready = sem("logits_ready"), sem("steps"), sem("exp_asked"), sem("exp_ready")
        gates_ready, gatesT_ready, gatesT_copied = sem("gates_ready"), sem("gatesT_ready"), sem("gatesT_copied")
        y_ready, y_copied = sem("y_ready"), sem("y_copied")
        block = core["phases"].block(c)

        @block.tensor
        def _(pe):
            for b in range(B):
                for k in range(KD):
                    last = nc.tensor.matmul(ps[0:TQ, 0, b * cols:(b + 1) * cols], xT[:, k, b * TQ:(b + 1) * TQ],
                                            wr[:, k, :], start=k == 0, stop=k == KD - 1)
            last.then_inc(logits_ready, 1)
            if b2_in:
                pe.wait_ge(gates_ready, 1)
                for b in range(B):
                    last = nc.tensor.transpose(ps[0:E, 1 + b // 4, (b % 4) * TQ:(b % 4 + 1) * TQ], gates[:, b, 0:E],
                                               ident[0:TQ, 0:TQ])
                last.then_inc(gatesT_ready, 1)
                pe.wait_ge(gatesT_copied, 2)
                for b in range(B):
                    if b >= 4:
                        pe.wait_ge(y_copied, b - 3)
                    nc.tensor.matmul(ps[0:TQ, 4 + b % 4, 0:D], gatesT[:, b * TQ:(b + 1) * TQ], b2[:],
                                     start=True, stop=True).then_inc(y_ready, 1)

        @block.scalar
        def _(act):
            act.wait_ge(exp_asked, 1)
            nc.scalar.activation(exps[:, :, 0:G if kind == "hier" else E], shifted[:, :, 0:G if kind == "hier" else E],
                                 ACT.Exp).then_inc(exp_ready, 1)
            if kind == "hier":
                nc.scalar.activation(eexp[:], eshift[:], ACT.Exp).then_inc(exp_ready, 1)

        @block.vector
        def _(dve):
            chain = Chain(dve, steps)
            v = nc.vector
            dve.wait_ge(logits_ready, 1)
            from_pe = ps[0:TQ, 0, 0:B * cols].rearrange("p (b e) -> p b e", e=cols)
            if "br" in A:
                chain.step(v.tensor_tensor(logits[:], from_pe, bcast(bias[:], 1, B), ALU.add))
            else:
                chain.step(v.tensor_copy(logits[:], from_pe))
            choose = G if kind == "hier" else E
            lg = logits[:, :, 0:choose]
            chain.step(v.tensor_reduce(top[:], lg, AX.X, ALU.max))
            sh = shifted[:, :, 0:choose]
            if kind == "hier":
                el = logits[:, :, G:].rearrange("p b (g e) -> p b g e", e=2)
                chain.step(v.tensor_reduce(etop[:], el, AX.X, ALU.max))
                chain.step(v.tensor_tensor(eshift[:], el, bcast(etop[:], 3, 2), ALU.subtract))
            v.tensor_tensor(sh, lg, bcast(top[:], 2, choose), ALU.subtract).then_inc(exp_asked, 1)
            ranks(nc, chain, lg, before[:, 0:choose, 0:choose], choose, greater[:, :, 0:choose, 0:choose],
                  equal[:, :, 0:choose, 0:choose], rank[:, :, 0:choose])
            k = {"hier": 1, "top1": 1, "top4": 4, "top2": 2}[kind]
            chain.step(v.tensor_scalar(picked[:, :, 0:choose], rank[:, :, 0:choose], k - 0.5, None, ALU.is_lt))
            dve.wait_ge(exp_ready, 2 if kind == "hier" else 1)
            ex = exps[:, :, 0:choose]
            if kind == "top4":
                chain.step(v.tensor_tensor(ex, ex, picked[:], ALU.mult))
            chain.step(v.tensor_reduce(total[:], ex, AX.X, ALU.add))
            chain.step(v.reciprocal(inv[:], total[:]))
            if kind == "hier":
                chain.step(v.tensor_reduce(etotal[:], eexp[:], AX.X, ALU.add))
                chain.step(v.reciprocal(einv[:], etotal[:]))
                chain.step(v.tensor_tensor(epick[:, :, :, 0], el[:, :, :, 0], el[:, :, :, 1], ALU.is_ge))
                chain.step(v.tensor_tensor(epick[:, :, :, 1], el[:, :, :, 1], el[:, :, :, 0], ALU.is_gt))
                chain.step(v.tensor_tensor(einv[:], einv[:], bcast(inv[:], 2, G), ALU.mult))
                chain.step(v.tensor_tensor(einv[:], einv[:], picked[:, :, 0:G], ALU.mult))
                v.tensor_tensor(gates[:, :, 0:E].rearrange("p b (g e) -> p b g e", e=2), epick[:], bcast(einv[:], 3, 2),
                                ALU.mult).then_inc(gates_ready, 1)
            elif kind == "top1":
                v.tensor_tensor(gates[:, :, 0:E], picked[:], bcast(inv[:], 2, E), ALU.mult).then_inc(gates_ready, 1)
            else:
                if kind == "top2":
                    chain.step(v.tensor_tensor(ex, ex, picked[:], ALU.mult))
                v.tensor_tensor(gates[:, :, 0:E], ex, bcast(inv[:], 2, E), ALU.mult).then_inc(gates_ready, 1)
            if kind == "top4":
                v.memset(gates[:, :, E:E + 1], 1.0).then_inc(gates_ready, 1)
                v.memset(y[:], 0.0).then_inc(gates_ready, 1)
            if b2_in:
                for i in range(2):
                    dve.wait_ge(gatesT_ready, 1)
                    v.tensor_copy(gatesT[:, i * HALF:(i + 1) * HALF], ps[0:E, 1 + i, 0:HALF]).then_inc(gatesT_copied, 1)
                for b in range(B):
                    dve.wait_ge(y_ready, b + 1)
                    v.tensor_copy(y[:, b, :], ps[0:TQ, 4 + b % 4, 0:D]).then_inc(y_copied, 1)


def experts(nc, core, tag, A, xT, gates, y, E, F, tile, swiglu):
    ps = core["ps"]
    NF = -(-F // tile)
    size = [min(tile, F - f * tile) for f in range(NF)]
    UP = ("w1", "w2") if swiglu else ("w1",)
    down = A["w3"] if swiglu else A["w2"]
    LOADS = len(UP) + 1 + (size[-1] != tile) + (not swiglu)
    with ExitStack() as c:
        sb = lambda n, s: c.enter_context(nc.sbuf_tensor(f"{tag}_{n}", s, FP32))
        sem = lambda n: core["phases"].sem(f"{tag}_{n}")
        up_w = [[sb(f"{u}_{s}", [P, KD, F]) for u in UP] for s in range(2)]
        down_w = [sb(f"down_{s}", [tile, NF, D]) for s in range(2)]
        hT = sb("hT", [tile, NF, N])
        if swiglu:
            sig, gated = sb("sig", [tile, 2, HALF]), sb("gated", [tile, 2, HALF])
        else:
            b1 = [sb(f"b1_{s}", [P, NF]) for s in range(2)]
        weights_ready = [sem("weights_ready_0"), sem("weights_ready_1")]
        weights_used, up_ready, sig_ready, gated_ready = sem("weights_used"), sem("up_ready"), sem("sig_ready"), sem("gated_ready")
        hT_ready, y_ready, y_added = sem("hT_ready"), sem("y_ready"), sem("y_added")
        PARTS = 2 * NF
        BANKS = 2 if swiglu else 4
        block = c.enter_context(nc.Block())

        def pairs(engine, one, first=0):
            for n in range(first):
                one(n, n % 2, n // 2)
            with engine.Fori(first // 2, E // 2, 1) as i:
                for s in range(2):
                    one(2 * i + s, s, i)
            if E % 2:
                one(E - 1, 0, E // 2)

        @block.sync
        def _(sp):
            def load(n, s, i):
                if not isinstance(n, int) or n >= 2:
                    sp.wait_ge(weights_used, n - 1)
                for u, w in zip(UP, up_w[s]):
                    sp.dma_start(w[:], A[u][n].rearrange("(k p) f -> p k f", p=P)).then_inc(weights_ready[s], 16)
                if not swiglu:
                    sp.dma_start(b1[s][:], A["b1"][n]).then_inc(weights_ready[s], 16)
                whole = NF if size[-1] == tile else NF - 1
                sp.dma_start(down_w[s][:, 0:whole, :], down[n, 0:whole * tile, :].rearrange("(f p) d -> p f d", p=tile)).then_inc(weights_ready[s], 16)
                if whole < NF:
                    sp.dma_start(down_w[s][0:size[-1], whole, :], down[n, whole * tile:F, :]).then_inc(weights_ready[s], 16)
            pairs(sp, load, first=2)

        @block.tensor
        def _(pe):
            def one(n, s, i):
                pe.wait_ge(weights_ready[s], i * (16 * LOADS) + 16 * LOADS)
                for part in range(PARTS):
                    f, chunk = divmod(part, 2)
                    if part >= BANKS:
                        pe.wait_ge(hT_ready, n * PARTS + part - BANKS + 2)
                    else:
                        pe.wait_ge(hT_ready, n * PARTS + 1)
                    for u in range(len(UP)):
                        bank = (part % BANKS) * len(UP) + u
                        for k in range(KD):
                            last = nc.tensor.matmul(ps[0:size[f], bank, 0:HALF], up_w[s][u][:, k, f * tile:f * tile + size[f]],
                                                    xT[:, k, chunk * HALF:(chunk + 1) * HALF], start=k == 0, stop=k == KD - 1)
                    last.then_inc(up_ready, 1)
                for b in range(B):
                    if b == 0:
                        pe.wait_ge(hT_ready, n * PARTS + PARTS)
                    if b == 4:
                        pe.wait_ge(hT_ready, n * PARTS + PARTS + 1)
                    if b >= 4:
                        pe.wait_ge(y_added, n * B + b - 2)
                    else:
                        pe.wait_ge(y_added, n * B + 1)
                    for f in range(NF):
                        last = nc.tensor.matmul(ps[0:TQ, 4 + b % 4, 0:D], hT[0:size[f], f, b * TQ:(b + 1) * TQ],
                                                down_w[s][0:size[f], f, :], start=f == 0, stop=f == NF - 1)
                    last.then_inc(y_ready, 1)
                    if b == B - 1:
                        pe.wait_ge(y_ready, n * B + B + 1)
                        pe.sem_inc(weights_used, 1)
            pe.sem_inc(y_ready, 1)
            pairs(pe, one)

        @block.scalar
        def _(act):
            def one(n, s, i):
                act.wait_ge(y_ready, n * B + 1)
                for part in range(PARTS):
                    f, chunk = divmod(part, 2)
                    act.wait_ge(up_ready, n * PARTS + part + 1)
                    if swiglu:
                        if part >= 2:
                            act.wait_ge(gated_ready, n * PARTS + part)
                        else:
                            act.wait_ge(gated_ready, n * PARTS + 1)
                        nc.scalar.activation(sig[0:size[f], part % 2, :], ps[0:size[f], 2 * (part % BANKS), 0:HALF],
                                             ACT.Sigmoid).then_inc(sig_ready, 1)
                    else:
                        nc.scalar.activation(hT[:, f, chunk * HALF:(chunk + 1) * HALF], ps[:, part % BANKS, 0:HALF], ACT.Relu,
                                             bias=b1[s][:, f:f + 1]).then_inc(hT_ready, 1)
            if not swiglu:
                act.sem_inc(hT_ready, 1)
            pairs(act, one)

        @block.vector
        def _(dve):
            def one(n, s, i):
                if swiglu:
                    for part in range(PARTS):
                        f, chunk = divmod(part, 2)
                        m = size[f]
                        dve.wait_ge(sig_ready, n * PARTS + part + 1)
                        nc.vector.tensor_tensor(gated[0:m, part % 2, :], ps[0:m, 2 * (part % BANKS), 0:HALF], sig[0:m, part % 2, :],
                                                ALU.mult).then_inc(gated_ready, 1)
                        dve.wait_ge(gated_ready, n * PARTS + part + 2)
                        nc.vector.tensor_tensor(hT[0:m, f, chunk * HALF:(chunk + 1) * HALF], ps[0:m, 2 * (part % BANKS) + 1, 0:HALF],
                                                gated[0:m, part % 2, :], ALU.mult).then_inc(hT_ready, 1)
                for b in range(B):
                    dve.wait_ge(y_ready, n * B + b + 2)
                    dve.wait_ge(y_added, n * B + 1)
                    gate = gates[:, b, n:n + 1] if isinstance(n, int) else gates[:, b, bass.ds(n, 1)]
                    nc.vector.scalar_tensor_tensor(y[:, b, :], ps[0:TQ, 4 + b % 4, 0:D], gate, y[:, b, :], ALU.mult,
                                                   ALU.add).then_inc(y_added, 1)
            dve.sem_inc(y_added, 1)
            if swiglu:
                dve.sem_inc(hT_ready, 1)
                dve.sem_inc(gated_ready, 1)
            pairs(dve, one)


def add_all(nc, core, tag, dst, a, x=None, gate=None):
    with ExitStack() as c:
        done = core["phases"].sem(f"{tag}_done")
        block = core["phases"].block(c)

        @block.vector
        def _(dve):
            for b in range(B):
                if x is None:
                    nc.vector.tensor_tensor(dst[:, b, :], dst[:, b, :], a[:, b, :], ALU.add).then_inc(done, 1)
                else:
                    nc.vector.scalar_tensor_tensor(x[:, b, :], a[:, b, :], gate, x[:, b, :], ALU.mult, ALU.add).then_inc(done, 1)
            dve.wait_ge(done, B)


def lora(nc, core, tag, A, x, gate, xn, xnT, gates):
    ps, ident = core["ps"], core["ident"]
    E, R = 8, 4
    ER = E * R
    with ExitStack() as c:
        sb = lambda n, s: c.enter_context(nc.sbuf_tensor(f"{tag}_{n}", s, FP32))
        sem = lambda n: core["phases"].sem(f"{tag}_{n}")
        wl, left, right, bias = sb("wl", [P, KD, D]), sb("left", [P, KD, ER]), sb("right", [ER, D]), sb("bias", [TQ, D])
        low, lowT, part = sb("low", [TQ, B, ER]), sb("lowT", [ER, N]), sb("part", [TQ, 2, D])
        load_all(nc, core, tag, [(wl[:], A["wl"].rearrange("(k p) n -> p k n", p=P)), (left[:], A["left"].rearrange("(k p) n -> p k n", p=P)),
                           (right[:], A["right"]), (bias[:], A["bl"].partition_broadcast(TQ))])
        low_ready, low_scaled, lowT_ready, lowT_copied = sem("low_ready"), sem("low_scaled"), sem("lowT_ready"), sem("lowT_copied")
        out_ready, biased, x_done = sem("out_ready"), sem("biased"), sem("x_done")
        block = core["phases"].block(c)

        @block.tensor
        def _(pe):
            for b in range(B):
                for k in range(KD):
                    last = nc.tensor.matmul(ps[0:TQ, 0, b * ER:(b + 1) * ER], xnT[:, k, b * TQ:(b + 1) * TQ], left[:, k, :],
                                            start=k == 0, stop=k == KD - 1)
            last.then_inc(low_ready, 1)
            pe.wait_ge(low_scaled, 1)
            for b in range(B):
                last = nc.tensor.transpose(ps[0:ER, 1 + b // 4, (b % 4) * TQ:(b % 4 + 1) * TQ], low[:, b, :], ident[0:TQ, 0:TQ])
            last.then_inc(lowT_ready, 1)
            pe.wait_ge(lowT_copied, 2)
            for b in range(B):
                if b >= 4:
                    pe.wait_ge(biased, b - 3)
                for k in range(KD):
                    nc.tensor.matmul(ps[0:TQ, 4 + b % 4, 0:D], xnT[:, k, b * TQ:(b + 1) * TQ], wl[:, k, :], start=k == 0, stop=False)
                nc.tensor.matmul(ps[0:TQ, 4 + b % 4, 0:D], lowT[:, b * TQ:(b + 1) * TQ], right[:], start=False, stop=True)\
                    .then_inc(out_ready, 1)

        @block.vector
        def _(dve):
            v = nc.vector
            dve.wait_ge(low_ready, 1)
            v.tensor_tensor(low[:].rearrange("p b (e r) -> p b e r", r=R),
                            ps[0:TQ, 0, 0:B * ER].rearrange("p (b e r) -> p b e r", e=E, r=R),
                            bcast(gates[:, :, 0:E], 3, R), ALU.mult).then_inc(low_scaled, 1)
            dve.wait_ge(lowT_ready, 1)
            for i in range(2):
                v.tensor_copy(lowT[:, i * HALF:(i + 1) * HALF], ps[0:ER, 1 + i, 0:HALF]).then_inc(lowT_copied, 1)
            for b in range(B):
                dve.wait_ge(out_ready, b + 1)
                if b >= 2:
                    dve.wait_ge(x_done, b - 1)
                v.tensor_tensor(part[:, b % 2, :], ps[0:TQ, 4 + b % 4, 0:D], bias[:], ALU.add).then_inc(biased, 1)
                dve.wait_ge(biased, b + 1)
                v.scalar_tensor_tensor(x[:, b, :], part[:, b % 2, :], gate, x[:, b, :], ALU.mult, ALU.add).then_inc(x_done, 1)
            dve.wait_ge(x_done, B)



def start(nc, core, A):
    with ExitStack() as c:
        landed, tanh_done = core["phases"].sem("start_landed"), core["phases"].sem("start_tanh")
        raw = c.enter_context(nc.sbuf_tensor("start_gates", [P, 8], FP32))
        block = core["phases"].block(c)

        @block.sync
        def _(sp):
            sp.dma_start(core["x"][:], A["x"].rearrange("b t d -> t b d")).then_inc(landed, 16)
            sp.dma_start(core["ident"][:], A["ident"]).then_inc(landed, 16)
            sp.dma_start(raw[:, 0:4], A["g_xattn"].partition_broadcast(P)).then_inc(landed, 16)
            sp.dma_start(raw[:, 4:8], A["g_ffn"].partition_broadcast(P)).then_inc(landed, 16)

        @block.scalar
        def _(act):
            act.wait_ge(landed, 64)
            nc.scalar.activation(core["gate"][:], raw[:], ACT.Tanh).then_inc(tanh_done, 1)
            act.wait_ge(tanh_done, 1)


def network(nc, A, y_out, stages=8):
    with ExitStack() as c:
        sb = lambda n, s: c.enter_context(nc.sbuf_tensor(n, s, FP32))
        core = {"ps": c.enter_context(nc.psum_tensor("ps", [P, 8, BANK], FP32)), "ident": sb("ident", [P, P]),
                "x": sb("x_now", [TQ, B, D]), "gate": sb("gate", [P, 8]), "phases": Phases(nc)}
        x, xn, xnT, y = core["x"], sb("xn", [TQ, B, D]), sb("xnT", [P, KD, N]), sb("y_acc", [TQ, B, D])
        gates = sb("gates", [TQ, B, 9])
        gate = lambda i: core["gate"][0:TQ, i:i + 1]
        start(nc, core, A)
        sub = lambda prefix, names: {n: A[prefix + m] for n, m in names.items()}
        const = {n: A[n] for n in ("before", "ctx", "ctxT", "same_head", "rot", "cosq", "sinq", "cosk", "sink")}

        def rows(c2, name, *names):
            out = [c2.enter_context(nc.sbuf_tensor(f"row_{n}", [TQ, D], FP32)) for n in names]
            load_all(nc, core, f"rows_{name}", [(t[:], A[n].partition_broadcast(TQ)) for t, n in zip(out, names)])
            return out

        if stages >= 1:
            with ExitStack() as c2:
                cols = [c2.enter_context(nc.sbuf_tensor(f"col_{n}", [P, KD], FP32)) for n in ("ln_in_g", "ln_in_b")]
                load_all(nc, core, "ln_in", [(cols[0][:], A["L0_ln_in_g"]), (cols[1][:], A["L0_ln_in_b"])])
                layernorm_all(nc, core, "l0a", x, xn)
                layernorm_all(nc, core, "l0b", xn, xn, xT=xnT, xT_affine=cols)
            attention(nc, core, "a0", "cosine", {**const, **sub("L0_xattn_", dict(
                wq="Wq", wk="Wk", wv="Wv", wo="Wo", q_scale="q_scale", k_scale="k_scale", ctx_gain="ln_ctx_g",
                ctx_offset="ln_ctx_b", null_k="null_k", null_v="null_v")), "mask": A["mask2"]}, x, gate(0), xn, xnT, out=y)
            with ExitStack() as c2:
                g, o = rows(c2, "out", "L0_ln_out_g", "L0_ln_out_b")
                layernorm_all(nc, core, "l0c", y, y, affine=(g, o), update=(x, gate(0)))
        if stages >= 2:
            layernorm_all(nc, core, "l1a", x, xn, xT=xnT)
            attention(nc, core, "s0", "self", {**const, **sub("L0_ffn_", dict(
                wq="wq", wk="wk", wv="wv", bq="bq", bk="bk", bv="bv", wo="wo", bo="out_proj_b")), "mask": A["mask_quarter"]},
                x, gate(4), xn, xnT, out=y)
            with ExitStack() as c2:
                g, o = rows(c2, "ln1", "L0_ffn_ln1_g", "L0_ffn_ln1_b")
                layernorm_all(nc, core, "l1b", y, xn, affine=(g, o), xT=xnT)
            route(nc, core, "r0", "hier", {**const, **sub("L0_ffn_", dict(wr="wr", br="br", b2="b2"))}, xnT, gates, y)
            experts(nc, core, "e0", sub("L0_ffn_", dict(w1="w1", b1="b1", w2="w2")), xnT, gates, y, 8, 512, P, False)
            add_all(nc, core, "add0", y, xn)
            with ExitStack() as c2:
                g, o = rows(c2, "ln2", "L0_ffn_ln2_g", "L0_ffn_ln2_b")
                layernorm_all(nc, core, "l1c", y, y, affine=(g, o), update=(x, gate(4)))
        if stages >= 3:
            layernorm_all(nc, core, "l2a", x, xn, xT=xnT)
            attention(nc, core, "a1", "linear", {**const, **sub("L1_xattn_", dict(
                wq="Wq", wk="Wk", wv="Wv", bq="bq", bk="bk", bv="bv", wo="Wo", bo="bo")), "mask": A["mask_quarter"]},
                x, gate(1), xn, xnT)
        if stages >= 4:
            layernorm_all(nc, core, "l3a", x, xn, xT=xnT)
            route(nc, core, "r1", "top4", {**const, **sub("L1_ffn_", dict(wr="Wg", br="routing_bias"))}, xnT, gates, y)
            experts(nc, core, "e1", sub("L1_ffn_", dict(w1="W1", w2="W2", w3="W3")), xnT, gates, y, 9, 682, 114, True)
            add_all(nc, core, "add1", None, y, x, gate(5))
        if stages >= 5:
            layernorm_all(nc, core, "l4a", x, xn, xT=xnT)
            attention(nc, core, "a2", "raw", {**const, **sub("L2_xattn_", dict(wo="W_out", bo="b_out")),
                                              "mask": A["mask_one"]}, x, gate(2), xn, xnT)
        if stages >= 6:
            layernorm_all(nc, core, "l5a", x, xn, xT=xnT)
            route(nc, core, "r2", "top1", {**const, **sub("L2_ffn_", dict(wr="router_W", br="router_b", b2="b2"))}, xnT, gates, y)
            experts(nc, core, "e2", sub("L2_ffn_", dict(w1="W1", b1="b1", w2="W2")), xnT, gates, y, 8, 1024, P, False)
            add_all(nc, core, "add2", None, y, x, gate(6))
        if stages >= 7:
            layernorm_all(nc, core, "l6a", x, xn, xT=xnT)
            attention(nc, core, "a3", "rope", {**const, **sub("L3_xattn_", dict(
                wq="Wq", wk="Wk", wv="Wv", bq="bq", bk="bk", bv="bv", wo="Wo", bo="bo")), "mask": A["mask_eighth"],
                "allow": A["mask"]}, x, gate(3), xn, xnT)
        if stages >= 8:
            layernorm_all(nc, core, "l7a", x, xn, xT=xnT)
            route(nc, core, "r3", "top2", {**const, **sub("L3_ffn_", dict(wr="gate_w"))}, xnT, gates)
            lora(nc, core, "f3", sub("L3_ffn_", dict(wl="W_lin", bl="b_lin", left="left", right="right")), x, gate(7), xn, xnT, gates)
        with ExitStack() as c2:
            stored = core["phases"].sem("stored")
            block = core["phases"].block(c2)

            @block.sync
            def _(sp):
                sp.dma_start(y_out.rearrange("b t d -> t b d"), x[:]).then_inc(stored, 16)
                sp.wait_ge(stored, 16)


def layouts(i):
    c = np.ascontiguousarray
    a = {k: np.asarray(v) for k, v in i.items()}
    column = lambda t: c(t.reshape(-1, P).T)
    r = {"x": a["x"], "ctx": a["ctx_1024"], "g_xattn": a["g_xattn"], "g_ffn": a["g_ffn"], "mask": c(a["mask_BxS2_bf1"]).view(np.uint8)}
    r["ctxT"] = c(a["ctx_1024"].transpose(0, 2, 1).reshape(B, KD, P, CK).transpose(0, 2, 1, 3))
    w = a["L0_xattn_Wkv"]
    r["L0_xattn_Wq"], r["L0_xattn_Wo"] = a["L0_xattn_Wq"], a["L0_xattn_Wo"]
    r["L0_xattn_Wk"], r["L0_xattn_Wv"] = c(w[:, :1024]), c(w[:, 1024:])
    for n in ("q_scale", "k_scale"):
        t = a[f"L0_xattn_{n}"]
        r[f"L0_xattn_{n}"] = c(np.concatenate([t, t])[:, None])
    nk, nv = a["L0_xattn_null_kv"]
    r["L0_xattn_null_k"], r["L0_xattn_null_v"] = c(np.concatenate([nk, nk])[:, None]), c(nv[None])
    for n in ("ln_in_g", "ln_in_b"):
        r[f"L0_{n}"] = column(a[f"L0_xattn_{n}"])
    for n in ("ln_ctx_g", "ln_ctx_b"):
        r[f"L0_xattn_{n}"] = column(a[f"L0_xattn_{n}"])
    for n in ("ln_out_g", "ln_out_b"):
        r[f"L0_{n}"] = a[f"L0_xattn_{n}"]
    w, t = a["L0_ffn_in_proj_w"].T, a["L0_ffn_in_proj_b"]
    for j, n in enumerate("qkv"):
        r[f"L0_ffn_w{n}"] = c(w[:, j * D:(j + 1) * D])
        r[f"L0_ffn_b{n}"] = c(t[j * D:(j + 1) * D]) if n == "v" else column(t[j * D:(j + 1) * D])
    r["L0_ffn_wo"] = c(a["L0_ffn_out_proj_w"].T)
    for n in ("out_proj_b", "ln1_g", "ln1_b", "ln2_g", "ln2_b", "b2", "w1", "w2"):
        r[f"L0_ffn_{n}"] = a[f"L0_ffn_{n}"]
    r["L0_ffn_wr"] = c(np.concatenate([a["L0_ffn_w_group"], a["L0_ffn_w_expert"].transpose(1, 0, 2).reshape(D, 8)], 1))
    r["L0_ffn_br"] = c(np.concatenate([a["L0_ffn_b_group"], a["L0_ffn_b_expert"].reshape(8)]))
    r["L0_ffn_b1"] = c(a["L0_ffn_b1"].reshape(8, -1, P).transpose(0, 2, 1))
    for n in ("Wq", "Wk", "Wv", "Wo", "bv", "bo"):
        r[f"L1_xattn_{n}"] = a[f"L1_xattn_{n}"]
    for n in ("bq", "bk"):
        r[f"L1_xattn_{n}"] = column(a[f"L1_xattn_{n}"])
    r["L1_ffn_Wg"], r["L1_ffn_routing_bias"] = c(a["L1_ffn_Wg"].T), a["L1_ffn_routing_bias"]
    for n in ("1", "2", "3"):
        r[f"L1_ffn_W{n}"] = c(np.concatenate([a[f"L1_ffn_W{n}"], a[f"L1_ffn_Ws{n}"][None]]).transpose(0, 2, 1))
    r["L2_xattn_W_out"], r["L2_xattn_b_out"] = c(a["L2_xattn_W_out"].T), a["L2_xattn_b_out"]
    for n in ("router_W", "router_b", "W1", "W2", "b2"):
        r[f"L2_ffn_{n}"] = a[f"L2_ffn_{n}"]
    r["L2_ffn_b1"] = c(a["L2_ffn_b1"].reshape(8, -1, P).transpose(0, 2, 1))
    w, t = a["L3_xattn_Wkv"], a["L3_xattn_bkv"]
    r["L3_xattn_Wq"], r["L3_xattn_Wk"], r["L3_xattn_Wv"] = a["L3_xattn_Wq"], c(w[:, :D]), c(w[:, D:])
    r["L3_xattn_bq"], r["L3_xattn_bk"], r["L3_xattn_bv"] = column(a["L3_xattn_bq"]), column(t[:D]), c(t[D:])
    r["L3_xattn_Wo"], r["L3_xattn_bo"] = a["L3_xattn_Wo"], a["L3_xattn_bo"]
    r["L3_ffn_W_lin"], r["L3_ffn_b_lin"], r["L3_ffn_gate_w"] = c(a["L3_ffn_W_lin"].T), a["L3_ffn_b_lin"], c(a["L3_ffn_gate_w"].T)
    r["L3_ffn_left"], r["L3_ffn_right"] = c(a["L3_ffn_left"].transpose(1, 0, 2).reshape(D, 32)), c(a["L3_ffn_right"].reshape(32, D))
    f32 = np.float32
    r["ident"] = np.eye(P, dtype=f32)
    rows = np.arange(P)
    r["same_head"] = (rows[:, None] // 64 == rows[None] // 64).astype(f32)
    r["before"] = (np.arange(8)[None] < np.arange(8)[:, None]).astype(f32)
    own = lambda hd: (rows[:, None] // hd == np.arange(P // hd)[None]).astype(f32)
    r["mask2"], r["mask_quarter"], r["mask_one"], r["mask_eighth"] = 8 * own(64), own(16) / 4, own(16), own(16) / 8
    r["mask2"], r["mask_quarter"], r["mask_eighth"] = [r[n].astype(f32) for n in ("mask2", "mask_quarter", "mask_eighth")]
    rot = np.zeros((P, P), f32)
    even = rows[::2]
    rot[even + 1, even], rot[even, even + 1] = -1.0, 1.0
    r["rot"] = rot
    inv_freq = (1.0 / 10000.0 ** (np.arange(0, 16, 2, dtype=f32) / f32(16))).astype(f32)
    for n, length in (("q", TQ), ("k", CK)):
        pos = f32(10.0) * (np.arange(length, dtype=f32) / f32(length))
        angle = pos[None] * inv_freq[(rows % 16) // 2][:, None]
        r["cos" + n], r["sin" + n] = np.cos(angle).astype(f32), np.sin(angle).astype(f32)
    return r


def kernel(**inputs):
    import concourse.bacc as bacc
    from concourse.bass_utils import run_bass_kernel_spmd

    arrays = {f"in_{n}": t for n, t in layouts(inputs).items()}
    nc = bacc.Bacc("TRN2", target_bir_lowering=False, num_devices=1)
    A = {n[3:]: nc.dram_tensor(n, t.shape, mybir.dt.from_np(t.dtype), kind="ExternalInput").ap() for n, t in arrays.items()}
    out = nc.dram_tensor("out", (B, TQ, D), FP32, kind="ExternalOutput").ap()
    network(nc, A, out)
    r = run_bass_kernel_spmd(nc, [arrays], core_ids=[0])
    return r.results[0]["out"]
```

```python
from contextlib import ExitStack

import numpy as np

import concourse.bass as bass
from concourse import mybir

FP32 = mybir.dt.float32
FP32R = mybir.dt.float32r
BF16 = mybir.dt.bfloat16
U8 = mybir.dt.uint8
ALU = mybir.AluOpType
ACT = mybir.ActivationFunctionType
AX = mybir.AxisListType

B, TQ, D = 8, 112, 256
N = B * TQ
P = 128
KD = D // P
CK, KT = 375, 125
H = 16
GROUPS = H // 2
HALF = N // 2
BANK = 512
LN_EPS = 1e-5


def bcast(ap, axis, n):
    ap = ap.unsqueeze(axis)
    shape = list(ap.shape)
    shape[axis] = n
    return ap.broadcast_to(shape)


class Chain:

    def __init__(self, engine, sem, start=0):
        self.engine, self.sem, self.start, self.k = engine, sem, start, 0

    def step(self, instruction):
        self.k += 1
        instruction.then_inc(self.sem, 1)
        self.engine.wait_ge(self.sem, self.start + self.k)


class Phases:

    def __init__(self, nc):
        self.nc, self.used, self.clearing = nc, [], []

    def sem(self, name):
        held = self.nc.semaphore(name)
        s = held.__enter__()
        self.used.append((held, s))
        return s

    def block(self, c):
        nc = self.nc
        for held, _ in self.clearing:
            held.__exit__(None, None, None)
        self.clearing, old = [], self.before
        block = c.enter_context(nc.Block())
        if old:
            @block.gpsimd
            def _(pool):
                for _, s in old:
                    pool.sem_clear(s)
        self.clearing, self.before, self.used = old, self.used, []
        return block

    before = ()


    asked = ()

    def ask(self, tag, loads, zero=()):
        self.asked = list(self.asked) + [{"tag": tag, "loads": loads, "zero": zero, "held": None}]

    def run_ahead(self, block, settle):
        nc = self.nc
        for g in reversed(self.asked):
            if g["held"] is None:
                g["held"] = [nc.semaphore(f"{g['tag']}_{n}") for n in ("landed", "cleared")]
                g["landed"], g["cleared"] = [h.__enter__() for h in g["held"]]
                if g["zero"]:
                    @block.gpsimd
                    def _(pool):
                        for t in g["zero"]:
                            nc.gpsimd.memset(t, 0.0).then_inc(g["cleared"], 1)

                @block.sync
                def _(sp):
                    if g["zero"]:
                        sp.wait_ge(g["cleared"], len(g["zero"]))
                    for to, src in g["loads"]:
                        sp.dma_start(to, src).then_inc(g["landed"], 16)
        if settle:
            g = self.asked.pop()
            self.used += [(g["held"][0], g["landed"]), (g["held"][1], g["cleared"])]

            @block.sync
            def _(sp):
                sp.wait_ge(g["landed"], 16 * len(g["loads"]))



def layernorm_all(nc, core, tag, src, dst, affine=None, update=None, xT=None, xT_affine=None,
                  add=None, settle=False):
    ps, ident = core["ps"], core["ident"]
    with ExitStack() as c:
        sb = lambda n, s: c.enter_context(nc.sbuf_tensor(f"{tag}_{n}", s, FP32))
        sem = lambda n: core["phases"].sem(f"{tag}_{n}")
        stats, mv = sb("stats", [TQ, B, 6]), sb("mv", [TQ, B, 2])
        var_eps, std, rstd = sb("var_eps", [TQ, B]), sb("std", [TQ, B]), sb("rstd", [TQ, B])
        stats_ready, mv_ready, var_ready = sem("stats_ready"), sem("mv_ready"), sem("var_ready")
        std_ready, rstd_ready, rows_normal = sem("std_ready"), sem("rstd_ready"), sem("rows_normal")
        scaled, rows_ready, updated = sem("scaled"), sem("rows_ready"), sem("updated")
        transposed, copied, added, affine_landed = sem("transposed"), sem("copied"), sem("added"), sem("affine_landed")
        if affine is not None:
            gain, offset = sb("gain", [TQ, D]), sb("offset", [TQ, D])
        block = core["phases"].block(c)

        if affine is not None:
            @block.sync
            def _(sp):
                sp.dma_start(gain[:], affine[0].partition_broadcast(TQ)).then_inc(affine_landed, 16)
                sp.dma_start(offset[:], affine[1].partition_broadcast(TQ)).then_inc(affine_landed, 16)

        @block.vector
        def _(dve):
            if add is not None:
                a, add_gate = add
                for b in range(B):
                    if add_gate is None:
                        nc.vector.tensor_tensor(src[:, b, :], src[:, b, :], a[:, b, :], ALU.add).then_inc(added, 1)
                    else:
                        nc.vector.scalar_tensor_tensor(src[:, b, :], a[:, b, :], add_gate, src[:, b, :], ALU.mult, ALU.add).then_inc(added, 1)
            for b in range(B):
                if add is not None:
                    dve.wait_ge(added, b + 1)
                nc.vector.bn_stats(stats[:, b, :], src[:, b, :]).then_inc(stats_ready, 1)
            for b in range(B):
                dve.wait_ge(stats_ready, b + 1)
                nc.vector.bn_aggr(mv[:, b, :], stats[:, b, :]).then_inc(mv_ready, 1)
            dve.wait_ge(mv_ready, B)
            nc.vector.tensor_scalar(var_eps[:], mv[:, :, 1], LN_EPS, None, ALU.add).then_inc(var_ready, 1)
            dve.wait_ge(std_ready, 1)
            nc.vector.reciprocal(rstd[:], std[:]).then_inc(rstd_ready, 1)
            dve.wait_ge(rstd_ready, 1)
            first = rows_ready if affine is None else rows_normal
            for b in range(B):
                nc.vector.tensor_scalar(dst[:, b, :], src[:, b, :], mv[:, b, 0:1], rstd[:, b:b + 1],
                                        ALU.subtract, ALU.mult).then_inc(first, 1)
            if affine is not None:
                dve.wait_ge(affine_landed, 32)
                for b in range(B):
                    dve.wait_ge(rows_normal, b + 1)
                    nc.vector.tensor_tensor(dst[:, b, :], dst[:, b, :], gain[:], ALU.mult).then_inc(scaled, 1)
                for b in range(B):
                    dve.wait_ge(scaled, b + 1)
                    nc.vector.tensor_tensor(dst[:, b, :], dst[:, b, :], offset[:], ALU.add).then_inc(rows_ready, 1)
            if update is not None:
                x, gate = update
                for b in range(B):
                    dve.wait_ge(rows_ready, b + 1)
                    nc.vector.scalar_tensor_tensor(x[:, b, :], dst[:, b, :], gate, x[:, b, :],
                                                   ALU.mult, ALU.add).then_inc(updated, 1)

        @block.scalar
        def _(act):
            act.wait_ge(var_ready, 1)
            nc.scalar.activation(std[:], var_eps[:], ACT.Sqrt).then_inc(std_ready, 1)
            if xT is not None:
                for i in range(2 * KD):
                    chunk, k = divmod(i, KD)
                    act.wait_ge(transposed, i + 1)
                    to = xT[:, k, chunk * HALF:(chunk + 1) * HALF]
                    if xT_affine is None:
                        nc.scalar.activation(to, ps[:, i, 0:HALF], ACT.Copy).then_inc(copied, 1)
                    else:
                        nc.scalar.activation(to, ps[:, i, 0:HALF], ACT.Identity, scale=xT_affine[0][:, k:k + 1],
                                             bias=xT_affine[1][:, k:k + 1]).then_inc(copied, 1)

        if xT is not None:
            @block.tensor
            def _(pe):
                for i in range(2 * KD):
                    chunk, k = divmod(i, KD)
                    pe.wait_ge(rows_ready, 4 * (chunk + 1))
                    for j in range(4):
                        last = nc.tensor.transpose(ps[:, i, j * TQ:(j + 1) * TQ],
                                                   dst[:, 4 * chunk + j, k * P:(k + 1) * P], ident[0:TQ, 0:TQ])
                    last.then_inc(transposed, 1)

        core["phases"].run_ahead(block, settle)



def load_all(nc, core, tag, loads, zero=()):
    with ExitStack() as c:
        landed = core["phases"].sem(f"{tag}_landed")
        cleared = core["phases"].sem(f"{tag}_cleared")
        block = core["phases"].block(c)

        @block.vector
        def _(dve):
            for t in zero:
                nc.vector.memset(t, 0.0).then_inc(cleared, 1)

        @block.sync
        def _(sp):
            if zero:
                sp.wait_ge(cleared, len(zero))
            for to, src in loads:
                sp.dma_start(to, src).then_inc(landed, 16)
            sp.wait_ge(landed, 16 * len(loads))


def attention(nc, core, tag, kind, A, x, gate, xn, xnT, before, out=None):
    ps, ident = core["ps"], core["ident"]
    cosine, self_, rope, raw, linear = [kind == k for k in ("cosine", "self", "rope", "raw", "linear")]
    hd = 64 if cosine else 16
    width = 64 if cosine else 32
    per_set = P // width
    SETS = H // per_set
    FILLS = SETS // 4
    per_half = P // hd
    inner = H * hd
    KI = inner // P
    nk = CK + 1 if cosine else TQ if self_ else CK
    tiles = [(0, TQ)] if self_ else [(t * KT, KT + (cosine and t == 2)) for t in range(3)]
    NT = len(tiles)
    S_LAG, PV_LAG = 4, 6
    OUT_BANK, PIECE_BANK = 6, 7

    if cosine:
        proj = (["c0", "c1", "q0", "q1"] + [f"k{i}" for i in range(6)] + [f"v{i}" for i in range(6)]
                + ["a0", "a1"] + [f"t{i}" for i in range(8)])
        room = [s for s in range(1, 16) for _ in range(2) if (s, _) not in ((4, 0), (6, 0), (7, 0))]
        where = {4: ["R0"], 6: ["R1"], 7: ["O"]}
    else:
        proj = {"self": ["q0", "k0", "v0"], "linear": ["q0", "k0", "k1", "v0", "v1", "v2"],
                "rope": ["q0", "r0", "k0", "s0", "k1", "s1", "v0", "v1", "v2"], "raw": []}[kind]
        room = {"self": [0, 1, 8], "linear": [0, 1, 2, 8, 9, 10], "rope": [0, 1, 2, 3, 4, 5, 8, 9, 10], "raw": []}[kind]
        where = {6: ["R0"], 7: ["O"]}
    for name, s in zip(proj, room):
        where.setdefault(s, []).append(name)
    tail = ["R0", "R1", "O"] if cosine else ["R0", "O"]
    order = [name for s in range(H) for name in where.get(s, [])]
    Q, M = len(proj), len(proj) + len(tail)
    assert len(order) == M

    def piece_count(name, n):
        if isinstance(n, int) and n < 1:
            return Q * (n + 1) + proj.index(name) + 2
        if isinstance(n, int) and n >= B - 1:
            return 2 * Q + M * (B - 2) + len(tail) * (n - B + 1) + tail.index(name) + 2
        return M * (n - 1) + 2 * Q + order.index(name) + 2

    with ExitStack() as c:
        def sb(name, shape):
            return c.enter_context(nc.sbuf_tensor(f"{tag}_{name}", shape, FP32))

        def sem(name):
            return core["phases"].sem(f"{tag}_{name}")

        loads, zero = [], []
        wo = sb("wo", [P, SETS, D])
        if cosine:
            loads.append((wo[:], A["wo"].rearrange("(s p) n -> p s n", p=P)))
        else:
            zero.append(wo[:])
            rows = A["wo"].rearrange("(s j r) n -> j r s n", j=per_set, r=hd)
            for j in range(per_set):
                loads.append((wo[j * width:j * width + hd, :, :], rows[j]))
        mask = sb("mask", [P, per_half])
        loads.append((mask[:], A["mask"]))
        if not raw:
            wq, wk, wv = sb("wq", [P, KD, inner]), sb("wk", [P, KD, inner]), sb("wv", [P, KD, inner])
            for w, name in ((wq, "wq"), (wk, "wk"), (wv, "wv")):
                loads.append((w[:], A[name].rearrange("(k p) n -> p k n", p=P)))
        if not raw and not cosine:
            bq, bk, bv = sb("bq", [P, KD]), sb("bk", [P, KD]), sb("bv", [KT, D])
            loads += [(bq[:], A["bq"]), (bk[:], A["bk"]), (bv[:], A["bv"].partition_broadcast(KT))]
        if not cosine:
            bo = sb("bo", [TQ, D])
            loads.append((bo[:], A["bo"].partition_broadcast(TQ)))
        if rope:
            rot, cosq, sinq = sb("rot", [P, P]), sb("cosq", [P, TQ]), sb("sinq", [P, TQ])
            cosk, sink = sb("cosk", [P, CK]), sb("sink", [P, CK])
            loads += [(rot[:], A["rot"]), (cosq[:], A["cosq"]), (sinq[:], A["sinq"]), (cosk[:], A["cosk"]), (sink[:], A["sink"])]
            allow8 = c.enter_context(nc.sbuf_tensor(f"{tag}_allow8", [1, B, CK], U8))
            hidden = c.enter_context(nc.sbuf_tensor(f"{tag}_hidden", [P, B, CK], BF16))
            one_row = c.enter_context(nc.sbuf_tensor(f"{tag}_one_row", [P, TQ], BF16))
            loads.append((allow8[:], A["allow"].rearrange("(o b) k -> o b k", o=1)))
            zero += [hidden[:], one_row[:]]
            q_raw, k_raw = sb("q_raw", [P, KD, TQ]), sb("k_raw", [P, KD, CK])
            q_cos, q_rot = sb("q_cos", [P, KD, TQ]), sb("q_rot", [P, KD, TQ])
            k_sin = sb("k_sin", [P, KD, CK])
        if cosine:
            qk_gain = sb("qk_gain", [P, 2])
            loads += [(qk_gain[:, 0:1], A["q_scale"]), (qk_gain[:, 1:2], A["k_scale"])]
            ctx_gain, ctx_offset = sb("ctx_gain", [P, KD]), sb("ctx_offset", [P, KD])
            loads += [(ctx_gain[:], A["ctx_gain"]), (ctx_offset[:], A["ctx_offset"])]
            head_mask = sb("head_mask", [P, per_half])
            cmv, crs = sb("cmv", [KT, 3 * B, 2]), sb("crs", [KT, 3 * B])
            ss, norm, inv_norm = sb("ss", [KT, 4 * H]), sb("norm", [KT, 4 * H]), sb("inv_norm", [KT, 4 * H])
            zero.append(ss[:])
        kT = [sb(f"kT{p}", [P, KI, nk]) for p in range(2)]
        v = [sb(f"v{p}", [KT + 1 if cosine else KT, NT, inner]) for p in range(2)]
        if cosine:
            loads += [(t[KT:KT + 1, 2, :].rearrange("p (h d) -> p h d", h=H), bcast(A["null_v"], 1, H)) for t in v]
        core["phases"].ask(tag, loads, zero)
        before()
        if rope:
            mask_row(nc, core, tag, allow8, hidden, one_row, sb)
        if cosine:
            context_stats(nc, core, tag, A, cmv, crs)
            null_row(nc, core, tag, A, kT, head_mask, mask, qk_gain, hd, sb)
            cx, cn = sb("cx", [KT, 3, D]), sb("cn", [KT, 3, D])
            k_tok, sq, q_tok = sb("k_tok", [KT, 3, inner]), sb("sq", [KT, 4, BANK]), sb("q_tok", [TQ, inner])
        xs = sb("xs", [P, KD, TQ]) if (self_ or cosine) else None
        cT = kT if raw else None if self_ else sb("cT", [P, KD, CK])
        qm = [sb(f"qm{p}", [P, H, TQ]) for p in range(2)]
        probs = sb("probs", [TQ, 4, nk])
        probsT = sb("probsT", [KT + 1, 8, NT * TQ])
        nmax, sums, inv = sb("nmax", [TQ, 2, H]), sb("sums", [TQ, 2, H]), sb("inv", [TQ, H])
        inv_wide, heads_raw = sb("inv_wide", [TQ, H, width]), sb("heads_raw", [P, FILLS, 4 * TQ])
        headsT, part = sb("headsT", [P, FILLS, 4 * TQ]), sb("part", [TQ, D])

        scores_ready, max_ready, probs_ready = sem("scores_ready"), sem("max_ready"), sem("probs_ready")
        pT_ready, pT_copied, heads_ready, heads_copied = sem("pT_ready"), sem("pT_copied"), sem("heads_ready"), sem("heads_copied")
        piece_ready, piece_read = sem("piece_ready"), sem("piece_read")
        inv_ready, inv_wide_ready = sem("inv_ready"), sem("inv_wide_ready")
        ctx_ready = [sem("ctx_ready_0"), sem("ctx_ready_1")]
        values_ready = [sem("values_ready_0"), sem("values_ready_1")]
        xs_ready, qm_ready, kT_ready = sem("xs_ready"), sem("qm_ready"), sem("kT_ready")
        q_cos_ready, k_cos_ready, rot_steps = sem("q_cos_ready"), sem("k_cos_ready"), sem("rot_steps")
        cn_ready, sq_ready, summed, floored = sem("cn_ready"), sem("sq_ready"), sem("summed"), sem("floored")
        norm_ready, inv_norm_ready, scaled = sem("norm_ready"), sem("inv_norm_ready"), sem("scaled")
        block = core["phases"].block(c)

        def batches(engine, before, batch, after):
            before()
            batch(0, 0, True, False)
            with engine.Fori(0, B // 2 - 1, 1) as i:
                batch(2 * i + 1, 1, False, False)
                batch(2 * i + 2, 0, False, False)
            batch(B - 1, 1, False, True)
            after()

        def pieces(slot, n, first, last):
            for name in where.get(slot, []):
                if name in tail and not first:
                    yield name, n - 1, piece_count(name, n)
                if name in proj and not last:
                    yield name, n + 1, piece_count(name, n)

        def square_part(kind, i):
            if kind == "q":
                return i, TQ, q_tok[:, i * BANK:(i + 1) * BANK]
            t, half = divmod(i, 2)
            return 2 + i, KT, k_tok[:, t, half * BANK:(half + 1) * BANK]

        @block.sync
        def _(sp):
            for n in range(B):
                s = n % 2 if raw else 0
                if raw:
                    if n >= 2:
                        sp.wait_ge(heads_ready, SETS * (n - 1))
                    sp.dma_start(kT[s][:], A["ctxT"][n]).then_inc(ctx_ready[s], 16)
                    sp.dma_start(v[s][:], A["ctx"][n].rearrange("(t p) d -> p t d", p=KT)).then_inc(values_ready[s], 16)
                elif cosine:
                    if n:
                        sp.wait_ge(cn_ready, n)
                    sp.dma_start(cx[:], A["ctx"][n].rearrange("(t p) d -> p t d", p=KT)).then_inc(ctx_ready[0], 16)
                elif not self_:
                    if n:
                        sp.wait_ge(piece_ready, piece_count("v2", n - 2))
                    sp.dma_start(cT[:], A["ctxT"][n]).then_inc(ctx_ready[0], 16)

        if self_ or cosine or rope:
            @block.gpsimd
            def _(pool):
                for n in range(B):
                    if not rope:
                        if n:
                            pool.wait_ge(piece_ready, piece_count("v0" if self_ else "q1", n - 2))
                        pool.tensor_copy(xs[:], xnT[:, :, n * TQ:(n + 1) * TQ]).then_inc(xs_ready, 1)
                    else:
                        pool.wait_ge(piece_read, piece_count("q0", n - 1))
                        if n:
                            pool.wait_ge(rot_steps, n)
                        pool.tensor_tensor(q_cos[:], q_raw[:], bcast(cosq[:], 1, KD), ALU.mult).then_inc(q_cos_ready, 1)
                        if n >= 2:
                            pool.wait_ge(scores_ready, H * (n - 1))
                        for k in range(KD):
                            pool.wait_ge(piece_read, piece_count(f"k{k}", n - 1))
                            pool.tensor_tensor(kT[n % 2][:, k, :], k_raw[:, k, :], cosk[:], ALU.mult).then_inc(k_cos_ready, 1)

        @block.tensor
        def _(pe):
            bank = ps[:, PIECE_BANK, :]

            def piece(name, m, count, p):
                pe.wait_ge(piece_read, count - 1)
                kind, i = name[0], int(name[1:] or 0)
                if kind == "R":
                    if i == 0:
                        pe.wait_ge(inv_wide_ready, m + 1)
                    for j in range(4):
                        s = 4 * i + j
                        last = nc.tensor.transpose(bank[:, j * TQ:(j + 1) * TQ],
                                                   inv_wide[:, s * per_set:(s + 1) * per_set, :].rearrange("p h w -> p (h w)"),
                                                   ident[0:TQ, 0:TQ])
                elif kind == "O":
                    for s in range(SETS):
                        last = nc.tensor.matmul(bank[0:TQ, 0:D], headsT[:, s // 4, (s % 4) * TQ:(s % 4 + 1) * TQ], wo[:, s, :],
                                                start=s == 0, stop=s == SETS - 1)
                elif cosine and kind == "c":
                    pe.wait_ge(cn_ready, m + 1)
                    for t in range(3):
                        last = nc.tensor.transpose(bank[:, t * KT:(t + 1) * KT], cn[:, t, i * P:(i + 1) * P], ident[0:KT, 0:KT])
                elif cosine and kind in "qkv":
                    if kind == "q":
                        pe.wait_ge(xs_ready, m + 1)
                    t, half = (0, i) if kind == "q" else divmod(i, 2)
                    w = {"q": wq, "k": wk, "v": wv}[kind]
                    rows = TQ if kind == "q" else KT
                    for k in range(KD):
                        lhsT = xs[:, k, :] if kind == "q" else cT[:, k, t * KT:(t + 1) * KT]
                        last = nc.tensor.matmul(bank[0:rows, :], lhsT, w[:, k, half * BANK:(half + 1) * BANK],
                                                start=k == 0, stop=k == KD - 1)
                elif kind == "a":
                    pe.wait_ge(scaled, 4 * m + 1)
                    for j in range(4):
                        at = (4 * i + j) * P
                        last = nc.tensor.transpose(bank[:, j * TQ:(j + 1) * TQ], q_tok[:, at:at + P], ident[0:TQ, 0:TQ])
                elif kind == "t":
                    pe.wait_ge(scaled, 4 * m + 4)
                    for t in range(3):
                        last = nc.tensor.transpose(bank[:, t * KT:(t + 1) * KT], k_tok[:, t, i * P:(i + 1) * P], ident[0:KT, 0:KT])
                elif kind == "q":
                    if self_:
                        pe.wait_ge(xs_ready, m + 1)
                    for half in range(KD):
                        for k in range(KD):
                            last = nc.tensor.matmul(bank[:, half * TQ:(half + 1) * TQ], wq[:, k, half * P:(half + 1) * P],
                                                    xs[:, k, :] if self_ else xnT[:, k, bass.ds(m * TQ, TQ)],
                                                    start=k == 0, stop=k == KD - 1)
                elif kind == "k" and self_:
                    for half in range(KD):
                        for k in range(KD):
                            last = nc.tensor.matmul(bank[:, half * TQ:(half + 1) * TQ], wk[:, k, half * P:(half + 1) * P],
                                                    xs[:, k, :], start=k == 0, stop=k == KD - 1)
                elif kind == "k":
                    if i == 0:
                        pe.wait_ge(ctx_ready[0], 16 * m + 16)
                    for k in range(KD):
                        last = nc.tensor.matmul(bank[:, 0:nk], wk[:, k, i * P:(i + 1) * P], cT[:, k, :], start=k == 0, stop=k == KD - 1)
                elif kind == "v":
                    at, kt = tiles[i]
                    for k in range(KD):
                        last = nc.tensor.matmul(bank[0:kt, 0:D], (xs if self_ else cT)[:, k, at:at + kt], wv[:, k, :],
                                                start=k == 0, stop=k == KD - 1)
                elif kind == "r":
                    for half in range(KD):
                        last = nc.tensor.matmul(bank[:, half * TQ:(half + 1) * TQ], rot[:], q_raw[:, half, :], start=True, stop=True)
                elif kind == "s":
                    last = nc.tensor.matmul(bank[:, 0:nk], rot[:], k_raw[:, i, :], start=True, stop=True)
                last.then_inc(piece_ready, 1)

            def transposes(a, k):
                pe.wait_ge(probs_ready, a + 1)
                if not (isinstance(a, int) and a < 2):
                    pe.wait_ge(pT_copied, a - 1)
                for t, (at, kt) in enumerate(tiles):
                    last = nc.tensor.transpose(ps[0:kt, 4 + k % 2, t * TQ:(t + 1) * TQ], probs[:, k % 4, at:at + kt],
                                               ident[0:TQ, 0:TQ])
                last.then_inc(pT_ready, 1)

            def outputs(m, k, p):
                if (k + 1) % per_set:
                    return
                s = k // per_set
                pe.wait_ge(pT_copied, H * m + k + 1)
                if s == 0 and raw:
                    pe.wait_ge(values_ready[p], 8 * m + (8 if p else 16))
                if s % 4 == 0 and not (isinstance(m, int) and m == 0 and s == 0):
                    pe.wait_ge(heads_copied, FILLS * m + s // 4)
                for t, (at, kt) in enumerate(tiles):
                    for j in range(per_set):
                        h = s * per_set + j
                        last = nc.tensor.matmul(ps[j * width:j * width + hd, OUT_BANK, (s % 4) * TQ:(s % 4 + 1) * TQ],
                                                v[p][0:kt, t, h * hd:(h + 1) * hd], probsT[0:kt, h % 8, t * TQ:(t + 1) * TQ],
                                                start=t == 0, stop=t == NT - 1)
                last.then_inc(heads_ready, 1)

            def scores(n, k, p):
                a = H * n + k
                if k == 0:
                    if Q:
                        pe.wait_ge(piece_read, Q + 1 if isinstance(n, int) and n == 0 else M * (n - 1) + 2 * Q + 1)
                    if raw:
                        pe.wait_ge(ctx_ready[p], 8 * n + (8 if p else 16))
                    if raw or rope:
                        pe.wait_ge(qm_ready, 2 * n + 2)
                    if rope:
                        pe.wait_ge(kT_ready, KD * n + KD)
                if not (isinstance(a, int) and a < 4):
                    pe.wait_ge(probs_ready, a - 3)
                last = nc.tensor.matmul(ps[0:TQ, k % 4, 0:nk], qm[p][:, k, :], kT[p][:, k // per_half, :], start=True, stop=not rope)
                if rope:
                    last = nc.tensor.matmul(ps[0:TQ, k % 4, 0:nk], one_row[:], hidden[:, n, :], start=False, stop=True)
                last.then_inc(scores_ready, 1)

            def first_projections():
                pe.sem_inc(piece_ready, 1)
                pe.sem_inc(piece_read, 1)
                for name in proj:
                    piece(name, 0, piece_count(name, -1), 0)

            def slot(n, k, p, first, last):
                if k < H:
                    scores(n, k, p)
                todo = list(pieces(k, n, first, last)) if k < H else [(name, n, piece_count(name, B)) for name in tail if name in where.get(k - H, [])]
                for name, m, count in todo[:1]:
                    piece(name, m, count, p)
                if k >= S_LAG or not first:
                    transposes_at = k - S_LAG
                    if transposes_at < H:
                        transposes(H * n + transposes_at, transposes_at % H)
                for name, m, count in todo[1:]:
                    piece(name, m, count, p)
                if k >= PV_LAG:
                    if k - PV_LAG < H:
                        outputs(n, k - PV_LAG, p)
                elif not first:
                    outputs(n - 1, k - PV_LAG + H, 1 - p)

            def batch(n, p, first, last):
                for k in range(H):
                    slot(n, k, p, first, last)

            def after():
                for k in range(H, H + 8):
                    slot(B - 1, k, 1, False, True)

            batches(pe, first_projections, batch, after)

        @block.scalar
        def _(act):
            bank = ps[:, PIECE_BANK, :]

            def piece(name, m, count, p):
                kind, i = name[0], int(name[1:] or 0)
                read = lambda ins: ins.then_inc(piece_read, 1)
                if cosine and kind in "qk":
                    j, rows, tokens = square_part(kind, i)
                    act.wait_ge(piece_read, count)
                    if j >= 4 or not (isinstance(m, int) and m == 0):
                        act.wait_ge(summed, 8 * m + j - 3)
                    nc.scalar.activation(sq[0:rows, j % 4, :], tokens, ACT.Square).then_inc(sq_ready, 1)
                    return
                if kind in "RO" or kind in "ra" or (not cosine and (kind == "v" or kind == "s" or (kind == "q" and not rope))):
                    return
                if cosine and kind == "a":
                    return
                act.wait_ge(piece_ready, count)
                if kind == "c":
                    read(nc.scalar.activation(cT[:, i, :], bank[:, 0:CK], ACT.Identity, scale=ctx_gain[:, i:i + 1],
                                              bias=ctx_offset[:, i:i + 1]))
                elif cosine and kind == "v":
                    t, half = divmod(i, 2)
                    read(nc.scalar.activation(v[p][0:KT, t, half * BANK:(half + 1) * BANK], bank[0:KT, :], ACT.Copy))
                elif kind == "t":
                    read(nc.scalar.activation(kT[p][:, i, 0:CK], bank[:, 0:CK], ACT.Copy))
                elif kind == "q":
                    if not (isinstance(m, int) and m == 0):
                        act.wait_ge(q_cos_ready, m)
                    for half in range(KD):
                        last = nc.scalar.activation(q_raw[:, half, :], bank[:, half * TQ:(half + 1) * TQ], ACT.Identity,
                                                    bias=bq[:, half:half + 1])
                    read(last)
                elif kind == "k" and self_:
                    for half in range(KD):
                        last = nc.scalar.activation(kT[p][:, half, :], bank[:, half * TQ:(half + 1) * TQ], ACT.Identity,
                                                    bias=bk[:, half:half + 1])
                    read(last)
                elif kind == "k":
                    if rope and not (isinstance(m, int) and m == 0):
                        act.wait_ge(k_cos_ready, KD * m)
                    to = k_raw if rope else kT[p]
                    read(nc.scalar.activation(to[:, i, :], bank[:, 0:nk], ACT.Identity, bias=bk[:, i:i + 1]))

            def exp(m, k, p):
                a = H * m + k
                act.wait_ge(max_ready, GROUPS * m + k // 2 + 1)
                if not (isinstance(a, int) and a < 4):
                    act.wait_ge(pT_ready, a - 3)
                nc.scalar.activation(probs[:, k % 4, :], ps[0:TQ, k % 4, 0:nk], ACT.Exp, bias=nmax[:, p, k:k + 1],
                                     accum_out=sums[:, p, k:k + 1]).then_inc(probs_ready, 1)

            def roots(m):
                act.wait_ge(floored, m + 1)
                nc.scalar.activation(norm[:], ss[:], ACT.Sqrt).then_inc(norm_ready, 1)

            def copy_heads(m, fill):
                act.wait_ge(heads_ready, SETS * m + 4 * (fill + 1))
                if not (isinstance(m, int) and m == 0):
                    act.wait_ge(piece_read, piece_count(f"R{fill}", m))
                nc.scalar.activation(heads_raw[:, fill, :], ps[:, OUT_BANK, 0:4 * TQ], ACT.Copy).then_inc(heads_copied, 1)

            def first_projections():
                for name in proj:
                    piece(name, 0, piece_count(name, -1), 0)
                    if name == "k5":
                        roots(0)

            def slot(n, k, p, first, last):
                todo = list(pieces(k, n, first, last)) if k < H else []
                for name, m, count in todo[:1]:
                    piece(name, m, count, 1 - p)
                    if name == "k5":
                        roots(m)
                if 1 <= k <= H:
                    exp(n, k - 1, p)
                elif k == 0 and not first:
                    exp(n - 1, H - 1, 1 - p)
                for name, m, count in todo[1:]:
                    piece(name, m, count, 1 - p)
                    if name == "k5":
                        roots(m)
                done = k - PV_LAG
                if done < 0:
                    if not first and (done + H + 1) % (4 * per_set) == 0:
                        copy_heads(n - 1, (done + H) // (4 * per_set))
                elif done < H and (done + 1) % (4 * per_set) == 0:
                    copy_heads(n, done // (4 * per_set))

            def batch(n, p, first, last):
                for k in range(H):
                    slot(n, k, p, first, last)

            def after():
                for k in range(H, H + 8):
                    slot(B - 1, k, 1, False, True)

            batches(act, first_projections, batch, after)

        @block.vector
        def _(dve):
            bank = ps[:, PIECE_BANK, :]

            def piece(name, m, count, p):
                kind, i = name[0], int(name[1:] or 0)
                read = lambda ins: ins.then_inc(piece_read, 1)
                if kind == "R":
                    dve.wait_ge(piece_ready, count)
                    dve.wait_ge(heads_copied, FILLS * m + i + 1)
                    read(nc.vector.tensor_tensor(headsT[:, i, :], bank[:, 0:4 * TQ], heads_raw[:, i, :], ALU.mult))
                elif kind == "O":
                    dve.wait_ge(piece_ready, count)
                    at = out[:, m, :] if cosine else part[:]
                    if cosine:
                        read(nc.vector.tensor_copy(at, bank[0:TQ, 0:D]))
                    else:
                        read(nc.vector.tensor_tensor(at, bank[0:TQ, 0:D], bo[:], ALU.add))
                        dve.wait_ge(piece_read, count)
                        if self_:
                            nc.vector.tensor_tensor(out[:, m, :], part[:], xn[:, m, :], ALU.add)
                        else:
                            nc.vector.scalar_tensor_tensor(x[:, m, :], part[:], gate, x[:, m, :], ALU.mult, ALU.add)
                elif cosine and kind in "qk":
                    j, rows, tokens = square_part(kind, i)
                    dve.wait_ge(piece_ready, count)
                    read(nc.vector.tensor_copy(tokens, bank[0:rows, :]))
                    for earlier in ([j - 2] if 2 <= j < 7 else [5, 6, 7] if j == 7 else []):
                        dve.wait_ge(sq_ready, 8 * m + earlier + 1)
                        rows, at = (TQ, earlier * 8) if earlier < 2 else (KT, H + (earlier - 2) * 8)
                        nc.vector.tensor_reduce(ss[0:rows, at:at + 8], sq[0:rows, earlier % 4, :].rearrange("p (h d) -> p h d", d=hd),
                                                AX.X, ALU.add).then_inc(summed, 1)
                    if name == "k5":
                        dve.wait_ge(summed, 8 * m + 8)
                        nc.vector.tensor_scalar(ss[:], ss[:], 1e-24, None, ALU.max).then_inc(floored, 1)
                elif cosine and kind == "v":
                    if i == 0:
                        dve.wait_ge(norm_ready, m + 1)
                        nc.vector.reciprocal(inv_norm[:], norm[:]).then_inc(inv_norm_ready, 1)
                        dve.wait_ge(inv_norm_ready, m + 1)
                        rows = q_tok[:].rearrange("p (h d) -> p h d", d=hd)
                        nc.vector.tensor_tensor(rows, rows, bcast(inv_norm[0:TQ, 0:H], 2, hd), ALU.mult).then_inc(scaled, 1)
                    elif i < 4:
                        rows = k_tok[:, i - 1, :].rearrange("p (h d) -> p h d", d=hd)
                        nc.vector.tensor_tensor(rows, rows, bcast(inv_norm[:, i * H:(i + 1) * H], 2, hd), ALU.mult).then_inc(scaled, 1)
                elif kind == "a":
                    dve.wait_ge(piece_ready, count)
                    read(nc.vector.tensor_tensor(qm[p][:, 8 * i:8 * i + 8, :].rearrange("p (i j) q -> p i j q", j=2),
                                                 bcast(bank[:, 0:4 * TQ].rearrange("p (i q) -> p i q", q=TQ), 2, 2),
                                                 bcast(bcast(head_mask[:], 1, 4), 3, TQ), ALU.mult))
                elif kind == "q" and not rope and not cosine:
                    dve.wait_ge(piece_ready, count)
                    for half in range(KD):
                        last = nc.vector.scalar_tensor_tensor(qm[p][:, half * per_half:(half + 1) * per_half, :],
                                                              bcast(bank[:, half * TQ:(half + 1) * TQ], 1, per_half), bq[:, half:half + 1],
                                                              bcast(mask[:], 2, TQ), ALU.add, ALU.mult)
                    read(last)
                elif kind == "v" and not cosine:
                    kt = tiles[i][1]
                    dve.wait_ge(piece_ready, count)
                    if i == 0 and not (isinstance(m, int) and m < 2):
                        dve.wait_ge(heads_ready, SETS * (m - 1))
                    read(nc.vector.tensor_tensor(v[p][0:kt, i, :], bank[0:kt, 0:D], bv[0:kt, :], ALU.add))
                elif kind == "r":
                    dve.wait_ge(piece_ready, count)
                    read(nc.vector.tensor_tensor(q_rot[:], bank[:, 0:KD * TQ].rearrange("p (k q) -> p k q", k=KD),
                                                 bcast(sinq[:], 1, KD), ALU.mult))
                    dve.wait_ge(piece_read, count)
                    dve.wait_ge(q_cos_ready, m + 1)
                    nc.vector.tensor_tensor(q_rot[:], q_rot[:], q_cos[:], ALU.add).then_inc(rot_steps, 1)
                    dve.wait_ge(rot_steps, m + 1)
                    for half in range(KD):
                        nc.vector.tensor_tensor(qm[p][:, half * per_half:(half + 1) * per_half, :], bcast(q_rot[:, half, :], 1, per_half),
                                                bcast(mask[:], 2, TQ), ALU.mult).then_inc(qm_ready, 1)
                elif kind == "s":
                    dve.wait_ge(piece_ready, count)
                    read(nc.vector.tensor_tensor(k_sin[:, i, :], bank[:, 0:nk], sink[:], ALU.mult))
                    dve.wait_ge(piece_read, count)
                    dve.wait_ge(k_cos_ready, KD * m + i + 1)
                    nc.vector.tensor_tensor(kT[p][:, i, :], kT[p][:, i, :], k_sin[:, i, :], ALU.add).then_inc(kT_ready, 1)

            def normalise_context(m):
                dve.wait_ge(ctx_ready[0], 16 * m + 16)
                for t in range(3):
                    r = 3 * m + t
                    last = nc.vector.tensor_scalar(cn[:, t, :], cx[:, t, :], cmv[:, bass.ds(r, 1), 0], crs[:, bass.ds(r, 1)],
                                                   ALU.subtract, ALU.mult)
                last.then_inc(cn_ready, 1)

            def raw_queries(m, p):
                for half in range(KD):
                    nc.vector.tensor_tensor(qm[p][:, half * per_half:(half + 1) * per_half, :],
                                            bcast(xnT[:, half, bass.ds(m * TQ, TQ)], 1, per_half),
                                            bcast(mask[:], 2, TQ), ALU.mult).then_inc(qm_ready, 1)

            def inverse_sums(m, p):
                dve.wait_ge(probs_ready, H * m + H)
                nc.vector.reciprocal(inv[:], sums[:, p, :]).then_inc(inv_ready, 1)
                dve.wait_ge(inv_ready, m + 1)
                nc.vector.tensor_copy(inv_wide[:], bcast(inv[:], 2, width)).then_inc(inv_wide_ready, 1)

            def copy_pT(m, k):
                dve.wait_ge(pT_ready, H * m + k + 1)
                if not (isinstance(m, int) and m == 0 and k < 8):
                    dve.wait_ge(heads_ready, SETS * m + (k - 8) // per_set + 1)
                rows = tiles[-1][1]
                nc.vector.tensor_copy(probsT[0:rows, k % 8, :], ps[0:rows, 4 + k % 2, 0:NT * TQ]).then_inc(pT_copied, 1)

            def first_projections():
                if cosine:
                    normalise_context(0)
                if raw:
                    raw_queries(0, 0)
                for name in proj:
                    piece(name, 0, piece_count(name, -1), 0)

            def slot(n, k, p, first, last):
                if k == 0 and cosine and not last:
                    normalise_context(n + 1)
                if k < H and k % 2:
                    dve.wait_ge(scores_ready, H * n + k + 1)
                    nc.vector.tensor_reduce(nmax[:, p, k - 1:k + 1], ps[0:TQ, (k - 1) % 4:(k - 1) % 4 + 2, 0:nk], AX.X, ALU.max,
                                            negate=True).then_inc(max_ready, 1)
                todo = list(pieces(k, n, first, last)) if k < H else [(name, n, piece_count(name, B)) for name in tail if name in where.get(k - H, [])]
                for name, m, count in todo[:1]:
                    piece(name, m, count, 1 - p)
                if k >= S_LAG or not first:
                    if k - S_LAG < H:
                        copy_pT(n if k >= S_LAG else n - 1, (k - S_LAG) % H)
                for name, m, count in todo[1:]:
                    piece(name, m, count, 1 - p)
                if k == 2 and not first:
                    inverse_sums(n - 1, 1 - p)
                if k == H + 2:
                    inverse_sums(n, p)
                if k == 8 and raw and not last:
                    raw_queries(n + 1, 1 - p)

            def batch(n, p, first, last):
                for k in range(H):
                    slot(n, k, p, first, last)

            def after():
                for k in range(H, H + 8):
                    slot(B - 1, k, 1, False, True)

            batches(dve, first_projections, batch, after)


def mask_row(nc, core, tag, allow8, hidden, one_row, sb):
    allow = sb("allow", [1, B, CK])
    with ExitStack() as c:
        steps = core["phases"].sem(f"{tag}_mask_steps")
        block = core["phases"].block(c)

        @block.vector
        def _(dve):
            chain = Chain(dve, steps)
            chain.step(nc.vector.tensor_copy(allow[:], allow8[:]))
            chain.step(nc.vector.tensor_scalar(hidden[0:1, :, :], allow[:], 1.0, 3e38, ALU.subtract, ALU.mult))
            chain.step(nc.vector.memset(one_row[0:1, :], 1.0))


def context_stats(nc, core, tag, A, cmv, crs):
    R = 3 * B
    with ExitStack() as c:
        sb = lambda n, s: c.enter_context(nc.sbuf_tensor(f"{tag}_{n}", s, FP32))
        sem = lambda n: core["phases"].sem(f"{tag}_c_{n}")
        rows, stats, var_eps, std = sb("rows", [KT, R, D]), sb("rstats", [KT, R, 6]), sb("var_eps", [KT, R]), sb("rstd", [KT, R])
        landed = [sem(f"landed_{q}") for q in range(4)]
        stats_ready, mv_ready, var_ready, std_ready, inv_ready = [sem(n) for n in ("stats", "mv", "var", "std", "inv")]
        block = core["phases"].block(c)

        @block.sync
        def _(sp):
            for q in range(4):
                sp.dma_start(rows[:, 6 * q:6 * q + 6, :],
                             A["ctx"][2 * q:2 * q + 2].rearrange("b (t p) d -> p (b t) d", p=KT)).then_inc(landed[q], 16)

        @block.vector
        def _(dve):
            for r in range(R):
                if r % 6 == 0:
                    dve.wait_ge(landed[r // 6], 16)
                nc.vector.bn_stats(stats[:, r, :], rows[:, r, :]).then_inc(stats_ready, 1)
            for r in range(R):
                dve.wait_ge(stats_ready, r + 1)
                nc.vector.bn_aggr(cmv[:, r, :], stats[:, r, :]).then_inc(mv_ready, 1)
            dve.wait_ge(mv_ready, R)
            nc.vector.tensor_scalar(var_eps[:], cmv[:, :, 1], LN_EPS, None, ALU.add).then_inc(var_ready, 1)
            dve.wait_ge(std_ready, 1)
            nc.vector.reciprocal(crs[:], std[:]).then_inc(inv_ready, 1)
            dve.wait_ge(inv_ready, 1)

        @block.scalar
        def _(act):
            act.wait_ge(var_ready, 1)
            nc.scalar.activation(std[:], var_eps[:], ACT.Sqrt).then_inc(std_ready, 1)


def null_row(nc, core, tag, A, kT, head_mask, mask, qk_gain, hd, sb):
    ps = core["ps"]
    nk_col, sq_col, both, tmp = sb("null_col", [P, 1]), sb("null_sq", [P, 1]), sb("same_head", [P, P]), sb("null_norm", [P, 4])
    with ExitStack() as c:
        sem = lambda n: core["phases"].sem(f"{tag}_n_{n}")
        landed, dve_steps, norm_ready, root = sem("landed"), sem("steps"), sem("norm_ready"), sem("root")
        block = core["phases"].block(c)

        @block.sync
        def _(sp):
            sp.dma_start(nk_col[:], A["null_k"]).then_inc(landed, 16)
            sp.dma_start(both[:], A["same_head"]).then_inc(landed, 16)
            sp.wait_ge(landed, 32)

        @block.vector
        def _(dve):
            chain = Chain(dve, dve_steps)
            dve.wait_ge(landed, 32)
            chain.step(nc.vector.tensor_tensor(sq_col[:], nk_col[:], nk_col[:], ALU.mult))
            dve.wait_ge(norm_ready, 1)
            chain.step(nc.vector.tensor_scalar(tmp[:, 0:1], ps[:, 0, 0:1], 1e-24, None, ALU.max))
            dve.wait_ge(root, 1)
            chain.step(nc.vector.reciprocal(tmp[:, 2:3], tmp[:, 1:2]))
            chain.step(nc.vector.tensor_tensor(tmp[:, 3:4], nk_col[:], tmp[:, 2:3], ALU.mult))
            for keys in kT:
                chain.step(nc.vector.tensor_copy(keys[:, :, CK:CK + 1], bcast(tmp[:, 3:4], 1, keys.shape[1])))
            chain.step(nc.vector.tensor_scalar(head_mask[:], mask[:], qk_gain[:, 0:1], qk_gain[:, 1:2], ALU.mult, ALU.mult))

        core["phases"].run_ahead(block, True)

        @block.tensor
        def _(pe):
            pe.wait_ge(dve_steps, 1)
            nc.tensor.matmul(ps[:, 0, 0:1], both[:], sq_col[:], start=True, stop=True).then_inc(norm_ready, 1)

        @block.scalar
        def _(act):
            act.wait_ge(dve_steps, 2)
            nc.scalar.activation(tmp[:, 1:2], tmp[:, 0:1], ACT.Sqrt).then_inc(root, 1)



def ranks(nc, chain, logits, before, E, greater, equal, rank):
    over_j, over_e = bcast(logits, 2, E), bcast(logits, 3, E)
    chain.step(nc.vector.tensor_tensor(greater, over_j, over_e, ALU.is_gt))
    chain.step(nc.vector.tensor_tensor(equal, over_j, over_e, ALU.is_equal))
    chain.step(nc.vector.tensor_tensor(equal, equal, bcast(before, 1, B), ALU.mult))
    chain.step(nc.vector.tensor_tensor(greater, greater, equal, ALU.add))
    chain.step(nc.vector.tensor_reduce(rank, greater, AX.X, ALU.add))


def route(nc, core, tag, kind, A, xT, gates, before_it, y=None):
    ps, ident = core["ps"], core["ident"]
    G, E = 4, 8
    cols = G + E if kind == "hier" else E
    b2_in = kind in ("hier", "top1")
    with ExitStack() as c:
        sb = lambda n, s: c.enter_context(nc.sbuf_tensor(f"{tag}_{n}", s, FP32))
        sem = lambda n: core["phases"].sem(f"{tag}_{n}")
        wr, bias, before = sb("wr", [P, KD, cols]), sb("bias", [TQ, cols]), sb("before", [TQ, E, E])
        logits = sb("logits", [TQ, B, cols])
        greater, equal = sb("greater", [TQ, B, E, E]), sb("equal", [TQ, B, E, E])
        rank, top, picked = sb("rank", [TQ, B, E]), sb("top", [TQ, B]), sb("picked", [TQ, B, E])
        shifted, exps = sb("shifted", [TQ, B, E]), sb("exps", [TQ, B, E])
        total, inv = sb("total", [TQ, B]), sb("inv", [TQ, B])
        loads = [(wr[:], A["wr"].rearrange("(k p) n -> p k n", p=P)), (before[:], A["before"].partition_broadcast(TQ))]
        if "br" in A:
            loads.append((bias[:], A["br"].partition_broadcast(TQ)))
        if b2_in:
            b2, gatesT = sb("b2", [E, D]), sb("gatesT", [E, N])
            loads.append((b2[:], A["b2"]))
        if kind == "hier":
            etop, eshift, eexp = sb("etop", [TQ, B, G]), sb("eshift", [TQ, B, G, 2]), sb("eexp", [TQ, B, G, 2])
            etotal, einv, epick = sb("etotal", [TQ, B, G]), sb("einv", [TQ, B, G]), sb("epick", [TQ, B, G, 2])
        core["phases"].ask(tag, loads)
        before_it()
        logits_ready, steps, exp_asked, exp_ready = sem("logits_ready"), sem("steps"), sem("exp_asked"), sem("exp_ready")
        gates_ready, gatesT_ready, gatesT_copied = sem("gates_ready"), sem("gatesT_ready"), sem("gatesT_copied")
        y_ready, y_copied = sem("y_ready"), sem("y_copied")
        block = core["phases"].block(c)
        core["phases"].run_ahead(block, True)

        @block.tensor
        def _(pe):
            for b in range(B):
                for k in range(KD):
                    last = nc.tensor.matmul(ps[0:TQ, 0, b * cols:(b + 1) * cols], xT[:, k, b * TQ:(b + 1) * TQ],
                                            wr[:, k, :], start=k == 0, stop=k == KD - 1)
            last.then_inc(logits_ready, 1)
            if b2_in:
                pe.wait_ge(gates_ready, 1)
                for b in range(B):
                    last = nc.tensor.transpose(ps[0:E, 1 + b // 4, (b % 4) * TQ:(b % 4 + 1) * TQ], gates[:, b, 0:E],
                                               ident[0:TQ, 0:TQ])
                last.then_inc(gatesT_ready, 1)
                pe.wait_ge(gatesT_copied, 2)
                for b in range(B):
                    if b >= 4:
                        pe.wait_ge(y_copied, b - 3)
                    nc.tensor.matmul(ps[0:TQ, 4 + b % 4, 0:D], gatesT[:, b * TQ:(b + 1) * TQ], b2[:],
                                     start=True, stop=True).then_inc(y_ready, 1)

        @block.scalar
        def _(act):
            act.wait_ge(exp_asked, 1)
            nc.scalar.activation(exps[:, :, 0:G if kind == "hier" else E], shifted[:, :, 0:G if kind == "hier" else E],
                                 ACT.Exp).then_inc(exp_ready, 1)
            if kind == "hier":
                nc.scalar.activation(eexp[:], eshift[:], ACT.Exp).then_inc(exp_ready, 1)

        @block.vector
        def _(dve):
            chain = Chain(dve, steps)
            v = nc.vector
            dve.wait_ge(logits_ready, 1)
            from_pe = ps[0:TQ, 0, 0:B * cols].rearrange("p (b e) -> p b e", e=cols)
            if "br" in A:
                chain.step(v.tensor_tensor(logits[:], from_pe, bcast(bias[:], 1, B), ALU.add))
            else:
                chain.step(v.tensor_copy(logits[:], from_pe))
            choose = G if kind == "hier" else E
            lg = logits[:, :, 0:choose]
            chain.step(v.tensor_reduce(top[:], lg, AX.X, ALU.max))
            sh = shifted[:, :, 0:choose]
            if kind == "hier":
                el = logits[:, :, G:].rearrange("p b (g e) -> p b g e", e=2)
                chain.step(v.tensor_reduce(etop[:], el, AX.X, ALU.max))
                chain.step(v.tensor_tensor(eshift[:], el, bcast(etop[:], 3, 2), ALU.subtract))
            v.tensor_tensor(sh, lg, bcast(top[:], 2, choose), ALU.subtract).then_inc(exp_asked, 1)
            ranks(nc, chain, lg, before[:, 0:choose, 0:choose], choose, greater[:, :, 0:choose, 0:choose],
                  equal[:, :, 0:choose, 0:choose], rank[:, :, 0:choose])
            k = {"hier": 1, "top1": 1, "top4": 4, "top2": 2}[kind]
            chain.step(v.tensor_scalar(picked[:, :, 0:choose], rank[:, :, 0:choose], k - 0.5, None, ALU.is_lt))
            dve.wait_ge(exp_ready, 2 if kind == "hier" else 1)
            ex = exps[:, :, 0:choose]
            if kind == "top4":
                chain.step(v.tensor_tensor(ex, ex, picked[:], ALU.mult))
            chain.step(v.tensor_reduce(total[:], ex, AX.X, ALU.add))
            chain.step(v.reciprocal(inv[:], total[:]))
            if kind == "hier":
                chain.step(v.tensor_reduce(etotal[:], eexp[:], AX.X, ALU.add))
                chain.step(v.reciprocal(einv[:], etotal[:]))
                chain.step(v.tensor_tensor(epick[:, :, :, 0], el[:, :, :, 0], el[:, :, :, 1], ALU.is_ge))
                chain.step(v.tensor_tensor(epick[:, :, :, 1], el[:, :, :, 1], el[:, :, :, 0], ALU.is_gt))
                chain.step(v.tensor_tensor(einv[:], einv[:], bcast(inv[:], 2, G), ALU.mult))
                chain.step(v.tensor_tensor(einv[:], einv[:], picked[:, :, 0:G], ALU.mult))
                v.tensor_tensor(gates[:, :, 0:E].rearrange("p b (g e) -> p b g e", e=2), epick[:], bcast(einv[:], 3, 2),
                                ALU.mult).then_inc(gates_ready, 1)
            elif kind == "top1":
                v.tensor_tensor(gates[:, :, 0:E], picked[:], bcast(inv[:], 2, E), ALU.mult).then_inc(gates_ready, 1)
            else:
                if kind == "top2":
                    chain.step(v.tensor_tensor(ex, ex, picked[:], ALU.mult))
                v.tensor_tensor(gates[:, :, 0:E], ex, bcast(inv[:], 2, E), ALU.mult).then_inc(gates_ready, 1)
            if kind == "top4":
                v.memset(gates[:, :, E:E + 1], 1.0).then_inc(gates_ready, 1)
                v.memset(y[:], 0.0).then_inc(gates_ready, 1)
            if b2_in:
                for i in range(2):
                    dve.wait_ge(gatesT_ready, 1)
                    v.tensor_copy(gatesT[:, i * HALF:(i + 1) * HALF], ps[0:E, 1 + i, 0:HALF]).then_inc(gatesT_copied, 1)
                for b in range(B):
                    dve.wait_ge(y_ready, b + 1)
                    v.tensor_copy(y[:, b, :], ps[0:TQ, 4 + b % 4, 0:D]).then_inc(y_copied, 1)


def experts(nc, core, tag, A, xT, gates, y, E, F, tile, swiglu, cut, before):
    ps = core["ps"]
    NF = -(-F // tile)
    size = [min(tile, F - f * tile) for f in range(NF)]
    UP = ("w1", "w2") if swiglu else ("w1",)
    down = A["w3"] if swiglu else A["w2"]
    whole = NF if size[-1] == tile else NF - 1
    SPLITS = len(UP) + 1 + (whole < NF)
    with ExitStack() as c:
        sb = lambda n, s, t=FP32: c.enter_context(nc.sbuf_tensor(f"{tag}_{n}", s, t))
        sem = lambda n: core["phases"].sem(f"{tag}_{n}")
        up_high = [[sb(f"{u}_high_{s}", [P, KD, F], FP32R) for u in UP] for s in range(2)]
        up_low = [[sb(f"{u}_low_{s}", [P, KD, F], FP32R) for u in UP] for s in range(2)]
        up_loaded, down_loaded = [sb(f"{u}_loaded", [P, KD, F]) for u in UP], sb("down_loaded", [tile, NF, D])
        down_high = [sb(f"down_high_{s}", [tile, NF, D], FP32R) for s in range(2)]
        down_low = [sb(f"down_low_{s}", [tile, NF, D], FP32R) for s in range(2)]
        x_high, x_low = sb("x_high", [P, KD, N], FP32R), sb("x_low", [P, KD, N], FP32R)
        h = sb("h", [tile, 2, HALF])
        h_high, h_low = sb("h_high", [tile, NF, N], FP32R), sb("h_low", [tile, NF, N], FP32R)
        if swiglu:
            sig, gated = sb("sig", [tile, 2, HALF]), sb("gated", [tile, 2, HALF])
        else:
            b1 = [sb(f"b1_{s}", [P, NF]) for s in range(2)]

        def weight_loads(n):
            out = [(t[:], A[u][n].rearrange("(k p) f -> p k f", p=P)) for u, t in zip(UP, up_loaded)]
            out.append((down_loaded[:, 0:whole, :], down[n, 0:whole * tile, :].rearrange("(f p) d -> p f d", p=tile)))
            if whole < NF:
                out.append((down_loaded[0:size[-1], whole, :], down[n, whole * tile:F, :]))
            return out

        core["phases"].ask(tag, weight_loads(0) + ([] if swiglu else [(b1[n][:], A["b1"][n]) for n in range(2)]))
        before()
        weights_ready, b1_ready = sem("weights_ready"), [sem("b1_ready_0"), sem("b1_ready_1")]
        weights_used, weights_high, weights_split = sem("weights_used"), sem("weights_high"), sem("weights_split")
        x_high_ready, x_split = sem("x_high_ready"), sem("x_split")
        up_ready, sig_ready, gated_ready = sem("up_ready"), sem("sig_ready"), sem("gated_ready")
        h_ready, h_high_ready, h_split = sem("h_ready"), sem("h_high_ready"), sem("h_split")
        y_ready, y_added = sem("y_ready"), sem("y_added")
        PARTS = 2 * NF
        BANKS = 2 if swiglu else 4
        block = core["phases"].block(c)

        def weights(s):
            out = [(t[:], high[:], low[:]) for t, high, low in zip(up_loaded, up_high[s], up_low[s])]
            out.append([t[:, 0:whole, :] for t in (down_loaded, down_high[s], down_low[s])])
            if whole < NF:
                out.append([t[0:size[-1], whole, :] for t in (down_loaded, down_high[s], down_low[s])])
            return out

        def experts_of(engine, one, with_pair=False):
            with engine.Fori(0, E // 2 - 1, 1) as i:
                for s in range(2):
                    one(2 * i + s, s, *([i] if with_pair else []))
            for n in range(E - 2, E):
                one(n, n % 2, *([n // 2] if with_pair else []))

        @block.sync
        def _(sp):
            def load(n, s):
                sp.wait_ge(weights_split, n * SPLITS)
                for to, src in weight_loads(n):
                    sp.dma_start(to, src).then_inc(weights_ready, 16)
                if not swiglu and not (isinstance(n, int) and n == 1):
                    sp.wait_ge(weights_used, n - 1)
                    sp.dma_start(b1[s][:], A["b1"][n]).then_inc(b1_ready[s], 16)
            load(1, 1)
            with sp.Fori(1, E // 2, 1) as i:
                for s in range(2):
                    load(2 * i + s, s)

        @block.gpsimd
        def _(pool):
            def split_low(n, s):
                for j, (loaded, high, low) in enumerate(weights(s)):
                    pool.wait_ge(weights_high, n * SPLITS + j + 1)
                    nc.gpsimd.tensor_tensor(low, loaded, high.bitcast(FP32), ALU.subtract).then_inc(weights_split, 1)
            experts_of(pool, split_low)

        @block.tensor
        def _(pe):
            def product(out, left, right, start, stop):
                nc.tensor.matmul(out, left[0], right[0], start=start, stop=False)
                nc.tensor.matmul(out, left[0], right[1], start=False, stop=False)
                return nc.tensor.matmul(out, left[1], right[0], start=False, stop=stop)

            def one(n, s):
                pe.wait_ge(weights_split, n * SPLITS + SPLITS)
                for part in range(PARTS):
                    chunk, f = divmod(part, NF)
                    pe.wait_ge(h_ready, n * PARTS + (part - BANKS + 2 if part >= BANKS else 1))
                    for u in range(len(UP)):
                        bank = (part % BANKS) * len(UP) + u
                        for k in range(KD):
                            at = slice(f * tile, f * tile + size[f])
                            tokens = slice(chunk * HALF, (chunk + 1) * HALF)
                            last = product(ps[0:size[f], bank, 0:HALF],
                                           (up_high[s][u][:, k, at], up_low[s][u][:, k, at]),
                                           (x_high[:, k, tokens], x_low[:, k, tokens]), k == 0, k == KD - 1)
                    last.then_inc(up_ready, 1)
                for b in range(B):
                    if b % 4 == 0:
                        pe.wait_ge(h_split, n * PARTS + (b // 4 + 1) * NF + 1)
                    pe.wait_ge(y_added, n * B + (b - 2 if b >= 4 else 1))
                    for f in range(NF):
                        tokens = slice(b * TQ, (b + 1) * TQ)
                        last = product(ps[0:TQ, 4 + b % 4, 0:D], (h_high[0:size[f], f, tokens], h_low[0:size[f], f, tokens]),
                                       (down_high[s][0:size[f], f, :], down_low[s][0:size[f], f, :]),
                                       f == 0, f == NF - 1)
                    last.then_inc(y_ready, 1)
                pe.wait_ge(y_ready, n * B + B + 1)
                pe.sem_inc(weights_used, 1)
            pe.sem_inc(y_ready, 1)
            pe.wait_ge(x_split, 1)
            experts_of(pe, one)

        @block.scalar
        def _(act):
            def split_high(n, s):
                for loaded, high, low in weights(s):
                    nc.scalar.activation(high, loaded, ACT.Copy).then_inc(weights_high, 1)

            def hidden_high(n, part):
                chunk, f = divmod(part, NF)
                m = size[f]
                act.wait_ge(h_ready, n * PARTS + part + 2)
                nc.scalar.activation(h_high[0:m, f, chunk * HALF:(chunk + 1) * HALF], h[0:m, part % 2, :], ACT.Copy).then_inc(h_high_ready, 1)

            def one(n, s):
                act.wait_ge(y_ready, n * B + 1)
                if not swiglu:
                    act.wait_ge(b1_ready[s], 8 * (n - s) + 1)
                for part in range(PARTS):
                    chunk, f = divmod(part, NF)
                    act.wait_ge(up_ready, n * PARTS + part + 1)
                    if swiglu:
                        act.wait_ge(gated_ready, n * PARTS + (part if part >= 2 else 1))
                        nc.scalar.activation(sig[0:size[f], part % 2, :], ps[0:size[f], 2 * (part % BANKS), 0:HALF],
                                             ACT.Sigmoid).then_inc(sig_ready, 1)
                    else:
                        act.wait_ge(h_split, n * PARTS + (part if part >= 2 else 1))
                        nc.scalar.activation(h[:, part % 2, :], ps[:, part % BANKS, 0:HALF], ACT.Relu,
                                             bias=b1[s][:, f:f + 1]).then_inc(h_ready, 1)
                    if part and swiglu:
                        hidden_high(n, part - 1)
                    if part == NF and not (isinstance(n, int) and n == E - 1):
                        act.wait_ge(weights_ready, 16 * SPLITS * (n + 1))
                        split_high(n + 1, 1 - s)
                if swiglu:
                    hidden_high(n, PARTS - 1)

            act.sem_inc(h_high_ready, 1)
            for ready in b1_ready:
                act.sem_inc(ready, 1)
            nc.scalar.activation(x_high[:], xT[:], ACT.Copy).then_inc(x_high_ready, 1)
            split_high(0, 0)
            experts_of(act, one)

        @block.vector
        def _(dve):
            def hidden_low(n, part):
                chunk, f = divmod(part, NF)
                m = size[f]
                tokens = slice(chunk * HALF, (chunk + 1) * HALF)
                if not swiglu:
                    dve.wait_ge(h_ready, n * PARTS + part + 2)
                    nc.vector.tensor_copy(h_high[0:m, f, tokens], h[0:m, part % 2, :]).then_inc(h_high_ready, 1)
                dve.wait_ge(h_high_ready, n * PARTS + part + 2)
                nc.vector.tensor_tensor(h_low[0:m, f, tokens], h[0:m, part % 2, :], h_high[0:m, f, tokens].bitcast(FP32),
                                        ALU.subtract).then_inc(h_split, 1)

            def one(n, s, pair):
                for part in range(PARTS):
                    f = part % NF
                    m = size[f]
                    if swiglu:
                        dve.wait_ge(sig_ready, n * PARTS + part + 1)
                        nc.vector.tensor_tensor(gated[0:m, part % 2, :], ps[0:m, 2 * (part % BANKS), 0:HALF], sig[0:m, part % 2, :],
                                                ALU.mult).then_inc(gated_ready, 1)
                        dve.wait_ge(gated_ready, n * PARTS + part + 2)
                        nc.vector.tensor_tensor(h[0:m, part % 2, :], ps[0:m, 2 * (part % BANKS) + 1, 0:HALF],
                                                gated[0:m, part % 2, :], ALU.mult).then_inc(h_ready, 1)
                    if part:
                        hidden_low(n, part - 1)
                hidden_low(n, PARTS - 1)
                for b in range(B):
                    dve.wait_ge(y_ready, n * B + b + 2)
                    dve.wait_ge(y_added, n * B + 1)
                    e = n if cut == 1 else pair
                    gate = gates[:, b, e:e + 1] if isinstance(e, int) else gates[:, b, bass.ds(e, 1)]
                    nc.vector.scalar_tensor_tensor(y[:, b, :], ps[0:TQ, 4 + b % 4, 0:D], gate, y[:, b, :], ALU.mult,
                                                   ALU.add).then_inc(y_added, 1)

            dve.sem_inc(y_added, 1)
            dve.sem_inc(h_ready, 1)
            dve.sem_inc(h_split, 1)
            if swiglu:
                dve.sem_inc(gated_ready, 1)
            dve.wait_ge(x_high_ready, 1)
            nc.vector.tensor_tensor(x_low[:], xT[:], x_high[:].bitcast(FP32), ALU.subtract).then_inc(x_split, 1)
            experts_of(dve, one, True)


def lora(nc, core, tag, A, x, gate, xn, xnT, gates, before):
    ps, ident = core["ps"], core["ident"]
    E, R = 8, 4
    ER = E * R
    with ExitStack() as c:
        sb = lambda n, s: c.enter_context(nc.sbuf_tensor(f"{tag}_{n}", s, FP32))
        sem = lambda n: core["phases"].sem(f"{tag}_{n}")
        wl, left, right, bias = sb("wl", [P, KD, D]), sb("left", [P, KD, ER]), sb("right", [ER, D]), sb("bias", [TQ, D])
        low, lowT, part = sb("low", [TQ, B, ER]), sb("lowT", [ER, N]), sb("part", [TQ, 2, D])
        core["phases"].ask(tag, [(wl[:], A["wl"].rearrange("(k p) n -> p k n", p=P)), (left[:], A["left"].rearrange("(k p) n -> p k n", p=P)),
                           (right[:], A["right"]), (bias[:], A["bl"].partition_broadcast(TQ))])
        before()
        low_ready, low_scaled, lowT_ready, lowT_copied = sem("low_ready"), sem("low_scaled"), sem("lowT_ready"), sem("lowT_copied")
        out_ready, biased, x_done = sem("out_ready"), sem("biased"), sem("x_done")
        block = core["phases"].block(c)

        @block.tensor
        def _(pe):
            for b in range(B):
                for k in range(KD):
                    last = nc.tensor.matmul(ps[0:TQ, 0, b * ER:(b + 1) * ER], xnT[:, k, b * TQ:(b + 1) * TQ], left[:, k, :],
                                            start=k == 0, stop=k == KD - 1)
            last.then_inc(low_ready, 1)
            pe.wait_ge(low_scaled, 1)
            for b in range(B):
                last = nc.tensor.transpose(ps[0:ER, 1 + b // 4, (b % 4) * TQ:(b % 4 + 1) * TQ], low[:, b, :], ident[0:TQ, 0:TQ])
            last.then_inc(lowT_ready, 1)
            pe.wait_ge(lowT_copied, 2)
            for b in range(B):
                if b >= 4:
                    pe.wait_ge(biased, b - 3)
                for k in range(KD):
                    nc.tensor.matmul(ps[0:TQ, 4 + b % 4, 0:D], xnT[:, k, b * TQ:(b + 1) * TQ], wl[:, k, :], start=k == 0, stop=False)
                nc.tensor.matmul(ps[0:TQ, 4 + b % 4, 0:D], lowT[:, b * TQ:(b + 1) * TQ], right[:], start=False, stop=True)\
                    .then_inc(out_ready, 1)

        @block.vector
        def _(dve):
            v = nc.vector
            dve.wait_ge(low_ready, 1)
            v.tensor_tensor(low[:].rearrange("p b (e r) -> p b e r", r=R),
                            ps[0:TQ, 0, 0:B * ER].rearrange("p (b e r) -> p b e r", e=E, r=R),
                            bcast(gates[:, :, 0:E], 3, R), ALU.mult).then_inc(low_scaled, 1)
            dve.wait_ge(lowT_ready, 1)
            for i in range(2):
                v.tensor_copy(lowT[:, i * HALF:(i + 1) * HALF], ps[0:ER, 1 + i, 0:HALF]).then_inc(lowT_copied, 1)
            for b in range(B):
                dve.wait_ge(out_ready, b + 1)
                if b >= 2:
                    dve.wait_ge(x_done, b - 1)
                v.tensor_tensor(part[:, b % 2, :], ps[0:TQ, 4 + b % 4, 0:D], bias[:], ALU.add).then_inc(biased, 1)
                dve.wait_ge(biased, b + 1)
                v.scalar_tensor_tensor(x[:, b, :], part[:, b % 2, :], gate, x[:, b, :], ALU.mult, ALU.add).then_inc(x_done, 1)
            dve.wait_ge(x_done, B)



def start(nc, core, A, cols):
    with ExitStack() as c:
        landed, tanh_done, cleared = [core["phases"].sem(f"start_{n}") for n in ("landed", "tanh", "cleared")]
        raw = c.enter_context(nc.sbuf_tensor("start_gates", [P, 8], FP32))
        block = core["phases"].block(c)

        @block.sync
        def _(sp):
            sp.dma_start(core["x"][:], A["x"].rearrange("b t d -> t b d")).then_inc(landed, 16)
            sp.dma_start(core["ident"][:], A["ident"]).then_inc(landed, 16)
            for to, n in zip(cols, ("L0_ln_in_g", "L0_ln_in_b")):
                sp.dma_start(to[:], A[n]).then_inc(landed, 16)
            sp.dma_start(raw[:, 0:4], A["g_xattn"].partition_broadcast(P)).then_inc(landed, 16)
            sp.dma_start(raw[:, 4:8], A["g_ffn"].partition_broadcast(P)).then_inc(landed, 16)

        core["phases"].run_ahead(block, False)

        @block.scalar
        def _(act):
            act.wait_ge(landed, 96)
            nc.scalar.activation(core["gate"][:], raw[:], ACT.Tanh).then_inc(tanh_done, 1)
            act.wait_ge(tanh_done, 1)

        @block.vector
        def _(dve):
            for bank in (4, 5, 6):
                nc.vector.memset(core["ps"][:, bank, :], 0.0).then_inc(cleared, 1)


def network(nc, A, y_out, stages=8):
    with ExitStack() as c:
        sb = lambda n, s: c.enter_context(nc.sbuf_tensor(n, s, FP32))
        core = {"ps": c.enter_context(nc.psum_tensor("ps", [P, 8, BANK], FP32)), "ident": sb("ident", [P, P]),
                "x": sb("x_now", [TQ, B, D]), "gate": sb("gate", [P, 8]), "phases": Phases(nc)}
        x, xn, xnT, y = core["x"], sb("xn", [TQ, B, D]), sb("xnT", [P, KD, N]), sb("y_acc", [TQ, B, D])
        gates = sb("gates", [TQ, B, 9])
        gate = lambda i: core["gate"][0:TQ, i:i + 1]
        sub = lambda prefix, names: {n: A[prefix + m] for n, m in names.items()}
        const = {n: A[n] for n in ("before", "ctx", "ctxT", "same_head", "rot", "cosq", "sinq", "cosk", "sink")}
        projections = dict(wq="Wq", wk="Wk", wv="Wv", bq="bq", bk="bk", bv="bv", wo="Wo", bo="bo")

        cols = [sb(f"col_{n}", [P, KD]) for n in ("ln_in_g", "ln_in_b")]

        def first_normal():
            start(nc, core, A, cols)
            layernorm_all(nc, core, "l0a", x, xn)
            layernorm_all(nc, core, "l0b", xn, xn, xT=xnT, xT_affine=cols)
        if stages >= 1:
            attention(nc, core, "a0", "cosine", {**const, **sub("L0_xattn_", dict(
                wq="Wq", wk="Wk", wv="Wv", wo="Wo", q_scale="q_scale", k_scale="k_scale", ctx_gain="ln_ctx_g",
                ctx_offset="ln_ctx_b", null_k="null_k", null_v="null_v")), "mask": A["mask2"]},
                x, gate(0), xn, xnT, first_normal, out=y)
            layernorm_all(nc, core, "l0c", y, y, affine=(A["L0_ln_out_g"], A["L0_ln_out_b"]), update=(x, gate(0)))
        if stages >= 2:
            attention(nc, core, "s0", "self", {**const, **sub("L0_ffn_", dict(
                wq="wq", wk="wk", wv="wv", bq="bq", bk="bk", bv="bv", wo="wo", bo="out_proj_b")), "mask": A["mask_quarter"]},
                x, gate(4), xn, xnT, lambda: layernorm_all(nc, core, "l1a", x, xn, xT=xnT, settle=True), out=y)
            normal = lambda: layernorm_all(nc, core, "l1b", y, xn, affine=(A["L0_ffn_ln1_g"], A["L0_ffn_ln1_b"]), xT=xnT, settle=True)
            routing = lambda: route(nc, core, "r0", "hier", {**const, **sub("L0_ffn_", dict(wr="wr", br="br", b2="b2"))},
                                    xnT, gates, normal, y)
            experts(nc, core, "e0", sub("L0_ffn_", dict(w1="w1", b1="b1", w2="w2")), xnT, gates, y, 8, 512, P, False, 1, routing)
            layernorm_all(nc, core, "l1c", y, y, add=(xn, None), affine=(A["L0_ffn_ln2_g"], A["L0_ffn_ln2_b"]), update=(x, gate(4)))
        if stages >= 3:
            attention(nc, core, "a1", "linear", {**const, **sub("L1_xattn_", projections), "mask": A["mask_quarter"]},
                      x, gate(1), xn, xnT, lambda: layernorm_all(nc, core, "l2a", x, xn, xT=xnT, settle=True))
        add = None
        if stages >= 4:
            normal = lambda: layernorm_all(nc, core, "l3a", x, xn, xT=xnT, settle=True)
            routing = lambda: route(nc, core, "r1", "top4", {**const, **sub("L1_ffn_", dict(wr="Wg", br="routing_bias"))},
                                    xnT, gates, normal, y)
            experts(nc, core, "e1", sub("L1_ffn_", dict(w1="W1", w2="W2", w3="W3")), xnT, gates, y, 18, 341, 114, True, 2, routing)
            add = (y, gate(5))
        if stages >= 5:
            attention(nc, core, "a2", "raw", {**const, **sub("L2_xattn_", dict(wo="W_out", bo="b_out")), "mask": A["mask_one"]},
                      x, gate(2), xn, xnT, lambda: layernorm_all(nc, core, "l4a", x, xn, xT=xnT, add=(y, gate(5)), settle=True))
            add = None
        if stages >= 6:
            normal = lambda: layernorm_all(nc, core, "l5a", x, xn, xT=xnT, settle=True)
            routing = lambda: route(nc, core, "r2", "top1", {**const, **sub("L2_ffn_", dict(wr="router_W", br="router_b", b2="b2"))},
                                    xnT, gates, normal, y)
            experts(nc, core, "e2", sub("L2_ffn_", dict(w1="W1", b1="b1", w2="W2")), xnT, gates, y, 16, 512, P, False, 2, routing)
            add = (y, gate(6))
        if stages >= 7:
            attention(nc, core, "a3", "rope", {**const, **sub("L3_xattn_", projections), "mask": A["mask_eighth"], "allow": A["mask"]},
                      x, gate(3), xn, xnT, lambda: layernorm_all(nc, core, "l6a", x, xn, xT=xnT, add=(y, gate(6)), settle=True))
            add = None
        if stages >= 8:
            normal = lambda: layernorm_all(nc, core, "l7a", x, xn, xT=xnT, settle=True)
            routing = lambda: route(nc, core, "r3", "top2", {**const, **sub("L3_ffn_", dict(wr="gate_w"))}, xnT, gates, normal)
            lora(nc, core, "f3", sub("L3_ffn_", dict(wl="W_lin", bl="b_lin", left="left", right="right")), x, gate(7), xn, xnT, gates, routing)
        if add is not None:
            layernorm_all(nc, core, "partial", x, xn, add=add)
        with ExitStack() as c2:
            stored = core["phases"].sem("stored")
            block = core["phases"].block(c2)

            @block.sync
            def _(sp):
                sp.dma_start(y_out.rearrange("b t d -> t b d"), x[:]).then_inc(stored, 16)
                sp.wait_ge(stored, 16)


def layouts(i):
    c = np.ascontiguousarray
    a = {k: np.asarray(v) for k, v in i.items()}
    column = lambda t: c(t.reshape(-1, P).T)
    r = {"x": a["x"], "ctx": a["ctx_1024"], "g_xattn": a["g_xattn"], "g_ffn": a["g_ffn"], "mask": c(a["mask_BxS2_bf1"]).view(np.uint8)}
    r["ctxT"] = c(a["ctx_1024"].transpose(0, 2, 1).reshape(B, KD, P, CK).transpose(0, 2, 1, 3))
    w = a["L0_xattn_Wkv"]
    r["L0_xattn_Wq"], r["L0_xattn_Wo"] = a["L0_xattn_Wq"], a["L0_xattn_Wo"]
    r["L0_xattn_Wk"], r["L0_xattn_Wv"] = c(w[:, :1024]), c(w[:, 1024:])
    for n in ("q_scale", "k_scale"):
        t = a[f"L0_xattn_{n}"]
        r[f"L0_xattn_{n}"] = c(np.concatenate([t, t])[:, None])
    nk, nv = a["L0_xattn_null_kv"]
    r["L0_xattn_null_k"], r["L0_xattn_null_v"] = c(np.concatenate([nk, nk])[:, None]), c(nv[None])
    for n in ("ln_in_g", "ln_in_b"):
        r[f"L0_{n}"] = column(a[f"L0_xattn_{n}"])
    for n in ("ln_ctx_g", "ln_ctx_b"):
        r[f"L0_xattn_{n}"] = column(a[f"L0_xattn_{n}"])
    for n in ("ln_out_g", "ln_out_b"):
        r[f"L0_{n}"] = a[f"L0_xattn_{n}"]
    w, t = a["L0_ffn_in_proj_w"].T, a["L0_ffn_in_proj_b"]
    for j, n in enumerate("qkv"):
        r[f"L0_ffn_w{n}"] = c(w[:, j * D:(j + 1) * D])
        r[f"L0_ffn_b{n}"] = c(t[j * D:(j + 1) * D]) if n == "v" else column(t[j * D:(j + 1) * D])
    r["L0_ffn_wo"] = c(a["L0_ffn_out_proj_w"].T)
    for n in ("out_proj_b", "ln1_g", "ln1_b", "ln2_g", "ln2_b", "b2", "w1", "w2"):
        r[f"L0_ffn_{n}"] = a[f"L0_ffn_{n}"]
    r["L0_ffn_wr"] = c(np.concatenate([a["L0_ffn_w_group"], a["L0_ffn_w_expert"].transpose(1, 0, 2).reshape(D, 8)], 1))
    r["L0_ffn_br"] = c(np.concatenate([a["L0_ffn_b_group"], a["L0_ffn_b_expert"].reshape(8)]))
    r["L0_ffn_b1"] = c(a["L0_ffn_b1"].reshape(8, -1, P).transpose(0, 2, 1))
    for n in ("Wq", "Wk", "Wv", "Wo", "bv", "bo"):
        r[f"L1_xattn_{n}"] = a[f"L1_xattn_{n}"]
    for n in ("bq", "bk"):
        r[f"L1_xattn_{n}"] = column(a[f"L1_xattn_{n}"])
    r["L1_ffn_Wg"], r["L1_ffn_routing_bias"] = c(a["L1_ffn_Wg"].T), a["L1_ffn_routing_bias"]
    for n in ("1", "2", "3"):
        r[f"L1_ffn_W{n}"] = c(np.concatenate([a[f"L1_ffn_W{n}"], a[f"L1_ffn_Ws{n}"][None]]).transpose(0, 2, 1))
    halves = lambda t: c(t.reshape(t.shape[0], D, 2, -1).transpose(0, 2, 1, 3).reshape(2 * t.shape[0], D, -1))
    r["L1_ffn_W1"], r["L1_ffn_W2"], r["L1_ffn_W3"] = halves(r["L1_ffn_W1"]), halves(r["L1_ffn_W2"]), r["L1_ffn_W3"].reshape(18, -1, D)
    r["L2_xattn_W_out"], r["L2_xattn_b_out"] = c(a["L2_xattn_W_out"].T), a["L2_xattn_b_out"]
    for n in ("router_W", "router_b", "W1", "W2", "b2"):
        r[f"L2_ffn_{n}"] = a[f"L2_ffn_{n}"]
    r["L2_ffn_W1"], r["L2_ffn_W2"] = halves(r["L2_ffn_W1"]), r["L2_ffn_W2"].reshape(16, -1, D)
    r["L2_ffn_b1"] = c(a["L2_ffn_b1"].reshape(16, -1, P).transpose(0, 2, 1))
    w, t = a["L3_xattn_Wkv"], a["L3_xattn_bkv"]
    r["L3_xattn_Wq"], r["L3_xattn_Wk"], r["L3_xattn_Wv"] = a["L3_xattn_Wq"], c(w[:, :D]), c(w[:, D:])
    r["L3_xattn_bq"], r["L3_xattn_bk"], r["L3_xattn_bv"] = column(a["L3_xattn_bq"]), column(t[:D]), c(t[D:])
    r["L3_xattn_Wo"], r["L3_xattn_bo"] = a["L3_xattn_Wo"], a["L3_xattn_bo"]
    r["L3_ffn_W_lin"], r["L3_ffn_b_lin"], r["L3_ffn_gate_w"] = c(a["L3_ffn_W_lin"].T), a["L3_ffn_b_lin"], c(a["L3_ffn_gate_w"].T)
    r["L3_ffn_left"], r["L3_ffn_right"] = c(a["L3_ffn_left"].transpose(1, 0, 2).reshape(D, 32)), c(a["L3_ffn_right"].reshape(32, D))
    f32 = np.float32
    r["ident"] = np.eye(P, dtype=f32)
    rows = np.arange(P)
    r["same_head"] = (rows[:, None] // 64 == rows[None] // 64).astype(f32)
    r["before"] = (np.arange(8)[None] < np.arange(8)[:, None]).astype(f32)
    own = lambda hd: (rows[:, None] // hd == np.arange(P // hd)[None]).astype(f32)
    r["mask2"], r["mask_quarter"], r["mask_one"], r["mask_eighth"] = 8 * own(64), own(16) / 4, own(16), own(16) / 8
    r["mask2"], r["mask_quarter"], r["mask_eighth"] = [r[n].astype(f32) for n in ("mask2", "mask_quarter", "mask_eighth")]
    rot = np.zeros((P, P), f32)
    even = rows[::2]
    rot[even + 1, even], rot[even, even + 1] = -1.0, 1.0
    r["rot"] = rot
    inv_freq = (1.0 / 10000.0 ** (np.arange(0, 16, 2, dtype=f32) / f32(16))).astype(f32)
    for n, length in (("q", TQ), ("k", CK)):
        pos = f32(10.0) * (np.arange(length, dtype=f32) / f32(length))
        angle = pos[None] * inv_freq[(rows % 16) // 2][:, None]
        r["cos" + n], r["sin" + n] = np.cos(angle).astype(f32), np.sin(angle).astype(f32)
    return r


def kernel(**inputs):
    import concourse.bacc as bacc
    from concourse.bass_utils import run_bass_kernel_spmd

    arrays = {f"in_{n}": t for n, t in layouts(inputs).items()}
    nc = bacc.Bacc("TRN2", target_bir_lowering=False, num_devices=1)
    A = {n[3:]: nc.dram_tensor(n, t.shape, mybir.dt.from_np(t.dtype), kind="ExternalInput").ap() for n, t in arrays.items()}
    out = nc.dram_tensor("out", (B, TQ, D), FP32, kind="ExternalOutput").ap()
    network(nc, A, out)
    r = run_bass_kernel_spmd(nc, [arrays], core_ids=[0])
    return r.results[0]["out"]
```

```python
from contextlib import ExitStack

import numpy as np

import concourse.bass as bass
from concourse import mybir

FP32 = mybir.dt.float32
FP32R = mybir.dt.float32r
BF16 = mybir.dt.bfloat16
U8 = mybir.dt.uint8
ALU = mybir.AluOpType
ACT = mybir.ActivationFunctionType
AX = mybir.AxisListType

B, TQ, D = 8, 112, 256
N = B * TQ
P = 128
KD = D // P
CK, KT = 375, 125
H = 16
GROUPS = H // 2
HALF = N // 2
BANK = 512
LN_EPS = 1e-5


def bcast(ap, axis, n):
    ap = ap.unsqueeze(axis)
    shape = list(ap.shape)
    shape[axis] = n
    return ap.broadcast_to(shape)


class Chain:

    def __init__(self, engine, sem, start=0):
        self.engine, self.sem, self.start, self.k = engine, sem, start, 0

    def step(self, instruction):
        self.k += 1
        instruction.then_inc(self.sem, 1)
        self.engine.wait_ge(self.sem, self.start + self.k)


class Phases:

    def __init__(self, nc):
        self.nc, self.used, self.last, self.clearing = nc, [], [], []
        self.asked = []

    def sem(self, name):
        held = self.nc.semaphore(name)
        s = held.__enter__()
        self.used.append((held, s))
        return s

    def block(self, c):
        nc = self.nc
        for held, _ in self.clearing:
            held.__exit__(None, None, None)
        self.clearing, self.last, self.used = self.last, self.used, []
        old = list(self.clearing)
        block = c.enter_context(nc.Block())
        if old:
            @block.gpsimd
            def _(pool):
                for _, s in old:
                    pool.sem_clear(s)
        return block


    def ask(self, tag, loads, zero=()):
        self.asked += [{"tag": tag, "loads": loads, "zero": zero, "held": None}]

    def run_ahead(self, block, settle):
        nc = self.nc
        for g in reversed(self.asked):
            if g["held"] is None:
                g["held"] = [nc.semaphore(f"{g['tag']}_{n}") for n in ("landed", "cleared")]
                g["landed"], g["cleared"] = [h.__enter__() for h in g["held"]]
                if g["zero"]:
                    @block.gpsimd
                    def _(pool):
                        for t in g["zero"]:
                            nc.gpsimd.memset(t, 0.0).then_inc(g["cleared"], 1)

                @block.sync
                def _(sp):
                    if g["zero"]:
                        sp.wait_ge(g["cleared"], len(g["zero"]))
                    for to, src in g["loads"]:
                        sp.dma_start(to, src).then_inc(g["landed"], 16)
        if settle:
            g = self.asked.pop()
            self.used += [(g["held"][0], g["landed"]), (g["held"][1], g["cleared"])]

            @block.sync
            def _(sp):
                sp.wait_ge(g["landed"], 16 * len(g["loads"]))



def layernorm_all(nc, core, tag, src, dst, affine=None, update=None, xT=None, xT_affine=None,
                  add=None, settle=False):
    ps, ident = core["ps"], core["ident"]
    with ExitStack() as c:
        sb = lambda n, s: c.enter_context(nc.sbuf_tensor(f"{tag}_{n}", s, FP32))
        sem = lambda n: core["phases"].sem(f"{tag}_{n}")
        stats, mv = sb("stats", [TQ, B, 6]), sb("mv", [TQ, B, 2])
        var_eps, std, rstd = sb("var_eps", [TQ, B]), sb("std", [TQ, B]), sb("rstd", [TQ, B])
        stats_ready, mv_ready, var_ready = sem("stats_ready"), sem("mv_ready"), sem("var_ready")
        std_ready, rstd_ready, rows_normal = sem("std_ready"), sem("rstd_ready"), sem("rows_normal")
        scaled, rows_ready, updated = sem("scaled"), sem("rows_ready"), sem("updated")
        transposed, copied, added, affine_landed = sem("transposed"), sem("copied"), sem("added"), sem("affine_landed")
        if affine is not None:
            gain, offset = sb("gain", [TQ, D]), sb("offset", [TQ, D])
        block = core["phases"].block(c)

        if affine is not None:
            @block.sync
            def _(sp):
                sp.dma_start(gain[:], affine[0].partition_broadcast(TQ)).then_inc(affine_landed, 16)
                sp.dma_start(offset[:], affine[1].partition_broadcast(TQ)).then_inc(affine_landed, 16)

        @block.vector
        def _(dve):
            if add is not None:
                a, add_gate = add
                for b in range(B):
                    if add_gate is None:
                        nc.vector.tensor_tensor(src[:, b, :], src[:, b, :], a[:, b, :], ALU.add).then_inc(added, 1)
                    else:
                        nc.vector.scalar_tensor_tensor(src[:, b, :], a[:, b, :], add_gate, src[:, b, :], ALU.mult, ALU.add).then_inc(added, 1)
            for b in range(B):
                if add is not None:
                    dve.wait_ge(added, b + 1)
                nc.vector.bn_stats(stats[:, b, :], src[:, b, :]).then_inc(stats_ready, 1)
            for b in range(B):
                dve.wait_ge(stats_ready, b + 1)
                nc.vector.bn_aggr(mv[:, b, :], stats[:, b, :]).then_inc(mv_ready, 1)
            dve.wait_ge(mv_ready, B)
            nc.vector.tensor_scalar(var_eps[:], mv[:, :, 1], LN_EPS, None, ALU.add).then_inc(var_ready, 1)
            dve.wait_ge(std_ready, 1)
            nc.vector.reciprocal(rstd[:], std[:]).then_inc(rstd_ready, 1)
            dve.wait_ge(rstd_ready, 1)
            first = rows_ready if affine is None else rows_normal
            for b in range(B):
                nc.vector.tensor_scalar(dst[:, b, :], src[:, b, :], mv[:, b, 0:1], rstd[:, b:b + 1],
                                        ALU.subtract, ALU.mult).then_inc(first, 1)
            if affine is not None:
                dve.wait_ge(affine_landed, 32)
                for b in range(B):
                    dve.wait_ge(rows_normal, b + 1)
                    nc.vector.tensor_tensor(dst[:, b, :], dst[:, b, :], gain[:], ALU.mult).then_inc(scaled, 1)
                for b in range(B):
                    dve.wait_ge(scaled, b + 1)
                    nc.vector.tensor_tensor(dst[:, b, :], dst[:, b, :], offset[:], ALU.add).then_inc(rows_ready, 1)
            if update is not None:
                x, gate = update
                for b in range(B):
                    dve.wait_ge(rows_ready, b + 1)
                    nc.vector.scalar_tensor_tensor(x[:, b, :], dst[:, b, :], gate, x[:, b, :],
                                                   ALU.mult, ALU.add).then_inc(updated, 1)

        @block.scalar
        def _(act):
            act.wait_ge(var_ready, 1)
            nc.scalar.activation(std[:], var_eps[:], ACT.Sqrt).then_inc(std_ready, 1)
            if xT is not None:
                for i in range(2 * KD):
                    chunk, k = divmod(i, KD)
                    act.wait_ge(transposed, i + 1)
                    to = xT[:, k, chunk * HALF:(chunk + 1) * HALF]
                    if xT_affine is None:
                        nc.scalar.activation(to, ps[:, i, 0:HALF], ACT.Copy).then_inc(copied, 1)
                    else:
                        nc.scalar.activation(to, ps[:, i, 0:HALF], ACT.Identity, scale=xT_affine[0][:, k:k + 1],
                                             bias=xT_affine[1][:, k:k + 1]).then_inc(copied, 1)

        if xT is not None:
            @block.tensor
            def _(pe):
                for i in range(2 * KD):
                    chunk, k = divmod(i, KD)
                    pe.wait_ge(rows_ready, 4 * (chunk + 1))
                    for j in range(4):
                        last = nc.tensor.transpose(ps[:, i, j * TQ:(j + 1) * TQ],
                                                   dst[:, 4 * chunk + j, k * P:(k + 1) * P], ident[0:TQ, 0:TQ])
                    last.then_inc(transposed, 1)

        core["phases"].run_ahead(block, settle)



def attention(nc, core, tag, kind, A, x, gate, xn, xnT, before, out=None):
    ps, ident = core["ps"], core["ident"]
    cosine, self_, rope, raw, linear = [kind == k for k in ("cosine", "self", "rope", "raw", "linear")]
    hd = 64 if cosine else 16
    width = 64 if cosine else 32
    per_set = P // width
    SETS = H // per_set
    FILLS = SETS // 4
    per_half = P // hd
    inner = H * hd
    KI = inner // P
    nk = CK + 1 if cosine else TQ if self_ else CK
    tiles = [(0, TQ)] if self_ else [(t * KT, KT + (cosine and t == 2)) for t in range(3)]
    NT = len(tiles)
    split = raw or linear or rope
    wide = nk + split
    S_LAG, PV_LAG = 4, 6
    PT_BANKS, OUT_BANK, PIECE_BANKS = ((4,), 6, (5, 7)) if cosine else ((4, 5), 6, (7,))
    PTS, PBS = len(PT_BANKS), len(PIECE_BANKS)

    if cosine:
        proj = (["c0", "c1", "q0", "q1"] + [f"k{i}" for i in range(6)] + [f"v{i}" for i in range(6)]
                + ["a0", "a1"] + [f"t{i}" for i in range(8)])
        room = [s for s in range(1, 16) for _ in range(2) if (s, _) not in ((4, 0), (6, 0), (7, 0))]
        where = {4: ["R0"], 6: ["R1"], 7: ["O"]}
    else:
        proj = {"self": ["q0", "k0", "v0"], "linear": ["q0", "k0", "k1", "v0", "v1", "v2"],
                "rope": ["q0", "r0", "k0", "s0", "k1", "s1", "v0", "v1", "v2"], "raw": []}[kind]
        room = {"self": [0, 1, 8], "linear": [0, 1, 2, 8, 9, 10], "rope": [0, 1, 2, 3, 4, 5, 8, 9, 10], "raw": []}[kind]
        where = {6: ["R0"], 7: ["O"]}
    for name, s in zip(proj, room):
        where.setdefault(s, []).append(name)
    tail = ["R0", "R1", "O"] if cosine else ["R0", "O"]
    order = [name for s in range(H) for name in where.get(s, [])]
    Q, M = len(proj), len(proj) + len(tail)
    assert len(order) == M

    timelines = {-1: proj, 0: [o for o in order if o in proj], **{n: order for n in range(1, B - 1)},
                 B - 1: [o for o in order if o in tail], B: tail}

    def before_timeline(n, length):
        if isinstance(n, int):
            return sum(length(timelines[m]) for m in range(-1, n))
        return length(timelines[-1]) + length(timelines[0]) + length(order) * (n - 1)

    def in_bank(bank):
        return lambda names: len(names[bank::PBS])

    def made(name, n):
        names = timelines[n] if isinstance(n, int) else order
        return before_timeline(n, len) + names.index(name) + 2

    def place(name, n):
        turn, bank = divmod((timelines[n] if isinstance(n, int) else order).index(name), PBS)
        return bank, before_timeline(n, in_bank(bank)) + turn + 2

    with ExitStack() as c:
        def sb(name, shape):
            return c.enter_context(nc.sbuf_tensor(f"{tag}_{name}", shape, FP32))

        def sem(name):
            return core["phases"].sem(f"{tag}_{name}")

        loads, zero = [], []
        wo = sb("wo", [P, SETS, D])
        if cosine:
            loads.append((wo[:], A["wo"].rearrange("(s p) n -> p s n", p=P)))
        else:
            zero.append(wo[:])
            rows = A["wo"].rearrange("(s j r) n -> j r s n", j=per_set, r=hd)
            for j in range(per_set):
                loads.append((wo[j * width:j * width + hd, :, :], rows[j]))
        mask = sb("mask", [P, per_half])
        loads.append((mask[:], A["mask"]))
        if not raw:
            wq, wk, wv = sb("wq", [P, KD, inner]), sb("wk", [P, KD, inner]), sb("wv", [P, KD, inner])
            for w, name in ((wq, "wq"), (wk, "wk"), (wv, "wv")):
                loads.append((w[:], A[name].rearrange("(k p) n -> p k n", p=P)))
        if not raw and not cosine:
            bq, bk, bv = sb("bq", [P, KD]), sb("bk", [P, KD]), sb("bv", [KT, D])
            loads += [(bq[:], A["bq"]), (bk[:], A["bk"]), (bv[:], A["bv"].partition_broadcast(KT))]
        if not cosine:
            bo = sb("bo", [TQ, D])
            loads.append((bo[:], A["bo"].partition_broadcast(TQ)))
        if rope:
            rot, cosq, sinq = sb("rot", [P, P]), sb("cosq", [P, TQ]), sb("sinq", [P, TQ])
            cosk, sink = sb("cosk", [P, CK]), sb("sink", [P, CK])
            loads += [(rot[:], A["rot"]), (cosq[:], A["cosq"]), (sinq[:], A["sinq"]), (cosk[:], A["cosk"]), (sink[:], A["sink"])]
            allow8 = c.enter_context(nc.sbuf_tensor(f"{tag}_allow8", [1, B, CK], U8))
            hidden = c.enter_context(nc.sbuf_tensor(f"{tag}_hidden", [P, B, CK], BF16))
            one_row = c.enter_context(nc.sbuf_tensor(f"{tag}_one_row", [P, TQ], BF16))
            loads.append((allow8[:], A["allow"].rearrange("(o b) k -> o b k", o=1)))
            zero += [hidden[:], one_row[:]]
            q_raw, k_raw = sb("q_raw", [P, KD, TQ]), sb("k_raw", [P, KD, CK])
            q_cos, q_rot = sb("q_cos", [P, KD, TQ]), sb("q_rot", [P, KD, TQ])
            k_sin = sb("k_sin", [P, KD, CK])
        if cosine:
            qk_gain = sb("qk_gain", [P, 2])
            loads += [(qk_gain[:, 0:1], A["q_scale"]), (qk_gain[:, 1:2], A["k_scale"])]
            ctx_gain, ctx_offset = sb("ctx_gain", [P, KD]), sb("ctx_offset", [P, KD])
            loads += [(ctx_gain[:], A["ctx_gain"]), (ctx_offset[:], A["ctx_offset"])]
            head_mask = sb("head_mask", [P, per_half])
            cmv, crs = sb("cmv", [KT, 3 * B, 2]), sb("crs", [KT, 3 * B])
            ss, norm, inv_norm = sb("ss", [KT, 4 * H]), sb("norm", [KT, 4 * H]), sb("inv_norm", [KT, 4 * H])
            zero.append(ss[:])
        kT = [sb(f"kT{p}", [P, KI, wide]) for p in range(2)]
        if split:
            zero += [t[:, :, nk:wide] for t in kT]
        v = [sb(f"v{p}", [KT + 1 if cosine else KT, NT, inner]) for p in range(2)]
        if cosine:
            loads += [(t[KT:KT + 1, 2, :].rearrange("p (h d) -> p h d", h=H), bcast(A["null_v"], 1, H)) for t in v]
        core["phases"].ask(tag, loads, zero)
        before()
        if rope:
            mask_row(nc, core, tag, allow8, hidden, one_row, sb)
        if cosine:
            context_stats(nc, core, tag, A, cmv, crs)
            null_row(nc, core, tag, A, kT, head_mask, mask, qk_gain, hd, sb)
            cx, cn = sb("cx", [KT, 3, D]), sb("cn", [KT, 3, D])
            k_tok, sq, q_tok = sb("k_tok", [KT, 3, inner]), sb("sq", [KT, 4, BANK]), sb("q_tok", [TQ, inner])
        xs = sb("xs", [P, KD, TQ]) if (self_ or cosine) else None
        cT = kT if raw else None if self_ else [sb(f"cT{p}", [P, KD, CK]) for p in range(1 if cosine else 2)]
        if split:
            fp32r = lambda n, shape: c.enter_context(nc.sbuf_tensor(f"{tag}_{n}", shape, FP32R))
            k_high, k_low = [[fp32r(f"k_{part}{p}", [P, KD, wide]) for p in range(2)] for part in ("high", "low")]
            qm_high, qm_low = [[fp32r(f"qm_{part}{p}", [P, H, TQ]) for p in range(2)] for part in ("high", "low")]
            q_high, q_low = fp32r("q_high", [P, KD, TQ]), fp32r("q_low", [P, KD, TQ])
            q_full = q_rot if rope else sb("q_full", [P, KD, TQ])
        else:
            qm = [sb(f"qm{p}", [P, H, TQ]) for p in range(2)]
        probs = sb("probs", [TQ, 4, nk])
        probsT = sb("probsT", [KT + 1, 8, NT * TQ])
        nmax, sums, inv = sb("nmax", [TQ, 2, H]), sb("sums", [TQ, 2, H]), sb("inv", [TQ, H])
        inv_wide, heads_raw = sb("inv_wide", [TQ, H, width]), sb("heads_raw", [P, FILLS, 4 * TQ])
        headsT, part = sb("headsT", [P, FILLS, 4 * TQ]), sb("part", [TQ, D])

        scores_ready, max_ready, probs_ready = sem("scores_ready"), sem("max_ready"), sem("probs_ready")
        pT_ready, pT_copied, heads_ready, heads_copied = sem("pT_ready"), sem("pT_copied"), sem("heads_ready"), sem("heads_copied")
        piece_ready, piece_read = sem("piece_ready"), [sem(f"piece_read_{b}") for b in range(PBS)]
        inv_ready, inv_wide_ready = sem("inv_ready"), sem("inv_wide_ready")
        ctx_ready = [sem("ctx_ready_0"), sem("ctx_ready_1")]
        values_ready = [sem("values_ready_0"), sem("values_ready_1")]
        xs_ready, qm_ready, kT_ready = sem("xs_ready"), sem("qm_ready"), sem("kT_ready")
        q_high_ready, q_low_ready, k_high_ready, low_ready = [sem(n) for n in ("q_high_ready", "q_low_ready", "k_high_ready", "low_ready")]
        q_cos_ready, k_cos_ready, rot_steps = sem("q_cos_ready"), sem("k_cos_ready"), sem("rot_steps")
        cn_ready, sq_ready, summed, floored = sem("cn_ready"), sem("sq_ready"), sem("summed"), sem("floored")
        norm_ready, inv_norm_ready, scaled = sem("norm_ready"), sem("inv_norm_ready"), sem("scaled")
        block = core["phases"].block(c)

        def batches(engine, before, batch, after):
            before()
            batch(0, 0, True, False)
            with engine.Fori(0, B // 2 - 1, 1) as i:
                batch(2 * i + 1, 1, False, False)
                batch(2 * i + 2, 0, False, False)
            batch(B - 1, 1, False, True)
            after()

        def wait_read(engine, name, n):
            b, value = place(name, n)
            engine.wait_ge(piece_read[b], value)

        def pieces(slot, n, first, last):
            if slot >= H:
                yield from ((name, n, B) for name in where.get(slot - H, []) if name in tail)
                return
            for name in where.get(slot, []):
                if name in tail and not first:
                    yield name, n - 1, n
                if name in proj and not last:
                    yield name, n + 1, n

        def square_part(kind, i):
            if kind == "q":
                return i, TQ, q_tok[:, i * BANK:(i + 1) * BANK]
            t, half = divmod(i, 2)
            return 2 + i, KT, k_tok[:, t, half * BANK:(half + 1) * BANK]

        @block.sync
        def _(sp):
            for n in range(B):
                s = n % 2 if raw else 0
                if raw:
                    if n >= 2:
                        sp.wait_ge(heads_ready, SETS * (n - 1))
                    sp.dma_start(kT[s][:, :, 0:CK], A["ctxT"][n]).then_inc(ctx_ready[s], 16)
                    sp.dma_start(v[s][:], A["ctx"][n].rearrange("(t p) d -> p t d", p=KT)).then_inc(values_ready[s], 16)
                elif cosine:
                    if n:
                        sp.wait_ge(cn_ready, n)
                    sp.dma_start(cx[:], A["ctx"][n].rearrange("(t p) d -> p t d", p=KT)).then_inc(ctx_ready[0], 16)
                elif not self_:
                    if n >= 2:
                        sp.wait_ge(piece_ready, made("v2", n - 3))
                    sp.dma_start(cT[n % 2][:], A["ctxT"][n]).then_inc(ctx_ready[n % 2], 16)

        @block.gpsimd
        def _(pool):
            for n in range(B):
                if self_ or cosine:
                    if n:
                        pool.wait_ge(piece_ready, made("v0" if self_ else "q1", n - 2))
                    pool.tensor_copy(xs[:], xnT[:, :, n * TQ:(n + 1) * TQ]).then_inc(xs_ready, 1)
                    continue
                if rope:
                    wait_read(pool, "q0", n - 1)
                    if n:
                        pool.wait_ge(rot_steps, n)
                    pool.tensor_tensor(q_cos[:], q_raw[:], bcast(cosq[:], 1, KD), ALU.mult).then_inc(q_cos_ready, 1)
                    if n >= 2:
                        pool.wait_ge(scores_ready, H * (n - 1))
                    for k in range(KD):
                        wait_read(pool, f"k{k}", n - 1)
                        pool.tensor_tensor(kT[n % 2][:, k, 0:nk], k_raw[:, k, :], cosk[:], ALU.mult).then_inc(k_cos_ready, 1)
                pool.wait_ge(q_low_ready, n + 1)
                for half in range(KD):
                    heads = slice(half * per_half, (half + 1) * per_half)
                    pool.tensor_tensor(qm_low[n % 2][:, heads, :], bcast(q_low[:, half, :].bitcast(FP32), 1, per_half),
                                       bcast(mask[:], 2, TQ), ALU.mult).then_inc(low_ready, 1)
                if raw:
                    pool.wait_ge(ctx_ready[n % 2], 16 * (n // 2) + 16)
                for k in range(KD):
                    if linear:
                        wait_read(pool, f"k{k}", n - 1)
                    elif rope:
                        pool.wait_ge(kT_ready, KD * n + k + 1)
                    pool.tensor_copy(k_high[n % 2][:, k, :], kT[n % 2][:, k, :]).then_inc(k_high_ready, 1)
                    pool.wait_ge(k_high_ready, KD * n + k + 1)
                    pool.tensor_tensor(k_low[n % 2][:, k, :], kT[n % 2][:, k, :], k_high[n % 2][:, k, :].bitcast(FP32),
                                       ALU.subtract).then_inc(low_ready, 1)

        @block.tensor
        def _(pe):
            def piece(name, m, line, p):
                b, value = place(name, line)
                bank = ps[:, PIECE_BANKS[b], :]
                pe.wait_ge(piece_read[b], value - 1)
                kind, i = name[0], int(name[1:] or 0)
                if kind == "R":
                    if i == 0:
                        pe.wait_ge(inv_wide_ready, m + 1)
                    for j in range(4):
                        s = 4 * i + j
                        last = nc.tensor.transpose(bank[:, j * TQ:(j + 1) * TQ],
                                                   inv_wide[:, s * per_set:(s + 1) * per_set, :].rearrange("p h w -> p (h w)"),
                                                   ident[0:TQ, 0:TQ])
                elif kind == "O":
                    wait_read(pe, tail[-2], line)
                    for s in range(SETS):
                        last = nc.tensor.matmul(bank[0:TQ, 0:D], headsT[:, s // 4, (s % 4) * TQ:(s % 4 + 1) * TQ], wo[:, s, :],
                                                start=s == 0, stop=s == SETS - 1)
                elif cosine and kind == "c":
                    pe.wait_ge(cn_ready, m + 1)
                    for t in range(3):
                        last = nc.tensor.transpose(bank[:, t * KT:(t + 1) * KT], cn[:, t, i * P:(i + 1) * P], ident[0:KT, 0:KT])
                elif cosine and kind in "qkv":
                    if name in ("k0", "v0"):
                        wait_read(pe, "c1", line)
                    if kind == "q":
                        pe.wait_ge(xs_ready, m + 1)
                    t, half = (0, i) if kind == "q" else divmod(i, 2)
                    w = {"q": wq, "k": wk, "v": wv}[kind]
                    rows = TQ if kind == "q" else KT
                    for k in range(KD):
                        lhsT = xs[:, k, :] if kind == "q" else cT[0][:, k, t * KT:(t + 1) * KT]
                        last = nc.tensor.matmul(bank[0:rows, :], lhsT, w[:, k, half * BANK:(half + 1) * BANK],
                                                start=k == 0, stop=k == KD - 1)
                elif kind == "a":
                    pe.wait_ge(scaled, 4 * m + 1)
                    for j in range(4):
                        at = (4 * i + j) * P
                        last = nc.tensor.transpose(bank[:, j * TQ:(j + 1) * TQ], q_tok[:, at:at + P], ident[0:TQ, 0:TQ])
                elif kind == "t":
                    pe.wait_ge(scaled, 4 * m + 4)
                    for t in range(3):
                        last = nc.tensor.transpose(bank[:, t * KT:(t + 1) * KT], k_tok[:, t, i * P:(i + 1) * P], ident[0:KT, 0:KT])
                elif kind == "q":
                    if self_:
                        pe.wait_ge(xs_ready, m + 1)
                    for half in range(KD):
                        for k in range(KD):
                            last = nc.tensor.matmul(bank[:, half * TQ:(half + 1) * TQ], wq[:, k, half * P:(half + 1) * P],
                                                    xs[:, k, :] if self_ else xnT[:, k, bass.ds(m * TQ, TQ)],
                                                    start=k == 0, stop=k == KD - 1)
                elif kind == "k" and self_:
                    for half in range(KD):
                        for k in range(KD):
                            last = nc.tensor.matmul(bank[:, half * TQ:(half + 1) * TQ], wk[:, k, half * P:(half + 1) * P],
                                                    xs[:, k, :], start=k == 0, stop=k == KD - 1)
                elif kind == "k":
                    if i == 0:
                        pe.wait_ge(ctx_ready[1 - p], 8 * m + (8 if 1 - p else 16))
                    for k in range(KD):
                        last = nc.tensor.matmul(bank[:, 0:nk], wk[:, k, i * P:(i + 1) * P], cT[1 - p][:, k, :], start=k == 0, stop=k == KD - 1)
                elif kind == "v":
                    at, kt = tiles[i]
                    for k in range(KD):
                        last = nc.tensor.matmul(bank[0:kt, 0:D], (xs if self_ else cT[1 - p])[:, k, at:at + kt], wv[:, k, :],
                                                start=k == 0, stop=k == KD - 1)
                elif kind == "r":
                    wait_read(pe, f"q{i}", line)
                    for half in range(KD):
                        last = nc.tensor.matmul(bank[:, half * TQ:(half + 1) * TQ], rot[:], q_raw[:, half, :], start=True, stop=True)
                elif kind == "s":
                    wait_read(pe, f"k{i}", line)
                    last = nc.tensor.matmul(bank[:, 0:nk], rot[:], k_raw[:, i, :], start=True, stop=True)
                last.then_inc(piece_ready, 1)

            def transposes(a, k):
                pe.wait_ge(probs_ready, a + 1)
                if not (isinstance(a, int) and a < PTS):
                    pe.wait_ge(pT_copied, a + 1 - PTS)
                for t, (at, kt) in enumerate(tiles):
                    last = nc.tensor.transpose(ps[0:kt, PT_BANKS[k % PTS], t * TQ:(t + 1) * TQ], probs[:, k % 4, at:at + kt],
                                               ident[0:TQ, 0:TQ])
                last.then_inc(pT_ready, 1)

            def outputs(m, k, p):
                if (k + 1) % per_set:
                    return
                s = k // per_set
                pe.wait_ge(pT_copied, H * m + k + 1)
                if s == 0 and raw:
                    pe.wait_ge(values_ready[p], 8 * m + (8 if p else 16))
                if s % 4 == 0 and not (isinstance(m, int) and m == 0 and s == 0):
                    pe.wait_ge(heads_copied, FILLS * m + s // 4)
                for t, (at, kt) in enumerate(tiles):
                    for j in range(per_set):
                        h = s * per_set + j
                        last = nc.tensor.matmul(ps[j * width:j * width + hd, OUT_BANK, (s % 4) * TQ:(s % 4 + 1) * TQ],
                                                v[p][0:kt, t, h * hd:(h + 1) * hd], probsT[0:kt, h % 8, t * TQ:(t + 1) * TQ],
                                                start=t == 0, stop=t == NT - 1)
                last.then_inc(heads_ready, 1)

            def scores(n, k, p):
                a = H * n + k
                if k == 0:
                    if Q:
                        for b in range(PBS):
                            pe.wait_ge(piece_read[b], before_timeline(n, in_bank(b)) + 1)
                    if raw:
                        pe.wait_ge(ctx_ready[p], 8 * n + (8 if p else 16))
                    if split:
                        pe.wait_ge(qm_ready, 2 * n + 2)
                        pe.wait_ge(low_ready, 4 * n + 4)
                if not (isinstance(a, int) and a < 4):
                    pe.wait_ge(probs_ready, a - 3)
                if split:
                    q, keys = (qm_high[p][:, k, :], qm_low[p][:, k, :]), (k_high[p][:, k // per_half, :], k_low[p][:, k // per_half, :])
                    nc.tensor.matmul(ps[0:TQ, k % 4, 0:wide], q[0], keys[0], start=True, stop=False)
                    nc.tensor.matmul(ps[0:TQ, k % 4, 0:wide], q[0], keys[1], start=False, stop=False)
                    last = nc.tensor.matmul(ps[0:TQ, k % 4, 0:wide], q[1], keys[0], start=False, stop=not rope)
                else:
                    last = nc.tensor.matmul(ps[0:TQ, k % 4, 0:nk], qm[p][:, k, :], kT[p][:, k // per_half, :], start=True, stop=True)
                if rope:
                    last = nc.tensor.matmul(ps[0:TQ, k % 4, 0:nk], one_row[:], hidden[:, n, :], start=False, stop=True)
                last.then_inc(scores_ready, 1)

            def first_projections():
                pe.sem_inc(piece_ready, 1)
                for read in piece_read:
                    pe.sem_inc(read, 1)
                for name in proj:
                    piece(name, 0, -1, 1)

            def slot(n, k, p, first, last):
                if k < H:
                    scores(n, k, p)
                todo = list(pieces(k, n, first, last))
                for name, m, line in todo[:1]:
                    piece(name, m, line, p)
                if k >= S_LAG or not first:
                    transposes_at = k - S_LAG
                    if transposes_at < H:
                        transposes(H * n + transposes_at, transposes_at % H)
                for name, m, line in todo[1:]:
                    piece(name, m, line, p)
                if k >= PV_LAG:
                    if k - PV_LAG < H:
                        outputs(n, k - PV_LAG, p)
                elif not first:
                    outputs(n - 1, k - PV_LAG + H, 1 - p)

            def batch(n, p, first, last):
                for k in range(H):
                    slot(n, k, p, first, last)

            def after():
                for k in range(H, H + 8):
                    slot(B - 1, k, 1, False, True)

            batches(pe, first_projections, batch, after)

        @block.scalar
        def _(act):
            def piece(name, m, line, p):
                kind, i = name[0], int(name[1:] or 0)
                b, value = place(name, line)
                bank = ps[:, PIECE_BANKS[b], :]
                read = lambda ins: ins.then_inc(piece_read[b], 1)
                if cosine and kind in "qk":
                    j, rows, tokens = square_part(kind, i)
                    act.wait_ge(piece_read[b], value)
                    if j >= 4 or not (isinstance(m, int) and m == 0):
                        act.wait_ge(summed, 8 * m + j - 3)
                    nc.scalar.activation(sq[0:rows, j % 4, :], tokens, ACT.Square).then_inc(sq_ready, 1)
                    return
                if kind in "RO" or kind in "ra" or (not cosine and (kind == "v" or kind == "s" or (kind == "q" and not rope))):
                    return
                if cosine and kind == "a":
                    return
                act.wait_ge(piece_ready, made(name, line))
                if kind == "c":
                    read(nc.scalar.activation(cT[0][:, i, :], bank[:, 0:CK], ACT.Identity, scale=ctx_gain[:, i:i + 1],
                                              bias=ctx_offset[:, i:i + 1]))
                elif cosine and kind == "v":
                    t, half = divmod(i, 2)
                    read(nc.scalar.activation(v[p][0:KT, t, half * BANK:(half + 1) * BANK], bank[0:KT, :], ACT.Copy))
                elif kind == "t":
                    read(nc.scalar.activation(kT[p][:, i, 0:CK], bank[:, 0:CK], ACT.Copy))
                elif kind == "q":
                    if not (isinstance(m, int) and m == 0):
                        act.wait_ge(q_cos_ready, m)
                    for half in range(KD):
                        last = nc.scalar.activation(q_raw[:, half, :], bank[:, half * TQ:(half + 1) * TQ], ACT.Identity,
                                                    bias=bq[:, half:half + 1])
                    read(last)
                elif kind == "k" and self_:
                    for half in range(KD):
                        last = nc.scalar.activation(kT[p][:, half, :], bank[:, half * TQ:(half + 1) * TQ], ACT.Identity,
                                                    bias=bk[:, half:half + 1])
                    read(last)
                elif kind == "k":
                    if rope and not (isinstance(m, int) and m == 0):
                        act.wait_ge(k_cos_ready, KD * m)
                    to = k_raw if rope else kT[p]
                    read(nc.scalar.activation(to[:, i, 0:nk], bank[:, 0:nk], ACT.Identity, bias=bk[:, i:i + 1]))

            def exp(m, k, p):
                a = H * m + k
                act.wait_ge(max_ready, GROUPS * m + k // 2 + 1)
                if not (isinstance(a, int) and a < 4):
                    act.wait_ge(pT_ready, a - 3)
                nc.scalar.activation(probs[:, k % 4, :], ps[0:TQ, k % 4, 0:nk], ACT.Exp, bias=nmax[:, p, k:k + 1],
                                     accum_out=sums[:, p, k:k + 1]).then_inc(probs_ready, 1)

            def roots(m):
                act.wait_ge(floored, m + 1)
                nc.scalar.activation(norm[:], ss[:], ACT.Sqrt).then_inc(norm_ready, 1)

            def copy_heads(m, fill):
                act.wait_ge(heads_ready, SETS * m + 4 * (fill + 1))
                if not (isinstance(m, int) and m == 0):
                    wait_read(act, f"R{fill}", m)
                nc.scalar.activation(heads_raw[:, fill, :], ps[:, OUT_BANK, 0:4 * TQ], ACT.Copy).then_inc(heads_copied, 1)

            def first_projections():
                for name in proj:
                    piece(name, 0, -1, 0)
                    if name == "k5":
                        roots(0)

            def slot(n, k, p, first, last):
                todo = list(pieces(k, n, first, last)) if k < H else []
                for name, m, line in todo[:1]:
                    piece(name, m, line, 1 - p)
                    if name == "k5":
                        roots(m)
                if 1 <= k <= H:
                    exp(n, k - 1, p)
                elif k == 0 and not first:
                    exp(n - 1, H - 1, 1 - p)
                for name, m, line in todo[1:]:
                    piece(name, m, line, 1 - p)
                    if name == "k5":
                        roots(m)
                done = k - PV_LAG
                if done < 0:
                    if not first and (done + H + 1) % (4 * per_set) == 0:
                        copy_heads(n - 1, (done + H) // (4 * per_set))
                elif done < H and (done + 1) % (4 * per_set) == 0:
                    copy_heads(n, done // (4 * per_set))

            def batch(n, p, first, last):
                for k in range(H):
                    slot(n, k, p, first, last)

            def after():
                for k in range(H, H + 8):
                    slot(B - 1, k, 1, False, True)

            batches(act, first_projections, batch, after)

        @block.vector
        def _(dve):
            def piece(name, m, line, p):
                kind, i = name[0], int(name[1:] or 0)
                b, value = place(name, line)
                bank = ps[:, PIECE_BANKS[b], :]
                read = lambda ins: ins.then_inc(piece_read[b], 1)
                if kind == "R":
                    dve.wait_ge(piece_ready, made(name, line))
                    dve.wait_ge(heads_copied, FILLS * m + i + 1)
                    read(nc.vector.tensor_tensor(headsT[:, i, :], bank[:, 0:4 * TQ], heads_raw[:, i, :], ALU.mult))
                elif kind == "O":
                    dve.wait_ge(piece_ready, made(name, line))
                    at = out[:, m, :] if cosine else part[:]
                    if cosine:
                        read(nc.vector.tensor_copy(at, bank[0:TQ, 0:D]))
                    else:
                        read(nc.vector.tensor_tensor(at, bank[0:TQ, 0:D], bo[:], ALU.add))
                        dve.wait_ge(piece_read[b], value)
                        if self_:
                            nc.vector.tensor_tensor(out[:, m, :], part[:], xn[:, m, :], ALU.add)
                        else:
                            nc.vector.scalar_tensor_tensor(x[:, m, :], part[:], gate, x[:, m, :], ALU.mult, ALU.add)
                elif cosine and kind in "qk":
                    j, rows, tokens = square_part(kind, i)
                    dve.wait_ge(piece_ready, made(name, line))
                    read(nc.vector.tensor_copy(tokens, bank[0:rows, :]))
                    for earlier in ([j - 2] if 2 <= j < 7 else [5, 6, 7] if j == 7 else []):
                        dve.wait_ge(sq_ready, 8 * m + earlier + 1)
                        rows, at = (TQ, earlier * 8) if earlier < 2 else (KT, H + (earlier - 2) * 8)
                        nc.vector.tensor_reduce(ss[0:rows, at:at + 8], sq[0:rows, earlier % 4, :].rearrange("p (h d) -> p h d", d=hd),
                                                AX.X, ALU.add).then_inc(summed, 1)
                    if name == "k5":
                        dve.wait_ge(summed, 8 * m + 8)
                        nc.vector.tensor_scalar(ss[:], ss[:], 1e-24, None, ALU.max).then_inc(floored, 1)
                elif cosine and kind == "v":
                    if i == 0:
                        dve.wait_ge(norm_ready, m + 1)
                        nc.vector.reciprocal(inv_norm[:], norm[:]).then_inc(inv_norm_ready, 1)
                        dve.wait_ge(inv_norm_ready, m + 1)
                        rows = q_tok[:].rearrange("p (h d) -> p h d", d=hd)
                        nc.vector.tensor_tensor(rows, rows, bcast(inv_norm[0:TQ, 0:H], 2, hd), ALU.mult).then_inc(scaled, 1)
                    elif i < 4:
                        rows = k_tok[:, i - 1, :].rearrange("p (h d) -> p h d", d=hd)
                        nc.vector.tensor_tensor(rows, rows, bcast(inv_norm[:, i * H:(i + 1) * H], 2, hd), ALU.mult).then_inc(scaled, 1)
                elif kind == "a":
                    dve.wait_ge(piece_ready, made(name, line))
                    read(nc.vector.tensor_tensor(qm[p][:, 8 * i:8 * i + 8, :].rearrange("p (i j) q -> p i j q", j=2),
                                                 bcast(bank[:, 0:4 * TQ].rearrange("p (i q) -> p i q", q=TQ), 2, 2),
                                                 bcast(bcast(head_mask[:], 1, 4), 3, TQ), ALU.mult))
                elif kind == "q" and not rope and not cosine:
                    dve.wait_ge(piece_ready, made(name, line))
                    if split:
                        for half in range(KD):
                            last = nc.vector.tensor_scalar(q_full[:, half, :], bank[:, half * TQ:(half + 1) * TQ],
                                                           bq[:, half:half + 1], None, ALU.add)
                        read(last)
                        dve.wait_ge(piece_read[b], value)
                        split_queries(q_full[:], m, p)
                        return
                    for half in range(KD):
                        last = nc.vector.scalar_tensor_tensor(qm[p][:, half * per_half:(half + 1) * per_half, :],
                                                              bcast(bank[:, half * TQ:(half + 1) * TQ], 1, per_half), bq[:, half:half + 1],
                                                              bcast(mask[:], 2, TQ), ALU.add, ALU.mult)
                    read(last)
                elif kind == "v" and not cosine:
                    kt = tiles[i][1]
                    dve.wait_ge(piece_ready, made(name, line))
                    if i == 0 and not (isinstance(m, int) and m < 2):
                        dve.wait_ge(heads_ready, SETS * (m - 1))
                    read(nc.vector.tensor_tensor(v[p][0:kt, i, :], bank[0:kt, 0:D], bv[0:kt, :], ALU.add))
                elif kind == "r":
                    dve.wait_ge(piece_ready, made(name, line))
                    read(nc.vector.tensor_tensor(q_rot[:], bank[:, 0:KD * TQ].rearrange("p (k q) -> p k q", k=KD),
                                                 bcast(sinq[:], 1, KD), ALU.mult))
                    dve.wait_ge(piece_read[b], value)
                    dve.wait_ge(q_cos_ready, m + 1)
                    nc.vector.tensor_tensor(q_rot[:], q_rot[:], q_cos[:], ALU.add).then_inc(rot_steps, 1)
                    dve.wait_ge(rot_steps, m + 1)
                    split_queries(q_rot[:], m, p)
                elif kind == "s":
                    dve.wait_ge(piece_ready, made(name, line))
                    read(nc.vector.tensor_tensor(k_sin[:, i, :], bank[:, 0:nk], sink[:], ALU.mult))
                    dve.wait_ge(piece_read[b], value)
                    dve.wait_ge(k_cos_ready, KD * m + i + 1)
                    nc.vector.tensor_tensor(kT[p][:, i, 0:nk], kT[p][:, i, 0:nk], k_sin[:, i, :], ALU.add).then_inc(kT_ready, 1)

            def normalise_context(m):
                dve.wait_ge(ctx_ready[0], 16 * m + 16)
                for t in range(3):
                    r = 3 * m + t
                    last = nc.vector.tensor_scalar(cn[:, t, :], cx[:, t, :], cmv[:, bass.ds(r, 1), 0], crs[:, bass.ds(r, 1)],
                                                   ALU.subtract, ALU.mult)
                last.then_inc(cn_ready, 1)

            def split_queries(q, m, p):
                nc.vector.tensor_copy(q_high[:], q).then_inc(q_high_ready, 1)
                dve.wait_ge(q_high_ready, m + 1)
                nc.vector.tensor_tensor(q_low[:], q, q_high[:].bitcast(FP32), ALU.subtract).then_inc(q_low_ready, 1)
                for half in range(KD):
                    nc.vector.tensor_tensor(qm_high[p][:, half * per_half:(half + 1) * per_half, :],
                                            bcast(q_high[:, half, :].bitcast(FP32), 1, per_half),
                                            bcast(mask[:], 2, TQ), ALU.mult).then_inc(qm_ready, 1)

            def inverse_sums(m, p):
                dve.wait_ge(probs_ready, H * m + H)
                nc.vector.reciprocal(inv[:], sums[:, p, :]).then_inc(inv_ready, 1)
                dve.wait_ge(inv_ready, m + 1)
                nc.vector.tensor_copy(inv_wide[:], bcast(inv[:], 2, width)).then_inc(inv_wide_ready, 1)

            def copy_pT(m, k):
                dve.wait_ge(pT_ready, H * m + k + 1)
                if not (isinstance(m, int) and m == 0 and k < 8):
                    dve.wait_ge(heads_ready, SETS * m + (k - 8) // per_set + 1)
                rows = tiles[-1][1]
                nc.vector.tensor_copy(probsT[0:rows, k % 8, :], ps[0:rows, PT_BANKS[k % PTS], 0:NT * TQ]).then_inc(pT_copied, 1)

            def first_projections():
                if cosine:
                    normalise_context(0)
                if raw:
                    split_queries(xnT[:, :, 0:TQ], 0, 0)
                for name in proj:
                    piece(name, 0, -1, 0)

            def slot(n, k, p, first, last):
                if k == 0 and cosine and not last:
                    normalise_context(n + 1)
                if k < H and k % 2:
                    dve.wait_ge(scores_ready, H * n + k + 1)
                    nc.vector.tensor_reduce(nmax[:, p, k - 1:k + 1], ps[0:TQ, (k - 1) % 4:(k - 1) % 4 + 2, 0:nk], AX.X, ALU.max,
                                            negate=True).then_inc(max_ready, 1)
                todo = list(pieces(k, n, first, last))
                for name, m, line in todo[:1]:
                    piece(name, m, line, 1 - p)
                if k >= S_LAG or not first:
                    if k - S_LAG < H:
                        copy_pT(n if k >= S_LAG else n - 1, (k - S_LAG) % H)
                for name, m, line in todo[1:]:
                    piece(name, m, line, 1 - p)
                if k == 2 and not first:
                    inverse_sums(n - 1, 1 - p)
                if k == H + 2:
                    inverse_sums(n, p)
                if k == 8 and raw and not last:
                    split_queries(xnT[:, :, bass.ds((n + 1) * TQ, TQ)], n + 1, 1 - p)

            def batch(n, p, first, last):
                for k in range(H):
                    slot(n, k, p, first, last)

            def after():
                for k in range(H, H + 8):
                    slot(B - 1, k, 1, False, True)

            batches(dve, first_projections, batch, after)


def mask_row(nc, core, tag, allow8, hidden, one_row, sb):
    allow = sb("allow", [1, B, CK])
    with ExitStack() as c:
        steps = core["phases"].sem(f"{tag}_mask_steps")
        block = core["phases"].block(c)

        @block.vector
        def _(dve):
            chain = Chain(dve, steps)
            chain.step(nc.vector.tensor_copy(allow[:], allow8[:]))
            chain.step(nc.vector.tensor_scalar(hidden[0:1, :, :], allow[:], 1.0, 3e38, ALU.subtract, ALU.mult))
            chain.step(nc.vector.memset(one_row[0:1, :], 1.0))


def context_stats(nc, core, tag, A, cmv, crs):
    R = 3 * B
    with ExitStack() as c:
        sb = lambda n, s: c.enter_context(nc.sbuf_tensor(f"{tag}_{n}", s, FP32))
        sem = lambda n: core["phases"].sem(f"{tag}_c_{n}")
        rows, stats, var_eps, std = sb("rows", [KT, R, D]), sb("rstats", [KT, R, 6]), sb("var_eps", [KT, R]), sb("rstd", [KT, R])
        landed = [sem(f"landed_{q}") for q in range(4)]
        stats_ready, mv_ready, var_ready, std_ready, inv_ready = [sem(n) for n in ("stats", "mv", "var", "std", "inv")]
        block = core["phases"].block(c)

        @block.sync
        def _(sp):
            for q in range(4):
                sp.dma_start(rows[:, 6 * q:6 * q + 6, :],
                             A["ctx"][2 * q:2 * q + 2].rearrange("b (t p) d -> p (b t) d", p=KT)).then_inc(landed[q], 16)

        @block.vector
        def _(dve):
            for r in range(R):
                if r % 6 == 0:
                    dve.wait_ge(landed[r // 6], 16)
                nc.vector.bn_stats(stats[:, r, :], rows[:, r, :]).then_inc(stats_ready, 1)
            for r in range(R):
                dve.wait_ge(stats_ready, r + 1)
                nc.vector.bn_aggr(cmv[:, r, :], stats[:, r, :]).then_inc(mv_ready, 1)
            dve.wait_ge(mv_ready, R)
            nc.vector.tensor_scalar(var_eps[:], cmv[:, :, 1], LN_EPS, None, ALU.add).then_inc(var_ready, 1)
            dve.wait_ge(std_ready, 1)
            nc.vector.reciprocal(crs[:], std[:]).then_inc(inv_ready, 1)
            dve.wait_ge(inv_ready, 1)

        @block.scalar
        def _(act):
            act.wait_ge(var_ready, 1)
            nc.scalar.activation(std[:], var_eps[:], ACT.Sqrt).then_inc(std_ready, 1)


def null_row(nc, core, tag, A, kT, head_mask, mask, qk_gain, hd, sb):
    ps = core["ps"]
    nk_col, sq_col, both, tmp = sb("null_col", [P, 1]), sb("null_sq", [P, 1]), sb("same_head", [P, P]), sb("null_norm", [P, 4])
    with ExitStack() as c:
        sem = lambda n: core["phases"].sem(f"{tag}_n_{n}")
        landed, dve_steps, norm_ready, root = sem("landed"), sem("steps"), sem("norm_ready"), sem("root")
        block = core["phases"].block(c)

        @block.sync
        def _(sp):
            sp.dma_start(nk_col[:], A["null_k"]).then_inc(landed, 16)
            sp.dma_start(both[:], A["same_head"]).then_inc(landed, 16)
            sp.wait_ge(landed, 32)

        @block.vector
        def _(dve):
            chain = Chain(dve, dve_steps)
            dve.wait_ge(landed, 32)
            chain.step(nc.vector.tensor_tensor(sq_col[:], nk_col[:], nk_col[:], ALU.mult))
            dve.wait_ge(norm_ready, 1)
            chain.step(nc.vector.tensor_scalar(tmp[:, 0:1], ps[:, 0, 0:1], 1e-24, None, ALU.max))
            dve.wait_ge(root, 1)
            chain.step(nc.vector.reciprocal(tmp[:, 2:3], tmp[:, 1:2]))
            chain.step(nc.vector.tensor_tensor(tmp[:, 3:4], nk_col[:], tmp[:, 2:3], ALU.mult))
            for keys in kT:
                chain.step(nc.vector.tensor_copy(keys[:, :, CK:CK + 1], bcast(tmp[:, 3:4], 1, keys.shape[1])))
            chain.step(nc.vector.tensor_scalar(head_mask[:], mask[:], qk_gain[:, 0:1], qk_gain[:, 1:2], ALU.mult, ALU.mult))

        core["phases"].run_ahead(block, True)

        @block.tensor
        def _(pe):
            pe.wait_ge(dve_steps, 1)
            nc.tensor.matmul(ps[:, 0, 0:1], both[:], sq_col[:], start=True, stop=True).then_inc(norm_ready, 1)

        @block.scalar
        def _(act):
            act.wait_ge(dve_steps, 2)
            nc.scalar.activation(tmp[:, 1:2], tmp[:, 0:1], ACT.Sqrt).then_inc(root, 1)



def ranks(nc, chain, logits, before, E, greater, equal, rank):
    over_j, over_e = bcast(logits, 2, E), bcast(logits, 3, E)
    chain.step(nc.vector.tensor_tensor(greater, over_j, over_e, ALU.is_gt))
    chain.step(nc.vector.tensor_tensor(equal, over_j, over_e, ALU.is_equal))
    chain.step(nc.vector.tensor_tensor(equal, equal, bcast(before, 1, B), ALU.mult))
    chain.step(nc.vector.tensor_tensor(greater, greater, equal, ALU.add))
    chain.step(nc.vector.tensor_reduce(rank, greater, AX.X, ALU.add))


def route(nc, core, tag, kind, A, xT, gates, before_it, y=None):
    ps, ident = core["ps"], core["ident"]
    G, E = 4, 8
    cols = G + E if kind == "hier" else E
    b2_in = kind in ("hier", "top1")
    with ExitStack() as c:
        sb = lambda n, s: c.enter_context(nc.sbuf_tensor(f"{tag}_{n}", s, FP32))
        sem = lambda n: core["phases"].sem(f"{tag}_{n}")
        wr, bias, before = sb("wr", [P, KD, cols]), sb("bias", [TQ, cols]), sb("before", [TQ, E, E])
        logits = sb("logits", [TQ, B, cols])
        greater, equal = sb("greater", [TQ, B, E, E]), sb("equal", [TQ, B, E, E])
        rank, top, picked = sb("rank", [TQ, B, E]), sb("top", [TQ, B]), sb("picked", [TQ, B, E])
        shifted, exps = sb("shifted", [TQ, B, E]), sb("exps", [TQ, B, E])
        total, inv = sb("total", [TQ, B]), sb("inv", [TQ, B])
        loads = [(wr[:], A["wr"].rearrange("(k p) n -> p k n", p=P)), (before[:], A["before"].partition_broadcast(TQ))]
        if "br" in A:
            loads.append((bias[:], A["br"].partition_broadcast(TQ)))
        if b2_in:
            b2, gatesT = sb("b2", [E, D]), sb("gatesT", [E, N])
            loads.append((b2[:], A["b2"]))
        if kind == "hier":
            etop, eshift, eexp = sb("etop", [TQ, B, G]), sb("eshift", [TQ, B, G, 2]), sb("eexp", [TQ, B, G, 2])
            etotal, einv, epick = sb("etotal", [TQ, B, G]), sb("einv", [TQ, B, G]), sb("epick", [TQ, B, G, 2])
        core["phases"].ask(tag, loads)
        before_it()
        logits_ready, steps, exp_asked, exp_ready = sem("logits_ready"), sem("steps"), sem("exp_asked"), sem("exp_ready")
        gates_ready, gatesT_ready, gatesT_copied = sem("gates_ready"), sem("gatesT_ready"), sem("gatesT_copied")
        y_ready, y_copied = sem("y_ready"), sem("y_copied")
        block = core["phases"].block(c)
        core["phases"].run_ahead(block, True)

        @block.tensor
        def _(pe):
            for b in range(B):
                for k in range(KD):
                    last = nc.tensor.matmul(ps[0:TQ, 0, b * cols:(b + 1) * cols], xT[:, k, b * TQ:(b + 1) * TQ],
                                            wr[:, k, :], start=k == 0, stop=k == KD - 1)
            last.then_inc(logits_ready, 1)
            if b2_in:
                pe.wait_ge(gates_ready, 1)
                for b in range(B):
                    last = nc.tensor.transpose(ps[0:E, 1 + b // 4, (b % 4) * TQ:(b % 4 + 1) * TQ], gates[:, b, 0:E],
                                               ident[0:TQ, 0:TQ])
                last.then_inc(gatesT_ready, 1)
                pe.wait_ge(gatesT_copied, 2)
                for b in range(B):
                    if b >= 4:
                        pe.wait_ge(y_copied, b - 3)
                    nc.tensor.matmul(ps[0:TQ, 4 + b % 4, 0:D], gatesT[:, b * TQ:(b + 1) * TQ], b2[:],
                                     start=True, stop=True).then_inc(y_ready, 1)

        @block.scalar
        def _(act):
            act.wait_ge(exp_asked, 1)
            nc.scalar.activation(exps[:, :, 0:G if kind == "hier" else E], shifted[:, :, 0:G if kind == "hier" else E],
                                 ACT.Exp).then_inc(exp_ready, 1)
            if kind == "hier":
                nc.scalar.activation(eexp[:], eshift[:], ACT.Exp).then_inc(exp_ready, 1)

        @block.vector
        def _(dve):
            chain = Chain(dve, steps)
            v = nc.vector
            dve.wait_ge(logits_ready, 1)
            from_pe = ps[0:TQ, 0, 0:B * cols].rearrange("p (b e) -> p b e", e=cols)
            if "br" in A:
                chain.step(v.tensor_tensor(logits[:], from_pe, bcast(bias[:], 1, B), ALU.add))
            else:
                chain.step(v.tensor_copy(logits[:], from_pe))
            choose = G if kind == "hier" else E
            lg = logits[:, :, 0:choose]
            chain.step(v.tensor_reduce(top[:], lg, AX.X, ALU.max))
            sh = shifted[:, :, 0:choose]
            if kind == "hier":
                el = logits[:, :, G:].rearrange("p b (g e) -> p b g e", e=2)
                chain.step(v.tensor_reduce(etop[:], el, AX.X, ALU.max))
                chain.step(v.tensor_tensor(eshift[:], el, bcast(etop[:], 3, 2), ALU.subtract))
            v.tensor_tensor(sh, lg, bcast(top[:], 2, choose), ALU.subtract).then_inc(exp_asked, 1)
            ranks(nc, chain, lg, before[:, 0:choose, 0:choose], choose, greater[:, :, 0:choose, 0:choose],
                  equal[:, :, 0:choose, 0:choose], rank[:, :, 0:choose])
            k = {"hier": 1, "top1": 1, "top4": 4, "top2": 2}[kind]
            chain.step(v.tensor_scalar(picked[:, :, 0:choose], rank[:, :, 0:choose], k - 0.5, None, ALU.is_lt))
            dve.wait_ge(exp_ready, 2 if kind == "hier" else 1)
            ex = exps[:, :, 0:choose]
            if kind == "top4":
                chain.step(v.tensor_tensor(ex, ex, picked[:], ALU.mult))
            chain.step(v.tensor_reduce(total[:], ex, AX.X, ALU.add))
            chain.step(v.reciprocal(inv[:], total[:]))
            if kind == "hier":
                chain.step(v.tensor_reduce(etotal[:], eexp[:], AX.X, ALU.add))
                chain.step(v.reciprocal(einv[:], etotal[:]))
                chain.step(v.tensor_tensor(epick[:, :, :, 0], el[:, :, :, 0], el[:, :, :, 1], ALU.is_ge))
                chain.step(v.tensor_tensor(epick[:, :, :, 1], el[:, :, :, 1], el[:, :, :, 0], ALU.is_gt))
                chain.step(v.tensor_tensor(einv[:], einv[:], bcast(inv[:], 2, G), ALU.mult))
                chain.step(v.tensor_tensor(einv[:], einv[:], picked[:, :, 0:G], ALU.mult))
                v.tensor_tensor(gates[:, :, 0:E].rearrange("p b (g e) -> p b g e", e=2), epick[:], bcast(einv[:], 3, 2),
                                ALU.mult).then_inc(gates_ready, 1)
            elif kind == "top1":
                v.tensor_tensor(gates[:, :, 0:E], picked[:], bcast(inv[:], 2, E), ALU.mult).then_inc(gates_ready, 1)
            else:
                if kind == "top2":
                    chain.step(v.tensor_tensor(ex, ex, picked[:], ALU.mult))
                v.tensor_tensor(gates[:, :, 0:E], ex, bcast(inv[:], 2, E), ALU.mult).then_inc(gates_ready, 1)
            if kind == "top4":
                v.memset(gates[:, :, E:E + 1], 1.0).then_inc(gates_ready, 1)
                v.memset(y[:], 0.0).then_inc(gates_ready, 1)
            if b2_in:
                for i in range(2):
                    dve.wait_ge(gatesT_ready, 1)
                    v.tensor_copy(gatesT[:, i * HALF:(i + 1) * HALF], ps[0:E, 1 + i, 0:HALF]).then_inc(gatesT_copied, 1)
                for b in range(B):
                    dve.wait_ge(y_ready, b + 1)
                    v.tensor_copy(y[:, b, :], ps[0:TQ, 4 + b % 4, 0:D]).then_inc(y_copied, 1)


def experts(nc, core, tag, A, xT, gates, y, E, F, tile, swiglu, cut, before):
    ps = core["ps"]
    NF = -(-F // tile)
    size = [min(tile, F - f * tile) for f in range(NF)]
    UP = ("w1", "w2") if swiglu else ("w1",)
    down = A["w3"] if swiglu else A["w2"]
    whole = NF if size[-1] == tile else NF - 1
    SPLITS = len(UP) + 1 + (whole < NF)
    with ExitStack() as c:
        sb = lambda n, s, t=FP32: c.enter_context(nc.sbuf_tensor(f"{tag}_{n}", s, t))
        sem = lambda n: core["phases"].sem(f"{tag}_{n}")
        up_high = [[sb(f"{u}_high_{s}", [P, KD, F], FP32R) for u in UP] for s in range(2)]
        up_low = [[sb(f"{u}_low_{s}", [P, KD, F], FP32R) for u in UP] for s in range(2)]
        up_loaded, down_loaded = [sb(f"{u}_loaded", [P, KD, F]) for u in UP], sb("down_loaded", [tile, NF, D])
        down_high = [sb(f"down_high_{s}", [tile, NF, D], FP32R) for s in range(2)]
        down_low = [sb(f"down_low_{s}", [tile, NF, D], FP32R) for s in range(2)]
        x_high, x_low = sb("x_high", [P, KD, N], FP32R), sb("x_low", [P, KD, N], FP32R)
        h = sb("h", [tile, 2, HALF])
        h_high, h_low = sb("h_high", [tile, NF, N], FP32R), sb("h_low", [tile, NF, N], FP32R)
        if swiglu:
            sig, gated = sb("sig", [tile, 2, HALF]), sb("gated", [tile, 2, HALF])
        else:
            b1 = [sb(f"b1_{s}", [P, NF]) for s in range(2)]

        def weight_loads(n):
            out = [(t[:], A[u][n].rearrange("(k p) f -> p k f", p=P)) for u, t in zip(UP, up_loaded)]
            out.append((down_loaded[:, 0:whole, :], down[n, 0:whole * tile, :].rearrange("(f p) d -> p f d", p=tile)))
            if whole < NF:
                out.append((down_loaded[0:size[-1], whole, :], down[n, whole * tile:F, :]))
            return out

        core["phases"].ask(tag, weight_loads(0) + ([] if swiglu else [(b1[n][:], A["b1"][n]) for n in range(2)]))
        before()
        weights_ready, b1_ready = sem("weights_ready"), [sem("b1_ready_0"), sem("b1_ready_1")]
        weights_used, weights_high, weights_split = sem("weights_used"), sem("weights_high"), sem("weights_split")
        x_high_ready, x_split = sem("x_high_ready"), sem("x_split")
        up_ready, sig_ready, gated_ready = sem("up_ready"), sem("sig_ready"), sem("gated_ready")
        h_ready, h_high_ready, h_split = sem("h_ready"), sem("h_high_ready"), sem("h_split")
        y_ready, y_added = sem("y_ready"), sem("y_added")
        PARTS = 2 * NF
        BANKS = 2 if swiglu else 4
        block = core["phases"].block(c)

        def weights(s):
            out = [(t[:], high[:], low[:]) for t, high, low in zip(up_loaded, up_high[s], up_low[s])]
            out.append([t[:, 0:whole, :] for t in (down_loaded, down_high[s], down_low[s])])
            if whole < NF:
                out.append([t[0:size[-1], whole, :] for t in (down_loaded, down_high[s], down_low[s])])
            return out

        def experts_of(engine, one, with_pair=False):
            with engine.Fori(0, E // 2 - 1, 1) as i:
                for s in range(2):
                    one(2 * i + s, s, *([i] if with_pair else []))
            for n in range(E - 2, E):
                one(n, n % 2, *([n // 2] if with_pair else []))

        @block.sync
        def _(sp):
            def load(n, s):
                sp.wait_ge(weights_split, n * SPLITS)
                for to, src in weight_loads(n):
                    sp.dma_start(to, src).then_inc(weights_ready, 16)
                if not swiglu and not (isinstance(n, int) and n == 1):
                    sp.wait_ge(weights_used, n - 1)
                    sp.dma_start(b1[s][:], A["b1"][n]).then_inc(b1_ready[s], 16)
            load(1, 1)
            with sp.Fori(1, E // 2, 1) as i:
                for s in range(2):
                    load(2 * i + s, s)

        @block.gpsimd
        def _(pool):
            def split_low(n, s):
                for j, (loaded, high, low) in enumerate(weights(s)):
                    pool.wait_ge(weights_high, n * SPLITS + j + 1)
                    nc.gpsimd.tensor_tensor(low, loaded, high.bitcast(FP32), ALU.subtract).then_inc(weights_split, 1)
            experts_of(pool, lambda n, s: None if isinstance(n, int) and n == E - 1 else split_low(n + 1, 1 - s))

        @block.tensor
        def _(pe):
            def product(out, left, right, start, stop):
                nc.tensor.matmul(out, left[0], right[0], start=start, stop=False)
                nc.tensor.matmul(out, left[0], right[1], start=False, stop=False)
                return nc.tensor.matmul(out, left[1], right[0], start=False, stop=stop)

            def one(n, s):
                pe.wait_ge(weights_split, n * SPLITS + SPLITS)
                for part in range(PARTS):
                    chunk, f = divmod(part, NF)
                    pe.wait_ge(h_ready, n * PARTS + (part - BANKS + 2 if part >= BANKS else 1))
                    for u in range(len(UP)):
                        bank = (part % BANKS) * len(UP) + u
                        for k in range(KD):
                            at = slice(f * tile, f * tile + size[f])
                            tokens = slice(chunk * HALF, (chunk + 1) * HALF)
                            last = product(ps[0:size[f], bank, 0:HALF],
                                           (up_high[s][u][:, k, at], up_low[s][u][:, k, at]),
                                           (x_high[:, k, tokens], x_low[:, k, tokens]), k == 0, k == KD - 1)
                    last.then_inc(up_ready, 1)
                for b in range(B):
                    if b % 4 == 0:
                        pe.wait_ge(h_split, n * PARTS + (b // 4 + 1) * NF + 1)
                    pe.wait_ge(y_added, n * B + (b - 2 if b >= 4 else 1))
                    for f in range(NF):
                        tokens = slice(b * TQ, (b + 1) * TQ)
                        last = product(ps[0:TQ, 4 + b % 4, 0:D], (h_high[0:size[f], f, tokens], h_low[0:size[f], f, tokens]),
                                       (down_high[s][0:size[f], f, :], down_low[s][0:size[f], f, :]),
                                       f == 0, f == NF - 1)
                    last.then_inc(y_ready, 1)
                pe.wait_ge(y_ready, n * B + B + 1)
                pe.sem_inc(weights_used, 1)
            pe.sem_inc(y_ready, 1)
            pe.wait_ge(x_split, 1)
            experts_of(pe, one)

        @block.scalar
        def _(act):
            def split_high(n, s):
                for loaded, high, low in weights(s):
                    nc.scalar.activation(high, loaded, ACT.Copy).then_inc(weights_high, 1)

            def hidden_high(n, part):
                chunk, f = divmod(part, NF)
                m = size[f]
                act.wait_ge(h_ready, n * PARTS + part + 2)
                nc.scalar.activation(h_high[0:m, f, chunk * HALF:(chunk + 1) * HALF], h[0:m, part % 2, :], ACT.Copy).then_inc(h_high_ready, 1)

            def one(n, s):
                act.wait_ge(y_ready, n * B + 1)
                if not swiglu:
                    act.wait_ge(b1_ready[s], 8 * (n - s) + 1)
                for part in range(PARTS):
                    chunk, f = divmod(part, NF)
                    act.wait_ge(up_ready, n * PARTS + part + 1)
                    if swiglu:
                        act.wait_ge(gated_ready, n * PARTS + (part if part >= 2 else 1))
                        nc.scalar.activation(sig[0:size[f], part % 2, :], ps[0:size[f], 2 * (part % BANKS), 0:HALF],
                                             ACT.Sigmoid).then_inc(sig_ready, 1)
                    else:
                        act.wait_ge(h_split, n * PARTS + (part if part >= 2 else 1))
                        nc.scalar.activation(h[:, part % 2, :], ps[:, part % BANKS, 0:HALF], ACT.Relu,
                                             bias=b1[s][:, f:f + 1]).then_inc(h_ready, 1)
                    if part and swiglu:
                        hidden_high(n, part - 1)
                    if part == NF and not (isinstance(n, int) and n == E - 1):
                        act.wait_ge(weights_ready, 16 * SPLITS * (n + 1))
                        split_high(n + 1, 1 - s)
                if swiglu:
                    hidden_high(n, PARTS - 1)

            act.sem_inc(h_high_ready, 1)
            for ready in b1_ready:
                act.sem_inc(ready, 1)
            split_high(0, 0)
            experts_of(act, one)

        @block.vector
        def _(dve):
            def hidden_low(n, part):
                chunk, f = divmod(part, NF)
                m = size[f]
                tokens = slice(chunk * HALF, (chunk + 1) * HALF)
                if not swiglu:
                    dve.wait_ge(h_ready, n * PARTS + part + 2)
                    nc.vector.tensor_copy(h_high[0:m, f, tokens], h[0:m, part % 2, :]).then_inc(h_high_ready, 1)
                dve.wait_ge(h_high_ready, n * PARTS + part + 2)
                nc.vector.tensor_tensor(h_low[0:m, f, tokens], h[0:m, part % 2, :], h_high[0:m, f, tokens].bitcast(FP32),
                                        ALU.subtract).then_inc(h_split, 1)

            def one(n, s, pair):
                for part in range(PARTS):
                    f = part % NF
                    m = size[f]
                    if swiglu:
                        dve.wait_ge(sig_ready, n * PARTS + part + 1)
                        nc.vector.tensor_tensor(gated[0:m, part % 2, :], ps[0:m, 2 * (part % BANKS), 0:HALF], sig[0:m, part % 2, :],
                                                ALU.mult).then_inc(gated_ready, 1)
                        dve.wait_ge(gated_ready, n * PARTS + part + 2)
                        nc.vector.tensor_tensor(h[0:m, part % 2, :], ps[0:m, 2 * (part % BANKS) + 1, 0:HALF],
                                                gated[0:m, part % 2, :], ALU.mult).then_inc(h_ready, 1)
                    if part:
                        hidden_low(n, part - 1)
                hidden_low(n, PARTS - 1)
                for b in range(B):
                    dve.wait_ge(y_ready, n * B + b + 2)
                    dve.wait_ge(y_added, n * B + 1)
                    e = n if cut == 1 else pair
                    gate = gates[:, b, e:e + 1] if isinstance(e, int) else gates[:, b, bass.ds(e, 1)]
                    nc.vector.scalar_tensor_tensor(y[:, b, :], ps[0:TQ, 4 + b % 4, 0:D], gate, y[:, b, :], ALU.mult,
                                                   ALU.add).then_inc(y_added, 1)

            dve.sem_inc(y_added, 1)
            dve.sem_inc(h_ready, 1)
            dve.sem_inc(h_split, 1)
            if swiglu:
                dve.sem_inc(gated_ready, 1)
            nc.vector.tensor_copy(x_high[:], xT[:]).then_inc(x_high_ready, 1)
            dve.wait_ge(x_high_ready, 1)
            nc.vector.tensor_tensor(x_low[:], xT[:], x_high[:].bitcast(FP32), ALU.subtract).then_inc(x_split, 1)
            for j, (loaded, high, low) in enumerate(weights(0)):
                dve.wait_ge(weights_high, j + 1)
                nc.vector.tensor_tensor(low, loaded, high.bitcast(FP32), ALU.subtract).then_inc(weights_split, 1)
            experts_of(dve, one, True)


def lora(nc, core, tag, A, x, gate, xn, xnT, gates, before):
    ps, ident = core["ps"], core["ident"]
    E, R = 8, 4
    ER = E * R
    with ExitStack() as c:
        sb = lambda n, s: c.enter_context(nc.sbuf_tensor(f"{tag}_{n}", s, FP32))
        sem = lambda n: core["phases"].sem(f"{tag}_{n}")
        wl, left, right, bias = sb("wl", [P, KD, D]), sb("left", [P, KD, ER]), sb("right", [ER, D]), sb("bias", [TQ, D])
        low, lowT, part = sb("low", [TQ, B, ER]), sb("lowT", [ER, N]), sb("part", [TQ, 2, D])
        core["phases"].ask(tag, [(wl[:], A["wl"].rearrange("(k p) n -> p k n", p=P)), (left[:], A["left"].rearrange("(k p) n -> p k n", p=P)),
                           (right[:], A["right"]), (bias[:], A["bl"].partition_broadcast(TQ))])
        before()
        low_ready, low_scaled, lowT_ready, lowT_copied = sem("low_ready"), sem("low_scaled"), sem("lowT_ready"), sem("lowT_copied")
        out_ready, biased, x_done = sem("out_ready"), sem("biased"), sem("x_done")
        block = core["phases"].block(c)

        @block.tensor
        def _(pe):
            for b in range(B):
                for k in range(KD):
                    last = nc.tensor.matmul(ps[0:TQ, 0, b * ER:(b + 1) * ER], xnT[:, k, b * TQ:(b + 1) * TQ], left[:, k, :],
                                            start=k == 0, stop=k == KD - 1)
            last.then_inc(low_ready, 1)
            pe.wait_ge(low_scaled, 1)
            for b in range(B):
                last = nc.tensor.transpose(ps[0:ER, 1 + b // 4, (b % 4) * TQ:(b % 4 + 1) * TQ], low[:, b, :], ident[0:TQ, 0:TQ])
            last.then_inc(lowT_ready, 1)
            pe.wait_ge(lowT_copied, 2)
            for b in range(B):
                if b >= 4:
                    pe.wait_ge(biased, b - 3)
                for k in range(KD):
                    nc.tensor.matmul(ps[0:TQ, 4 + b % 4, 0:D], xnT[:, k, b * TQ:(b + 1) * TQ], wl[:, k, :], start=k == 0, stop=False)
                nc.tensor.matmul(ps[0:TQ, 4 + b % 4, 0:D], lowT[:, b * TQ:(b + 1) * TQ], right[:], start=False, stop=True)\
                    .then_inc(out_ready, 1)

        @block.vector
        def _(dve):
            v = nc.vector
            dve.wait_ge(low_ready, 1)
            v.tensor_tensor(low[:].rearrange("p b (e r) -> p b e r", r=R),
                            ps[0:TQ, 0, 0:B * ER].rearrange("p (b e r) -> p b e r", e=E, r=R),
                            bcast(gates[:, :, 0:E], 3, R), ALU.mult).then_inc(low_scaled, 1)
            dve.wait_ge(lowT_ready, 1)
            for i in range(2):
                v.tensor_copy(lowT[:, i * HALF:(i + 1) * HALF], ps[0:ER, 1 + i, 0:HALF]).then_inc(lowT_copied, 1)
            for b in range(B):
                dve.wait_ge(out_ready, b + 1)
                if b >= 2:
                    dve.wait_ge(x_done, b - 1)
                v.tensor_tensor(part[:, b % 2, :], ps[0:TQ, 4 + b % 4, 0:D], bias[:], ALU.add).then_inc(biased, 1)
                dve.wait_ge(biased, b + 1)
                v.scalar_tensor_tensor(x[:, b, :], part[:, b % 2, :], gate, x[:, b, :], ALU.mult, ALU.add).then_inc(x_done, 1)
            dve.wait_ge(x_done, B)



def start(nc, core, A, cols):
    with ExitStack() as c:
        landed, tanh_done, cleared = [core["phases"].sem(f"start_{n}") for n in ("landed", "tanh", "cleared")]
        raw = c.enter_context(nc.sbuf_tensor("start_gates", [P, 8], FP32))
        block = core["phases"].block(c)

        @block.sync
        def _(sp):
            sp.dma_start(core["x"][:], A["x"].rearrange("b t d -> t b d")).then_inc(landed, 16)
            sp.dma_start(core["ident"][:], A["ident"]).then_inc(landed, 16)
            for to, n in zip(cols, ("L0_ln_in_g", "L0_ln_in_b")):
                sp.dma_start(to[:], A[n]).then_inc(landed, 16)
            sp.dma_start(raw[:, 0:4], A["g_xattn"].partition_broadcast(P)).then_inc(landed, 16)
            sp.dma_start(raw[:, 4:8], A["g_ffn"].partition_broadcast(P)).then_inc(landed, 16)

        core["phases"].run_ahead(block, False)

        @block.scalar
        def _(act):
            act.wait_ge(landed, 96)
            nc.scalar.activation(core["gate"][:], raw[:], ACT.Tanh).then_inc(tanh_done, 1)
            act.wait_ge(tanh_done, 1)

        @block.vector
        def _(dve):
            for bank in (4, 5, 6):
                nc.vector.memset(core["ps"][:, bank, :], 0.0).then_inc(cleared, 1)


def network(nc, A, y_out, stages=8):
    with ExitStack() as c:
        sb = lambda n, s: c.enter_context(nc.sbuf_tensor(n, s, FP32))
        core = {"ps": c.enter_context(nc.psum_tensor("ps", [P, 8, BANK], FP32)), "ident": sb("ident", [P, P]),
                "x": sb("x_now", [TQ, B, D]), "gate": sb("gate", [P, 8]), "phases": Phases(nc)}
        x, xn, xnT, y = core["x"], sb("xn", [TQ, B, D]), sb("xnT", [P, KD, N]), sb("y_acc", [TQ, B, D])
        gates = sb("gates", [TQ, B, 9])
        gate = lambda i: core["gate"][0:TQ, i:i + 1]
        sub = lambda prefix, names: {n: A[prefix + m] for n, m in names.items()}
        const = {n: A[n] for n in ("before", "ctx", "ctxT", "same_head", "rot", "cosq", "sinq", "cosk", "sink")}
        projections = dict(wq="Wq", wk="Wk", wv="Wv", bq="bq", bk="bk", bv="bv", wo="Wo", bo="bo")

        cols = [sb(f"col_{n}", [P, KD]) for n in ("ln_in_g", "ln_in_b")]

        def first_normal():
            start(nc, core, A, cols)
            layernorm_all(nc, core, "l0a", x, xn)
            layernorm_all(nc, core, "l0b", xn, xn, xT=xnT, xT_affine=cols)
        if stages >= 1:
            attention(nc, core, "a0", "cosine", {**const, **sub("L0_xattn_", dict(
                wq="Wq", wk="Wk", wv="Wv", wo="Wo", q_scale="q_scale", k_scale="k_scale", ctx_gain="ln_ctx_g",
                ctx_offset="ln_ctx_b", null_k="null_k", null_v="null_v")), "mask": A["mask2"]},
                x, gate(0), xn, xnT, first_normal, out=y)
            layernorm_all(nc, core, "l0c", y, y, affine=(A["L0_ln_out_g"], A["L0_ln_out_b"]), update=(x, gate(0)))
        if stages >= 2:
            attention(nc, core, "s0", "self", {**const, **sub("L0_ffn_", dict(
                wq="wq", wk="wk", wv="wv", bq="bq", bk="bk", bv="bv", wo="wo", bo="out_proj_b")), "mask": A["mask_quarter"]},
                x, gate(4), xn, xnT, lambda: layernorm_all(nc, core, "l1a", x, xn, xT=xnT, settle=True), out=y)
            normal = lambda: layernorm_all(nc, core, "l1b", y, xn, affine=(A["L0_ffn_ln1_g"], A["L0_ffn_ln1_b"]), xT=xnT, settle=True)
            routing = lambda: route(nc, core, "r0", "hier", {**const, **sub("L0_ffn_", dict(wr="wr", br="br", b2="b2"))},
                                    xnT, gates, normal, y)
            experts(nc, core, "e0", sub("L0_ffn_", dict(w1="w1", b1="b1", w2="w2")), xnT, gates, y, 8, 512, P, False, 1, routing)
            layernorm_all(nc, core, "l1c", y, y, add=(xn, None), affine=(A["L0_ffn_ln2_g"], A["L0_ffn_ln2_b"]), update=(x, gate(4)))
        if stages >= 3:
            attention(nc, core, "a1", "linear", {**const, **sub("L1_xattn_", projections), "mask": A["mask_quarter"]},
                      x, gate(1), xn, xnT, lambda: layernorm_all(nc, core, "l2a", x, xn, xT=xnT, settle=True))
        add = None
        if stages >= 4:
            normal = lambda: layernorm_all(nc, core, "l3a", x, xn, xT=xnT, settle=True)
            routing = lambda: route(nc, core, "r1", "top4", {**const, **sub("L1_ffn_", dict(wr="Wg", br="routing_bias"))},
                                    xnT, gates, normal, y)
            experts(nc, core, "e1", sub("L1_ffn_", dict(w1="W1", w2="W2", w3="W3")), xnT, gates, y, 18, 341, 114, True, 2, routing)
            add = (y, gate(5))
        if stages >= 5:
            attention(nc, core, "a2", "raw", {**const, **sub("L2_xattn_", dict(wo="W_out", bo="b_out")), "mask": A["mask_one"]},
                      x, gate(2), xn, xnT, lambda: layernorm_all(nc, core, "l4a", x, xn, xT=xnT, add=(y, gate(5)), settle=True))
            add = None
        if stages >= 6:
            normal = lambda: layernorm_all(nc, core, "l5a", x, xn, xT=xnT, settle=True)
            routing = lambda: route(nc, core, "r2", "top1", {**const, **sub("L2_ffn_", dict(wr="router_W", br="router_b", b2="b2"))},
                                    xnT, gates, normal, y)
            experts(nc, core, "e2", sub("L2_ffn_", dict(w1="W1", b1="b1", w2="W2")), xnT, gates, y, 16, 512, P, False, 2, routing)
            add = (y, gate(6))
        if stages >= 7:
            attention(nc, core, "a3", "rope", {**const, **sub("L3_xattn_", projections), "mask": A["mask_eighth"], "allow": A["mask"]},
                      x, gate(3), xn, xnT, lambda: layernorm_all(nc, core, "l6a", x, xn, xT=xnT, add=(y, gate(6)), settle=True))
            add = None
        if stages >= 8:
            normal = lambda: layernorm_all(nc, core, "l7a", x, xn, xT=xnT, settle=True)
            routing = lambda: route(nc, core, "r3", "top2", {**const, **sub("L3_ffn_", dict(wr="gate_w"))}, xnT, gates, normal)
            lora(nc, core, "f3", sub("L3_ffn_", dict(wl="W_lin", bl="b_lin", left="left", right="right")), x, gate(7), xn, xnT, gates, routing)
        if add is not None:
            layernorm_all(nc, core, "partial", x, xn, add=add)
        with ExitStack() as c2:
            stored = core["phases"].sem("stored")
            block = core["phases"].block(c2)

            @block.sync
            def _(sp):
                sp.dma_start(y_out.rearrange("b t d -> t b d"), x[:]).then_inc(stored, 16)
                sp.wait_ge(stored, 16)


def layouts(i):
    c = np.ascontiguousarray
    a = {k: np.asarray(v) for k, v in i.items()}
    column = lambda t: c(t.reshape(-1, P).T)
    r = {"x": a["x"], "ctx": a["ctx_1024"], "g_xattn": a["g_xattn"], "g_ffn": a["g_ffn"], "mask": c(a["mask_BxS2_bf1"]).view(np.uint8)}
    r["ctxT"] = c(a["ctx_1024"].transpose(0, 2, 1).reshape(B, KD, P, CK).transpose(0, 2, 1, 3))
    w = a["L0_xattn_Wkv"]
    r["L0_xattn_Wq"], r["L0_xattn_Wo"] = a["L0_xattn_Wq"], a["L0_xattn_Wo"]
    r["L0_xattn_Wk"], r["L0_xattn_Wv"] = c(w[:, :1024]), c(w[:, 1024:])
    for n in ("q_scale", "k_scale"):
        t = a[f"L0_xattn_{n}"]
        r[f"L0_xattn_{n}"] = c(np.concatenate([t, t])[:, None])
    nk, nv = a["L0_xattn_null_kv"]
    r["L0_xattn_null_k"], r["L0_xattn_null_v"] = c(np.concatenate([nk, nk])[:, None]), c(nv[None])
    for n in ("ln_in_g", "ln_in_b"):
        r[f"L0_{n}"] = column(a[f"L0_xattn_{n}"])
    for n in ("ln_ctx_g", "ln_ctx_b"):
        r[f"L0_xattn_{n}"] = column(a[f"L0_xattn_{n}"])
    for n in ("ln_out_g", "ln_out_b"):
        r[f"L0_{n}"] = a[f"L0_xattn_{n}"]
    w, t = a["L0_ffn_in_proj_w"].T, a["L0_ffn_in_proj_b"]
    for j, n in enumerate("qkv"):
        r[f"L0_ffn_w{n}"] = c(w[:, j * D:(j + 1) * D])
        r[f"L0_ffn_b{n}"] = c(t[j * D:(j + 1) * D]) if n == "v" else column(t[j * D:(j + 1) * D])
    r["L0_ffn_wo"] = c(a["L0_ffn_out_proj_w"].T)
    for n in ("out_proj_b", "ln1_g", "ln1_b", "ln2_g", "ln2_b", "b2", "w1", "w2"):
        r[f"L0_ffn_{n}"] = a[f"L0_ffn_{n}"]
    r["L0_ffn_wr"] = c(np.concatenate([a["L0_ffn_w_group"], a["L0_ffn_w_expert"].transpose(1, 0, 2).reshape(D, 8)], 1))
    r["L0_ffn_br"] = c(np.concatenate([a["L0_ffn_b_group"], a["L0_ffn_b_expert"].reshape(8)]))
    r["L0_ffn_b1"] = c(a["L0_ffn_b1"].reshape(8, -1, P).transpose(0, 2, 1))
    for n in ("Wq", "Wk", "Wv", "Wo", "bv", "bo"):
        r[f"L1_xattn_{n}"] = a[f"L1_xattn_{n}"]
    for n in ("bq", "bk"):
        r[f"L1_xattn_{n}"] = column(a[f"L1_xattn_{n}"])
    r["L1_ffn_Wg"], r["L1_ffn_routing_bias"] = c(a["L1_ffn_Wg"].T), a["L1_ffn_routing_bias"]
    for n in ("1", "2", "3"):
        r[f"L1_ffn_W{n}"] = c(np.concatenate([a[f"L1_ffn_W{n}"], a[f"L1_ffn_Ws{n}"][None]]).transpose(0, 2, 1))
    halves = lambda t: c(t.reshape(t.shape[0], D, 2, -1).transpose(0, 2, 1, 3).reshape(2 * t.shape[0], D, -1))
    r["L1_ffn_W1"], r["L1_ffn_W2"], r["L1_ffn_W3"] = halves(r["L1_ffn_W1"]), halves(r["L1_ffn_W2"]), r["L1_ffn_W3"].reshape(18, -1, D)
    r["L2_xattn_W_out"], r["L2_xattn_b_out"] = c(a["L2_xattn_W_out"].T), a["L2_xattn_b_out"]
    for n in ("router_W", "router_b", "W1", "W2", "b2"):
        r[f"L2_ffn_{n}"] = a[f"L2_ffn_{n}"]
    r["L2_ffn_W1"], r["L2_ffn_W2"] = halves(r["L2_ffn_W1"]), r["L2_ffn_W2"].reshape(16, -1, D)
    r["L2_ffn_b1"] = c(a["L2_ffn_b1"].reshape(16, -1, P).transpose(0, 2, 1))
    w, t = a["L3_xattn_Wkv"], a["L3_xattn_bkv"]
    r["L3_xattn_Wq"], r["L3_xattn_Wk"], r["L3_xattn_Wv"] = a["L3_xattn_Wq"], c(w[:, :D]), c(w[:, D:])
    r["L3_xattn_bq"], r["L3_xattn_bk"], r["L3_xattn_bv"] = column(a["L3_xattn_bq"]), column(t[:D]), c(t[D:])
    r["L3_xattn_Wo"], r["L3_xattn_bo"] = a["L3_xattn_Wo"], a["L3_xattn_bo"]
    r["L3_ffn_W_lin"], r["L3_ffn_b_lin"], r["L3_ffn_gate_w"] = c(a["L3_ffn_W_lin"].T), a["L3_ffn_b_lin"], c(a["L3_ffn_gate_w"].T)
    r["L3_ffn_left"], r["L3_ffn_right"] = c(a["L3_ffn_left"].transpose(1, 0, 2).reshape(D, 32)), c(a["L3_ffn_right"].reshape(32, D))
    f32 = np.float32
    r["ident"] = np.eye(P, dtype=f32)
    rows = np.arange(P)
    r["same_head"] = (rows[:, None] // 64 == rows[None] // 64).astype(f32)
    r["before"] = (np.arange(8)[None] < np.arange(8)[:, None]).astype(f32)
    own = lambda hd: (rows[:, None] // hd == np.arange(P // hd)[None]).astype(f32)
    r["mask2"], r["mask_quarter"], r["mask_one"], r["mask_eighth"] = 8 * own(64), own(16) / 4, own(16), own(16) / 8
    r["mask2"], r["mask_quarter"], r["mask_eighth"] = [r[n].astype(f32) for n in ("mask2", "mask_quarter", "mask_eighth")]
    rot = np.zeros((P, P), f32)
    even = rows[::2]
    rot[even + 1, even], rot[even, even + 1] = -1.0, 1.0
    r["rot"] = rot
    inv_freq = (1.0 / 10000.0 ** (np.arange(0, 16, 2, dtype=f32) / f32(16))).astype(f32)
    for n, length in (("q", TQ), ("k", CK)):
        pos = f32(10.0) * (np.arange(length, dtype=f32) / f32(length))
        angle = pos[None] * inv_freq[(rows % 16) // 2][:, None]
        r["cos" + n], r["sin" + n] = np.cos(angle).astype(f32), np.sin(angle).astype(f32)
    return r


def kernel(**inputs):
    import concourse.bacc as bacc
    from concourse.bass_utils import run_bass_kernel_spmd

    arrays = {f"in_{n}": t for n, t in layouts(inputs).items()}
    nc = bacc.Bacc("TRN2", target_bir_lowering=False, num_devices=1)
    A = {n[3:]: nc.dram_tensor(n, t.shape, mybir.dt.from_np(t.dtype), kind="ExternalInput").ap() for n, t in arrays.items()}
    out = nc.dram_tensor("out", (B, TQ, D), FP32, kind="ExternalOutput").ap()
    network(nc, A, out)
    r = run_bass_kernel_spmd(nc, [arrays], core_ids=[0])
    return r.results[0]["out"]
```
